# Optimizing a Trainium2 kernel written in Bass

```python
import numpy as np
import jax
import jax.numpy as jnp

def _softmax(x, axis=-1):
    return jax.nn.softmax(x, axis=axis)

def _gelu(x):
    return jax.nn.gelu(x, approximate=True)

def _silu(x):
    return jax.nn.silu(x)

def _sigmoid(x):
    return jax.nn.sigmoid(x)

def _layernorm(x, axis=-1, eps=1e-05):
    m = jnp.mean(x, axis=axis, keepdims=True)
    v = jnp.var(x, axis=axis, keepdims=True)
    return (x - m) / jnp.sqrt(v + eps)

def _scatter_add(tgt, idx, src, axis=0):
    return tgt.at[idx].add(src)

def _segment_sum(src, seg, n):
    return jax.ops.segment_sum(src, seg, n)
kernel_name = 'mk_decoder_postln_d1_seqx_r8_1aae87'

def setup_inputs(seed: int=0):
    np.random.seed(seed)
    _w = jnp.asarray

    def _rec_inputs():
        import jax
        import jax.numpy as jnp
        _rk = jax.random.key(seed)
        x = -0.0002928 + 1 * jax.random.normal(jax.random.fold_in(_rk, 1), (1, 1024, 128), jnp.float32)
        _lenS = 1024 - jax.random.randint(jax.random.fold_in(_rk, 7), (1,), 0, max(1, 1024 // 4) + 1, jnp.int32)
        _lenS2 = 6404 - jax.random.randint(jax.random.fold_in(_rk, 8), (1,), 0, max(1, 6404 // 4) + 1, jnp.int32)
        _ctx_1024P = jax.random.normal(jax.random.fold_in(_rk, 11), (1, 16, 128), jnp.float32)
        _ctx_1024c = jax.random.dirichlet(jax.random.fold_in(_rk, 511), 0.3 * jnp.ones((16,), jnp.float32), (1, 6404))
        _ctx_1024t = jnp.einsum('bsk,bkd->bsd', _ctx_1024c, _ctx_1024P)
        _ctx_1024t = _ctx_1024t * jax.lax.rsqrt(jnp.mean(jnp.square(_ctx_1024t)) + 1e-12) * 0.953939
        ctx_1024 = -1.39393e-06 + 0.999914 * (_ctx_1024t + 0.3 * jax.random.normal(jax.random.fold_in(_rk, 611), (1, 6404, 128), jnp.float32))
        _validS = jnp.arange(1024)[None, :] < _lenS[:, None]
        _validS2 = jnp.arange(6404)[None, :] < _lenS2[:, None]
        _causal = jnp.tril(jnp.ones((1024, 1024), dtype=bool))
        mask_Bx1x1xS2_fk0 = jnp.where(jnp.broadcast_to(_validS2[:, None, None, :], (1, 1, 1, 6404)), 0.0, 1.0).astype(jnp.float32)
        return (x, ctx_1024, mask_Bx1x1xS2_fk0)
    x, ctx_1024, mask_Bx1x1xS2_fk0 = _rec_inputs()

    def _L0_attn_setup():
        import jax, jax.numpy as jnp
        import numpy as np
        D_MODEL = 128
        N_HEADS = 4
        KEY_DIM = 128
        VALUE_DIM = 256
        DK = KEY_DIM // N_HEADS
        DV = VALUE_DIM // N_HEADS
        LOW_RANK = 16
        GATE_NORM = 16.0
        EPS = 1e-05

        def _gla_scan(q, k, v, gk):
            B, H, L, dk = q.shape
            dv = v.shape[-1]
            qs = jnp.moveaxis(q, 2, 0)
            ks_ = jnp.moveaxis(k, 2, 0)
            vs = jnp.moveaxis(v, 2, 0)
            gs = jnp.moveaxis(gk, 2, 0)

            def step(S, inp):
                q_t, k_t, v_t, g_t = inp
                S = S * jnp.exp(g_t)[..., None] + k_t[..., None] * v_t[..., None, :]
                o_t = jnp.einsum('bhk,bhkv->bhv', q_t, S)
                return (S, o_t)
            S0 = jnp.zeros((B, H, dk, dv), q.dtype)
            _, os = jax.lax.scan(step, S0, (qs, ks_, vs, gs))
            return jnp.moveaxis(os, 0, 2)
        key = jax.random.key(seed)
        ks = jax.random.split(key, 10)
        B, L = (2, 256)
        gain = 2.0 ** (-2.5)

        def xavier(k, shape, g=gain):
            fan_in, fan_out = (shape[0], shape[1])
            a = g * np.sqrt(6.0 / (fan_in + fan_out))
            return jax.random.uniform(k, shape, jnp.float32, -a, a)
        return {'x': jax.random.normal(ks[0], (B, L, D_MODEL), jnp.float32), 'Wq': xavier(ks[1], (D_MODEL, KEY_DIM)), 'Wk': xavier(ks[2], (D_MODEL, KEY_DIM)), 'Wv': xavier(ks[3], (D_MODEL, VALUE_DIM)), 'Wg': xavier(ks[4], (D_MODEL, VALUE_DIM)), 'gk_w1': xavier(ks[5], (D_MODEL, LOW_RANK)), 'gk_w2': xavier(ks[6], (LOW_RANK, KEY_DIM)), 'gk_b2': jnp.zeros((KEY_DIM,), jnp.float32), 'g_norm_w': jnp.ones((DV,), jnp.float32), 'Wo': xavier(ks[7], (VALUE_DIM, D_MODEL))}
    _L0_attn_all = _L0_attn_setup()
    _L0_attn_in = {k: v for k, v in _L0_attn_all.items() if k in ('Wq', 'Wk', 'Wv', 'Wg', 'gk_w1', 'gk_w2', 'gk_b2', 'g_norm_w', 'Wo')}
    del _L0_attn_all

    def _L0_xattn_setup():
        import jax, jax.numpy as jnp
        import numpy as np
        B, S, D, H = (2, 256, 128, 16)
        DH = D // H

        def _split_heads(x):
            b, s, _ = x.shape
            return x.reshape(b, s, H, DH).transpose(0, 2, 1, 3)
        key = jax.random.key(seed)
        ks = jax.random.split(key, 8)
        scale = 0.02
        return {'query': jax.random.normal(ks[0], (B, S, D), jnp.float32), 'key': jax.random.normal(ks[1], (B, S, D), jnp.float32), 'value': jax.random.normal(ks[2], (B, S, D), jnp.float32), 'mask': jax.random.randint(ks[3], (B, 1, 1, S), 0, 2).astype(jnp.float32), 'Wq': jax.random.normal(ks[4], (D, D), jnp.float32) * scale, 'bq': jnp.zeros((D,), jnp.float32), 'Wk': jax.random.normal(ks[5], (D, D), jnp.float32) * scale, 'bk': jnp.zeros((D,), jnp.float32), 'Wv': jax.random.normal(ks[6], (D, D), jnp.float32) * scale, 'bv': jnp.zeros((D,), jnp.float32), 'Wo': jax.random.normal(ks[7], (D, D), jnp.float32) * scale, 'bo': jnp.zeros((D,), jnp.float32)}
    _L0_xattn_all = _L0_xattn_setup()
    _L0_xattn_in = {k: v for k, v in _L0_xattn_all.items() if k in ('Wq', 'bq', 'Wk', 'bk', 'Wv', 'bv', 'Wo', 'bo')}
    del _L0_xattn_all

    def _L0_ffn_setup():
        import jax, jax.numpy as jnp
        import numpy as np
        B, S, D, H, E, K = (2, 128, 128, 64, 16, 4)
        HS = 2 * H

        def silu(z):
            return z * jax.nn.sigmoid(z)
        key = jax.random.key(seed)
        ks = jax.random.split(key, 8)
        sc = lambda fan_in: 1.0 / np.sqrt(fan_in)
        x = jax.random.normal(ks[0], (B, S, D), jnp.float32)
        gate_w = jax.random.normal(ks[1], (E, D), jnp.float32) * sc(D)
        ws_in = jax.random.normal(ks[2], (D, HS), jnp.float32) * sc(D)
        vs_in = jax.random.normal(ks[3], (D, HS), jnp.float32) * sc(D)
        ws_out = jax.random.normal(ks[4], (HS, D), jnp.float32) * sc(HS)
        e_win = jax.random.normal(ks[5], (E, D, H), jnp.float32) * sc(D)
        e_vin = jax.random.normal(ks[6], (E, D, H), jnp.float32) * sc(D)
        e_wout = jax.random.normal(ks[7], (E, H, D), jnp.float32) * sc(H)
        return {'x': x, 'gate_w': gate_w, 'ws_in': ws_in, 'vs_in': vs_in, 'ws_out': ws_out, 'e_win': e_win, 'e_vin': e_vin, 'e_wout': e_wout}
    _L0_ffn_all = _L0_ffn_setup()
    _L0_ffn_in = {k: v for k, v in _L0_ffn_all.items() if k in ('gate_w', 'ws_in', 'vs_in', 'ws_out', 'e_win', 'e_vin', 'e_wout')}
    del _L0_ffn_all
    return {'x': x, 'ctx_1024': ctx_1024, 'mask_Bx1x1xS2_fk0': mask_Bx1x1xS2_fk0, 'L0_attn_Wq': _L0_attn_in['Wq'], 'L0_attn_Wk': _L0_attn_in['Wk'], 'L0_attn_Wv': _L0_attn_in['Wv'], 'L0_attn_Wg': _L0_attn_in['Wg'], 'L0_attn_gk_w1': _L0_attn_in['gk_w1'], 'L0_attn_gk_w2': _L0_attn_in['gk_w2'], 'L0_attn_gk_b2': _L0_attn_in['gk_b2'], 'L0_attn_g_norm_w': _L0_attn_in['g_norm_w'], 'L0_attn_Wo': _L0_attn_in['Wo'], 'L0_xattn_Wq': _L0_xattn_in['Wq'], 'L0_xattn_bq': _L0_xattn_in['bq'], 'L0_xattn_Wk': _L0_xattn_in['Wk'], 'L0_xattn_bk': _L0_xattn_in['bk'], 'L0_xattn_Wv': _L0_xattn_in['Wv'], 'L0_xattn_bv': _L0_xattn_in['bv'], 'L0_xattn_Wo': _L0_xattn_in['Wo'], 'L0_xattn_bo': _L0_xattn_in['bo'], 'L0_ffn_gate_w': _L0_ffn_in['gate_w'], 'L0_ffn_ws_in': _L0_ffn_in['ws_in'], 'L0_ffn_vs_in': _L0_ffn_in['vs_in'], 'L0_ffn_ws_out': _L0_ffn_in['ws_out'], 'L0_ffn_e_win': _L0_ffn_in['e_win'], 'L0_ffn_e_vin': _L0_ffn_in['e_vin'], 'L0_ffn_e_wout': _L0_ffn_in['e_wout']}

def reference(x, ctx_1024, mask_Bx1x1xS2_fk0, L0_attn_Wq, L0_attn_Wk, L0_attn_Wv, L0_attn_Wg, L0_attn_gk_w1, L0_attn_gk_w2, L0_attn_gk_b2, L0_attn_g_norm_w, L0_attn_Wo, L0_xattn_Wq, L0_xattn_bq, L0_xattn_Wk, L0_xattn_bk, L0_xattn_Wv, L0_xattn_bv, L0_xattn_Wo, L0_xattn_bo, L0_ffn_gate_w, L0_ffn_ws_in, L0_ffn_vs_in, L0_ffn_ws_out, L0_ffn_e_win, L0_ffn_e_vin, L0_ffn_e_wout):
    import jax
    import jax.numpy as jnp

    def _L0_attn_ref(x, Wq, Wk, Wv, Wg, gk_w1, gk_w2, gk_b2, g_norm_w, Wo):
        import jax, jax.numpy as jnp
        import numpy as np
        D_MODEL = 128
        N_HEADS = 4
        KEY_DIM = 128
        VALUE_DIM = 256
        DK = KEY_DIM // N_HEADS
        DV = VALUE_DIM // N_HEADS
        LOW_RANK = 16
        GATE_NORM = 16.0
        EPS = 1e-05

        def _gla_scan(q, k, v, gk):
            B, H, L, dk = q.shape
            dv = v.shape[-1]
            qs = jnp.moveaxis(q, 2, 0)
            ks_ = jnp.moveaxis(k, 2, 0)
            vs = jnp.moveaxis(v, 2, 0)
            gs = jnp.moveaxis(gk, 2, 0)

            def step(S, inp):
                q_t, k_t, v_t, g_t = inp
                S = S * jnp.exp(g_t)[..., None] + k_t[..., None] * v_t[..., None, :]
                o_t = jnp.einsum('bhk,bhkv->bhv', q_t, S)
                return (S, o_t)
            S0 = jnp.zeros((B, H, dk, dv), q.dtype)
            _, os = jax.lax.scan(step, S0, (qs, ks_, vs, gs))
            return jnp.moveaxis(os, 0, 2)
        B, L, _ = x.shape
        scale = DK ** (-0.5)

        def heads(t, d):
            return t.reshape(B, L, N_HEADS, d).transpose(0, 2, 1, 3)
        q = heads(x @ Wq, DK) * scale
        k = heads(x @ Wk, DK)
        v = heads(x @ Wv, DV)
        gk = heads(jax.nn.log_sigmoid(x @ gk_w1 @ gk_w2 + gk_b2) / GATE_NORM, DK)
        o = _gla_scan(q, k, v, gk)
        o = o.transpose(0, 2, 1, 3)
        g = (x @ Wg).reshape(B, L, N_HEADS, DV)
        rms = o * jax.lax.rsqrt(jnp.mean(o * o, axis=-1, keepdims=True) + EPS)
        o = rms * g_norm_w * (g * jax.nn.sigmoid(g))
        o = o.reshape(B, L, VALUE_DIM)
        return o @ Wo

    def _L0_xattn_ref(query, key, value, mask, Wq, bq, Wk, bk, Wv, bv, Wo, bo):
        import jax, jax.numpy as jnp
        import numpy as np
        B, S, D, H = (2, 256, 128, 16)
        DH = D // H

        def _split_heads(x):
            b, s, _ = x.shape
            return x.reshape(b, s, H, DH).transpose(0, 2, 1, 3)
        q = _split_heads(query @ Wq + bq)
        k = _split_heads(key @ Wk + bk)
        v = _split_heads(value @ Wv + bv)
        logits = jnp.einsum('bhqd,bhkd->bhqk', q, k) / jnp.sqrt(jnp.float32(DH))
        logits = logits + mask * -1000000000.0
        attn = jax.nn.softmax(logits, axis=-1)
        out = jnp.einsum('bhqk,bhkd->bhqd', attn, v)
        out = out.transpose(0, 2, 1, 3).reshape(query.shape[0], -1, D)
        return out @ Wo + bo

    def _L0_ffn_ref(x, gate_w, ws_in, vs_in, ws_out, e_win, e_vin, e_wout):
        import jax, jax.numpy as jnp
        import numpy as np
        B, S, D, H, E, K = (2, 128, 128, 64, 16, 4)
        HS = 2 * H

        def silu(z):
            return z * jax.nn.sigmoid(z)
        b, s, d = x.shape
        T = b * s
        xf = x.reshape(T, d)
        g = jax.nn.sigmoid(xf @ gate_w.T)
        topv, topi = jax.lax.top_k(g, K)
        wn = topv / jnp.sum(topv, axis=-1, keepdims=True)
        combine = jnp.zeros_like(g).at[jnp.arange(T)[:, None], topi].add(wn)
        hin = jnp.einsum('td,edh->eth', xf, e_win)
        vin = jnp.einsum('td,edh->eth', xf, e_vin)
        h = silu(hin) * vin * combine.T[:, :, None]
        routed = jnp.einsum('eth,ehd->td', h, e_wout)
        shared = silu(xf @ ws_in) * (xf @ vs_in) @ ws_out
        return (shared + routed).reshape(b, s, d)
    x = _layernorm(x + _L0_attn_ref(x, L0_attn_Wq, L0_attn_Wk, L0_attn_Wv, L0_attn_Wg, L0_attn_gk_w1, L0_attn_gk_w2, L0_attn_gk_b2, L0_attn_g_norm_w, L0_attn_Wo), axis=-1)
    x = _layernorm(x + _L0_xattn_ref(x, ctx_1024, ctx_1024, mask_Bx1x1xS2_fk0, L0_xattn_Wq, L0_xattn_bq, L0_xattn_Wk, L0_xattn_bk, L0_xattn_Wv, L0_xattn_bv, L0_xattn_Wo, L0_xattn_bo), axis=-1)
    x = _layernorm(x + _L0_ffn_ref(x, L0_ffn_gate_w, L0_ffn_ws_in, L0_ffn_vs_in, L0_ffn_ws_out, L0_ffn_e_win, L0_ffn_e_vin, L0_ffn_e_wout), axis=-1)
    return x

_drawn_inputs = setup_inputs


def setup_inputs(seed=0):
    import zlib

    import numpy as np

    out = dict(_drawn_inputs(seed))
    spreads = {'L0_attn_gk_b2': (0.0, 2.0),
     'L0_attn_g_norm_w': (1.0, 0.6),
     'L0_xattn_bq': (0.0, 0.8),
     'L0_xattn_bk': (0.0, 2.0),
     'L0_xattn_bv': (0.0, 0.1),
     'L0_xattn_bo': (0.0, 0.1)}
    factors = {'L0_attn_gk_w1': 57.667, 'L0_attn_gk_w2': 89.948, 'L0_xattn_Wq': 8.0, 'L0_xattn_Wk': 8.0}
    for name, (base, spread) in spreads.items():
        noise = np.random.default_rng([zlib.crc32(name.encode()), seed]).standard_normal(out[name].shape)
        drawn = base * np.exp(spread * noise) if base else spread * noise
        out[name] = jnp.asarray(drawn.astype(out[name].dtype))
    for name, factor in factors.items():
        out[name] = (out[name] * factor).astype(out[name].dtype)
    return out
```

```python
from contextlib import ExitStack

import concourse.bass as bass
from concourse import mybir

F32 = mybir.dt.float32
BF16 = mybir.dt.bfloat16
U16 = mybir.dt.uint16
ACT = mybir.ActivationFunctionType
ALU = mybir.AluOpType
AX = mybir.AxisListType

P = 128
T = 1024
D = 128
NB, TB = 2, 512
NC = TB // P
GH, DK, DV = 4, 32, 64
LEVELS = 7
SKV = 6404
KT = -(-SKV // P)
SP = KT * P
XH, DH = 16, 8
NHG, HG = 4, 4
GT = 3
NG = KT // GT
STEPS = 4
UNITS = NB * NHG
SPLIT = 48
HALF = 64
ROW_MASK, ROW_SPLIT, ROW_MAX = 0, 3, 51
E, EH, TOPK = 16, 64, 4
NPS = E // 2 + 1
EPS = 1e-5
KC = GT * P
K_PART = (0, 0, 1, 1, 0, 2)
Q_PART = (0, 1, 0, 1, 2, 0)


def build(nc, A, out, dbg=None):
    dbg = dbg or {}
    with ExitStack() as ctx:
        def sb(name, shape, dt=F32):
            return ctx.enter_context(nc.sbuf_tensor(name, shape, dt))

        def sem(name):
            return ctx.enter_context(nc.semaphore(name))

        def dram(name, shape, dt):
            return nc.dram_tensor(name, shape, dt, kind="Internal").ap()

        def rep(ap, axis, n):
            dims = [list(d) for d in ap.ap]
            return bass.AP(ap.tensor, ap.offset, dims[:axis] + [[0, n]] + dims[axis:])

        ps = ctx.enter_context(nc.psum_tensor("ps", [P, 8, 512], F32))

        kbuf = sb("kbuf", [P, 2, 2, SP], BF16)
        qaug = sb("qaug", [P, NB * XH, TB], BF16)
        vaug = sb("vaug", [P, KT, XH, DH])
        vst = sb("vst", [P, GT, HG, 32])
        prob = sb("prob", [P, STEPS, 3, 512])
        osb = sb("osb", [P, UNITS, TB])
        ctxT = kbuf[:, 1, :, :].rearrange("p a s -> p (a s)").bitcast(F32)
        early = prob[:, :, :, :].rearrange("p a b c -> p (a b c)")

        def arena(area):
            at = [0]

            def carve(*shape, dt=F32):
                words = 1
                for n in shape:
                    words *= n
                words = words * (2 if dt == BF16 else 4) // 4
                at[0] += words
                assert at[0] <= area.shape[1], (at[0], area.shape)
                part = area[:, at[0] - words:at[0]]
                part = part.bitcast(dt) if dt != F32 else part
                names = "abc"[:len(shape)]
                return part.rearrange(f"p ({' '.join(names)}) -> p {' '.join(names)}",
                                      **dict(zip(names, shape)))

            return carve

        slot0 = kbuf[:, 0, :, :].rearrange("p a s -> p (a s)").bitcast(F32)
        probs = prob[:, :, :, :].rearrange("p a b c -> p (a b c)")
        sums_area = osb[:, :, :].rearrange("p a b -> p (a b)")
        shared = sb("shared", [P, 2304])

        carve = arena(slot0)
        q_t, k_t, pre, suf, z1, z2, zm = (carve(TB) for _ in range(7))
        ek, eq, q_l = (carve(2, TB // 2) for _ in range(3))
        k_l = carve(2, TB)
        carve = arena(probs)
        a_sc = carve(GH, TB)
        v_g, gw, og = (carve(NC, 256) for _ in range(3))
        ktok = carve(NC, P)
        carve = arena(sums_area)
        sq = carve(NC, 256)
        kd, qd = carve(TB), carve(TB)
        ogT = carve(2, TB)
        kvtmp = carve(NC, 256)
        carve = arena(shared[:, :])
        kf = carve(2, KC)
        kr = carve(KC)
        kp = carve(2, 3 * KC, dt=BF16)
        kp = kp.rearrange("p a (i k) -> p a i k", i=3)
        carve = arena(shared[:, :])
        mneg = carve(2, TB)[0:XH]
        mp = carve(3, TB, dt=BF16)[0:XH]
        carve = arena(slot0)
        win, vin, wout = (carve(NPS, P) for _ in range(3))
        wox = carve(NHG, D)
        dsel, bo = carve(P), carve(D)
        gate = carve(E)
        csel = carve(E // 2, P, dt=BF16)[0:3 * E]
        carve = arena(probs)
        rden, hsig, hid = (carve(2, TB) for _ in range(3))

        xT = sb("xT", [D, T])
        xtok = sb("xtok", [P, NB * NC, D])
        wqk = sb("wqk", [D, 2, P])
        wvg = sb("wvg", [D, 2, 256])
        w1 = sb("w1", [D, 16])
        w2 = sb("w2", [16, P])
        b2 = sb("b2", [P, 1])
        gnw = sb("gnw", [P, DV])
        wo = sb("wo", [P, 2, D])
        eye = sb("eye", [P, P])
        lmask = sb("lmask", [P, LEVELS, TB // 2], BF16)
        bdmask = sb("bdmask", [P, 256])
        xw = sb("xw", [D, 3, P])
        xb = sb("xb", [P, 2])
        bv = sb("bv", [P, P])
        low = sb("low", [16, TB])
        dec = sb("dec", [P, NC])
        state = sb("state", [P, NB * NC + 1, 256])
        ln_r = sb("ln_r", [P, NC, D])
        st6 = sb("st6", [P, NC, 6])
        mv = sb("mv", [P, NC, 2])
        rs = sb("rs", [P, 4, 16])
        x1 = sb("x1", [P, NB * NC, D])
        x1T = sb("x1T", [P, TB])
        qp = sb("qp", [P, 3, TB], BF16)
        mk = sb("mk", [KT, 2, P])
        mkp = sb("mkp", [KT, 3, P], BF16)
        mpart = sb("mpart", [P, 2, 4])
        mall = sb("mall", [P, UNITS * HG * NC])

        ssq = sb("ssq", [P, GH * NC])
        rt = sb("rt", [P, 3, NC, E])
        top = sb("top", [P, NC, 8])
        cb = sb("cb", [P, NC, E], BF16)
        comb = sb("comb", [P, NC, 3 * E])
        combT = sb("combT", [3 * E, TB], BF16)

        k_dram = dram("k_dram", [XH, SPLIT, SP], BF16)
        q_dram = dram("q_dram", [NB, 3, XH, DH, TB], BF16)
        m_dram = dram("m_dram", [NB, 3, XH, TB], BF16)
        mask_dram = dram("mask_dram", [3, SP], BF16)

        S = {}

        def s(name):
            if name not in S:
                S[name] = sem(name)
            return S[name]

        loads = {
            "ctx": [(ctxT[:, 0:SKV], A["ctxT"])],
            "xw": [(xw[:, 0, :], A["xWq"]), (xw[:, 1, :], A["xWk"]), (xw[:, 2, :], A["xWv"]),
                   (xb[:, 0:1], A["xbq"].rearrange("(p a) -> p a", a=1)),
                   (xb[:, 1:2], A["xbk"].rearrange("(p a) -> p a", a=1)),
                   (bv[:, :], A["xbv"].partition_broadcast(P))],
            "gw": [(wqk[:, 0, :], A["Wq"]), (wqk[:, 1, :], A["Wk"]), (w1[:, :], A["gk_w1"]),
                   (w2[:, :], A["gk_w2"]), (b2[:, :], A["gk_b2"].rearrange("(p a) -> p a", a=1)),
                   (wvg[:, 0, :], A["Wv"]), (wvg[:, 1, :], A["Wg"]),
                   (gnw[:, :], A["g_norm_w"].partition_broadcast(P)),
                   (wo[:, :, :], A["Wo"].rearrange("(a p) n -> p a n", p=P))],
            "x": [(xT[:, :], A["xT"]), (xtok[:, :, :], A["x"].rearrange("(c p) d -> p c d", p=P))],
            "late": [(bo[:, :], A["xbo"].partition_broadcast(P)), (dsel[:, :], A["c_dsel"]),
                     (gate[:, :], A["gate_wT"]), (csel[:, :, :], A["c_csel"]),
                     (win[:, 0, :], A["ws_in"]), (vin[:, 0, :], A["vs_in"]), (wout[:, 0, :], A["ws_out"]),
                     (win[:, 1:, :], A["e_winT"].rearrange("d (p n) -> d p n", n=P)),
                     (vin[:, 1:, :], A["e_vinT"].rearrange("d (p n) -> d p n", n=P)),
                     (wout[:, 1:, :], A["e_wout"].rearrange("(p n) d -> n p d", n=P))] +
                    [(wox[32 * h:32 * h + DH, :, :],
                      A["xWo"].rearrange("(g h d) n -> h d g n", h=HG, d=DH)[h]) for h in range(HG)],
            "cst": [(eye[:, :], A["c_eye"]), (lmask[:, :, :], A["c_lmask"]), (bdmask[:, :], A["c_bd"])],
        }
        LAST = SKV - (KT - 1) * P

        block = ctx.enter_context(nc.Block())

        @block.sync
        def _(sp):
            def load(key):
                for dst, src in loads[key]:
                    sp.dma_start(dst, src).then_inc(s("in_" + key), 16)

            load("xw")
            load("ctx")
            load("gw")
            load("x")
            load("cst")
            sp.wait_ge(s("mask_clear"), 1)
            sp.dma_start(mk[0:KT - 1, 0, :], A["mask"][0:(KT - 1) * P].rearrange("(a b) -> a b", b=P))\
              .then_inc(s("in_mask"), 16)
            sp.dma_start(mk[KT - 1:KT, 0, 0:LAST], A["mask"][(KT - 1) * P:SKV].rearrange("(a b) -> a b", a=1))\
              .then_inc(s("in_mask"), 16)
            for c in range(NG):
                sp.wait_ge(s("k_parts"), c + 1)
                for r in range(6):
                    sp.dma_start(k_dram[:, 8 * r:8 * r + 8, KC * c:KC * c + KC], kp[:, c % 2, K_PART[r], :])\
                      .then_inc(s(f"k_out{c % 2}"), 16)
            sp.wait_ge(s("k_out0"), 16 * 6 * (NG - NG // 2))
            sp.wait_ge(s("k_out1"), 16 * 6 * (NG // 2))
            sp.wait_ge(s("q_zero"), 1)
            for b in range(NB):
                sp.wait_ge(s("q_parts"), b + 1)
                sp.dma_start(q_dram[b].rearrange("i h d t -> (h d) i t"), qp[:, :, :]).then_inc(s("q_out"), 16)
                sp.wait_ge(s("q_out"), 16 * (b + 1))
                for par in range(2):
                    heads = slice(XH * b + par, XH * (b + 1), 2)
                    sp.dma_start(qaug[HALF * par:HALF * par + 3, heads, :], A["c_ones"]).then_inc(s("q_in"), 16)
                    for r in range(6):
                        row = HALF * par + ROW_SPLIT + 8 * r
                        sp.dma_start(qaug[row:row + 8, heads, :],
                                     q_dram[b, Q_PART[r], par:XH:2, :, :].rearrange("h d t -> d h t"))\
                          .then_inc(s("q_in"), 16)

            sp.wait_ge(s("mask_parts"), 1)
            for i in range(3):
                sp.dma_start(mask_dram[i].rearrange("(a b) -> a b", b=P), mkp[:, i, :])\
                  .then_inc(s("mask_out"), 16)
            sp.wait_ge(s("mask_out"), 48)
            sp.wait_ge(s("ctx_used"), 1)
            sp.wait_ge(s("x1T_sb"), NB)
            sp.wait_ge(s("q_parts"), NB)
            for slot in range(2):
                for par in range(2):
                    for pair in range(2):
                        sp.dma_start(kbuf[HALF * par:HALF * par + 3, slot, pair, :], mask_dram)\
                          .then_inc(s("k_rows"), 16)
                        sp.dma_start(kbuf[HALF * par + ROW_MAX:HALF * par + HALF, slot, pair, :], A["c_krows"])\
                          .then_inc(s("k_rows"), 16)
            def load_keys(v, slot, phase):
                sp.wait_ge(s("k_slot_free"), v * 2 + (phase * UNITS + slot + 1))
                head = (v % 2) * (2 * HG) + slot * HG
                for par in range(2):
                    sp.dma_start(kbuf[HALF * par + ROW_SPLIT:HALF * par + ROW_MAX, slot, :, :],
                                 k_dram[bass.ds(head, HG), :, :].rearrange("(a two) r k -> two r a k", two=2)[par])\
                      .then_inc(s(f"keys_in{slot}"), 16)

            with sp.Fori(0, UNITS // 2) as v:
                load_keys(v, 0, 0)
                load_keys(v, 1, 0)
            for b in range(NB):
                sp.wait_ge(s("m_parts"), b + 1)
                sp.dma_start(m_dram[b].rearrange("i h t -> h i t"), mp[:, :, :]).then_inc(s("m_out"), 16)
                sp.wait_ge(s("m_out"), 16 * (b + 1))
                for par in range(2):
                    sp.dma_start(qaug[HALF * par + ROW_MAX:HALF * par + ROW_MAX + 3,
                                      XH * b + par:XH * (b + 1):2, :],
                                 m_dram[b, :, par:XH:2, :]).then_inc(s("m_in"), 16)
            with sp.Fori(0, UNITS // 2) as v:
                load_keys(v, 0, 1)
                load_keys(v, 1, 1)
            sp.wait_ge(s("wox_zero"), 1)
            load("late")
            for b in range(NB):
                sp.wait_ge(s("y_ready"), b + 1)
                sp.dma_start(out[b * TB:(b + 1) * TB, :].rearrange("(c p) d -> p c d", p=P), x1[:, NC * b:NC * b + NC, :])\
                  .then_inc(s("stored"), 16)
            sp.wait_ge(s("stored"), 16 * NB)

        @block.gpsimd
        def _(pool):
            order = [0]

            def link(ins):
                order[0] += 1
                ins.then_inc(s("pool_order"), 1)
                pool.wait_ge(s("pool_order"), order[0])

            for b in range(NB):
                for lv in range(LEVELS):
                    m = 1 << lv
                    pv = pre[:, :].rearrange("p (n two m) -> p n two m", two=2, m=m)
                    sv = suf[:, :].rearrange("p (n two m) -> p n two m", two=2, m=m)
                    pool.wait_ge(s("lvl_exp"), b * LEVELS + lv + 1)
                    link(pool.tensor_tensor(sv[:, :, 0, :], sv[:, :, 0, :],
                                            rep(pv[:, :, 1, m - 1], 2, m), ALU.add))
                    pool.tensor_tensor(pv[:, :, 1, :], pv[:, :, 1, :],
                                       rep(pv[:, :, 0, m - 1], 2, m), ALU.add).then_inc(s("lvl_upd"), 1)
                    pool.wait_ge(s("lvl_upd"), b * LEVELS + lv + 1)

            pool.wait_ge(s("v_aug"), 1)
            pool.wait_ge(s("v_zero"), 1)
            with pool.Fori(0, UNITS // 2) as v:
                for slot in range(2):
                    head = (v % 2) * (2 * HG) + slot * HG
                    with pool.Fori(0, NG) as g:
                        for i in range(GT):
                            pool.wait_ge(s("p_free"), (v * (2 * NG) + slot * NG + g) * STEPS + (2 + i))
                            pool.tensor_copy(vst[:, i, :, 0:DH],
                                             vaug[:, bass.ds(g * GT + i, 1), bass.ds(head, HG), :])\
                                .then_inc(s("v_staged"), 1)

        @block.scalar
        def _(act):
            act.preload_act_table_set("natural_log_exp_and_others")
            order = [0]

            def link(ins):
                order[0] += 1
                ins.then_inc(s("act_order"), 1)
                act.wait_ge(s("act_order"), order[0])

            act.wait_ge(s("in_xw"), 16 * len(loads["xw"]))
            for c in range(NG):
                act.wait_ge(s("k_ps"), c + 1)
                if c >= 2:
                    act.wait_ge(s("k_parts"), c - 1)
                act.activation(kf[:, c % 2, :], ps[:, c % 2, 0:KC], ACT.Identity, bias=xb[:, 1:2])\
                   .then_inc(s("k_f"), 1)

            def rsqrt(n):
                act.wait_ge(s("rs_in"), n)
                link(act.activation(rs[:, 1, :], rs[:, 0, :], ACT.Ln))
                act.activation(rs[:, 2, :], rs[:, 1, :], ACT.Exp, scale=-0.5).then_inc(s("rs_exp"), 1)

            act.wait_ge(s("in_gw"), 16 * len(loads["gw"]))
            for b in range(NB):
                act.wait_ge(s("qk_ps"), b + 1)
                act.activation(q_t[:, :], ps[:, 0, :], ACT.Copy, scale=float(DK) ** -0.5)\
                   .then_inc(s("q_sb"), 1)
                act.wait_ge(s("z_ps"), b + 1)
                link(act.activation(z1[:, :], ps[:, 3, :], ACT.Abs, bias=b2[:, 0:1]))
                act.sem_inc(s("abs_sb"), 1)
                link(act.activation(z2[:, :], z1[:, :], ACT.Exp, scale=-1.0))
                act.activation(z1[:, :], z2[:, :], ACT.Ln, bias=1.0).then_inc(s("log_sb"), 1)
                for lv in range(LEVELS):
                    m = 1 << lv
                    pv = pre[:, :].rearrange("p (n two m) -> p n two m", two=2, m=m)
                    sv = suf[:, :].rearrange("p (n two m) -> p n two m", two=2, m=m)
                    if lv == 0:
                        act.wait_ge(s("gate"), b + 1)
                    else:
                        act.wait_ge(s("lvl_upd"), b * LEVELS + lv)
                    if b * LEVELS + lv >= 2:
                        act.wait_ge(s("lvl_kq"), b * LEVELS + lv - 1)
                    e1 = ek[:, lv % 2, :].rearrange("p (n m) -> p n m", m=m)
                    e2 = eq[:, lv % 2, :].rearrange("p (n m) -> p n m", m=m)
                    act.activation(e1, sv[:, :, 0, :], ACT.Exp, scale=1.0 / 16)
                    act.activation(e2, pv[:, :, 1, :], ACT.Exp, scale=1.0 / 16).then_inc(s("lvl_exp"), 1)
                    if lv == 0:
                        act.wait_ge(s("vg_ps"), b + 1)
                        if b:
                            act.wait_ge(s("og"), b)
                        act.activation(gw, ps[:, 4:8, 256:512], ACT.Exp, scale=-1.0)\
                           .then_inc(s("gate_exp"), 1)
                act.wait_ge(s("lvl_upd"), (b + 1) * LEVELS)
                act.activation(z1[:, :], suf[:, :], ACT.Exp, scale=1.0 / 16)
                act.activation(z2[:, :], pre[:, :], ACT.Exp, scale=1.0 / 16)
                act.activation(dec[:, :], pre[:, P - 1:TB:P], ACT.Exp, scale=1.0 / 16)\
                   .then_inc(s("fin_exp"), 1)
                act.wait_ge(s("o_ps"), b + 1)
                act.activation(sq, ps[:, 4:8, 0:256], ACT.Square).then_inc(s("o_sq"), 1)
                rsqrt(2 * b + 1)
                act.wait_ge(s("ogT_ps"), b + 1)
                act.activation(ogT, ps[:, 0:2, :], ACT.Copy).then_inc(s("ogT_sb"), 1)
                rsqrt(2 * b + 2)
                act.wait_ge(s("x1T_ps"), b + 1)
                act.activation(x1T[:, :], ps[:, 3, :], ACT.Copy).then_inc(s("x1T_sb"), 1)

            act.sem_inc(s("s_free"), 2)
            act.wait_ge(s("x1T_sb"), NB)
            with act.Fori(0, UNITS * NG) as g:
                for a in range(STEPS):
                    act.wait_ge(s("scores"), g * STEPS + (a + 1))
                    act.wait_ge(s("p_free"), g * STEPS + (a + 1))
                    act.activation(prob[:, a, :, :], ps[:, 3 * (a % 2):3 * (a % 2) + 3, :], ACT.Exp)\
                       .then_inc(s("s_free"), 1)

            for b in range(NB):
                rsqrt(2 * NB + 2 * b + 1)
                act.wait_ge(s("x2T_ps"), b + 1)
                act.activation(x1T[:, :], ps[:, 1, :], ACT.Copy).then_inc(s("x2T_sb"), 1)
                act.wait_ge(s("rt_ps"), b + 1)
                act.activation(rt[:, 1, :, :], ps[:, 2, 0:NC * E].rearrange("p (c e) -> p c e", e=E),
                               ACT.Exp, scale=-1.0).then_inc(s("rt_exp"), 1)
                for p in range(NPS):
                    n = b * NPS + p
                    act.wait_ge(s("h_ps"), n + 1)
                    if n >= 2:
                        act.wait_ge(s("hid"), n - 1)
                    act.activation(hsig[:, n % 2, :], ps[:, 1 + 3 * (n % 2), :], ACT.Exp, scale=-1.0)\
                       .then_inc(s("h_exp"), 1)
                rsqrt(2 * NB + 2 * b + 2)

        @block.vector
        def _(dve):
            order = [0]

            def link(ins):
                order[0] += 1
                ins.then_inc(s("dve_order"), 1)
                dve.wait_ge(s("dve_order"), order[0])

            dve.memset(mk[:, 0, :], 3e29).then_inc(s("mask_clear"), 1)
            dve.memset(ctxT[:, SKV:SP], 0.0).then_inc(s("ctx_pad"), 1)
            dve.memset(qaug[:, :, :], 0.0).then_inc(s("q_zero"), 1)
            link(dve.memset(vst[:, :, :, :], 0.0))
            dve.memset(vst[:, :, :, DH:DH + 1], 1.0).then_inc(s("v_zero"), 1)
            dve.memset(state[:, 0, :], 0.0)
            link(dve.memset(k_l[:, :, :], 0.0))

            dve.wait_ge(s("in_mask"), 32)
            link(dve.tensor_scalar(mk[:, 1, :], mk[:, 0, :], -1e9, None, ALU.mult))
            link(dve.tensor_copy(mkp[:, 0, :], mk[:, 1, :]))
            link(dve.tensor_tensor(mk[:, 0, :], mk[:, 1, :], mkp[:, 0, :], ALU.subtract))
            link(dve.tensor_copy(mkp[:, 1, :], mk[:, 0, :]))
            dve.tensor_tensor(mkp[:, 2, :], mk[:, 0, :], mkp[:, 1, :], ALU.subtract)\
               .then_inc(s("mask_parts"), 1)

            def split3(parts, full, rest, done):
                link(dve.tensor_copy(parts(0), full))
                link(dve.tensor_tensor(rest, full, parts(0), ALU.subtract))
                link(dve.tensor_copy(parts(1), rest))
                dve.tensor_tensor(parts(2), rest, parts(1), ALU.subtract).then_inc(s(done), 1)

            for c in range(NG):
                dve.wait_ge(s("k_f"), c + 1)
                if c >= 2:
                    dve.wait_ge(s(f"k_out{c % 2}"), 16 * 6 * (c // 2))
                split3(lambda i: kp[:, c % 2, i, :], kf[:, c % 2, :], kr[:, :], "k_parts")
                dve.wait_ge(s("v_ps"), c + 1)
                if c == 0:
                    dve.wait_ge(s("in_xw"), 16 * len(loads["xw"]))
                ins = dve.tensor_tensor(vaug[:, GT * c:GT * c + GT, :, 0:DH],
                                        ps[:, 2 + c % 2, 0:GT * P].rearrange("p (a h d) -> p a h d", a=GT, h=XH),
                                        rep(bv[:, :], 1, GT).rearrange("p a (h d) -> p a h d", h=XH), ALU.add)
                link(ins)
                dve.sem_inc(s("v_done"), 1)
            dve.sem_inc(s("v_aug"), 1)

            def rsqrt(src, scale, n, idx):
                dve.memset(rs[:, 0, :], 1.0)
                link(dve.memset(rs[:, 3, :], 1.0))
                dve.tensor_scalar(rs[:, 0, 0:n], src, scale, EPS, ALU.mult, ALU.add).then_inc(s("rs_in"), 1)
                dve.wait_ge(s("rs_exp"), idx)
                link(dve.tensor_tensor(rs[:, 1, 0:n], rs[:, 2, 0:n], rs[:, 2, 0:n], ALU.mult))
                link(dve.tensor_tensor(rs[:, 1, 0:n], rs[:, 1, 0:n], rs[:, 0, 0:n], ALU.mult))
                link(dve.tensor_scalar(rs[:, 1, 0:n], rs[:, 1, 0:n], -0.5, 1.5, ALU.mult, ALU.add))
                link(dve.tensor_tensor(rs[:, 3, 0:n], rs[:, 2, 0:n], rs[:, 1, 0:n], ALU.mult))

            def layer_norm(b, idx, done):
                for c in range(NC):
                    link(dve.bn_stats(st6[:, c, :], ln_r[:, c, :]))
                for c in range(NC):
                    link(dve.bn_aggr(mv[:, c, :], st6[:, c, :]))
                rsqrt(mv[:, :, 1], 1.0, NC, idx)
                for c in range(NC):
                    link(dve.tensor_scalar(x1[:, NC * b + c, :], ln_r[:, c, :], mv[:, c, 0:1], rs[:, 3, c:c + 1],
                                           ALU.subtract, ALU.mult))
                dve.sem_inc(s(done), 1)

            dve.wait_ge(s("in_gw"), 16 * len(loads["gw"]))
            dve.wait_ge(s("in_cst"), 16 * len(loads["cst"]))
            dve.wait_ge(s("in_x"), 16 * len(loads["x"]))
            for b in range(NB):
                dve.wait_ge(s("low_ps"), b + 1)
                link(dve.tensor_copy(low[:, :], ps[0:16, 2, :]))
                dve.sem_inc(s("low_sb"), 1)
                dve.wait_ge(s("qk_ps"), b + 1)
                dve.tensor_copy(k_t[:, :], ps[:, 1, :]).then_inc(s("k_sb"), 1)
                link(dve.memset(suf[:, :], 0.0))
                dve.wait_ge(s("abs_sb"), b + 1)
                link(dve.tensor_scalar(zm[:, :], ps[:, 3, :], b2[:, 0:1], 0.0, ALU.add, ALU.min))
                dve.wait_ge(s("log_sb"), b + 1)
                dve.tensor_tensor(pre[:, :], zm[:, :], z1[:, :], ALU.subtract).then_inc(s("gate"), 1)
                dve.wait_ge(s("gate_exp"), b + 1)
                link(dve.tensor_copy(v_g, ps[:, 4:8, 0:256]))
                dve.sem_inc(s("v_sb"), 1)
                link(dve.tensor_scalar(gw, gw, 1.0, None, ALU.add))
                link(dve.reciprocal(gw, gw))
                link(dve.tensor_tensor(gw, gw, ps[:, 4:8, 256:512], ALU.mult))
                dve.sem_inc(s("vg_free"), 1)
                gw4 = gw.rearrange("p c (h v) -> p (c h) v", v=DV)
                link(dve.tensor_tensor(gw4, gw4, rep(gnw[:, :], 1, NC * GH), ALU.mult))
                dve.wait_ge(s("diag_ps"), b + 1)
                link(dve.tensor_tensor(a_sc.rearrange("p h (c t) -> p (h c) t", c=NC),
                                       ps[:, 0:4, :].rearrange("p h (c t) -> p (h c) t", c=NC),
                                       rep(eye[:, :], 1, GH * NC), ALU.mult))
                dve.sem_inc(s("a_diag"), 1)

                def decayed(lv):
                    m = 1 << lv
                    n = b * LEVELS + lv
                    dve.wait_ge(s("lvl_exp"), n + 1)
                    if n >= 2:
                        dve.wait_ge(s("lvl_ps"), n - 1)
                    two = lambda t: t.rearrange("p (n two m) -> p n two m", two=2, m=m)
                    one = lambda t: t.rearrange("p (n m) -> p n m", m=m)
                    dve.tensor_tensor(two(k_l[:, lv % 2, :])[:, :, 0, :], two(k_t[:, :])[:, :, 0, :],
                                      one(ek[:, lv % 2, :]), ALU.mult)
                    dve.tensor_tensor(one(q_l[:, lv % 2, :]), two(q_t[:, :])[:, :, 1, :],
                                      one(eq[:, lv % 2, :]), ALU.mult).then_inc(s("lvl_kq"), 1)

                def select(lv):
                    m = 1 << lv
                    dve.wait_ge(s("lvl_ps"), b * LEVELS + lv + 1)
                    bank = 4 * ((lv + 1) % 2)
                    tgt = a_sc.rearrange("p h (n two m) -> p h n two m", two=2, m=m)[:, :, :, 1, :]
                    src = ps[:, bank:bank + 4, 0:TB // 2].rearrange("p h (n m) -> p h n m", m=m)
                    msk = rep(lmask[:, lv, :].bitcast(U16), 1, GH).rearrange("p h (n m) -> p h n m", m=m)
                    link(dve.copy_predicated(tgt, msk, src))
                    dve.sem_inc(s("a_sel"), 1)

                decayed(0)
                for lv in range(1, LEVELS):
                    decayed(lv)
                    select(lv - 1)
                select(LEVELS - 1)
                dve.wait_ge(s("fin_exp"), b + 1)
                dve.tensor_tensor(kd, k_t[:, :], z1[:, :], ALU.mult)
                dve.tensor_tensor(qd, q_t[:, :], z2[:, :], ALU.mult).then_inc(s("qkd"), 1)
                dve.wait_ge(s("ktok_ps"), b + 1)
                dve.tensor_copy(ktok[:, :, :], ps[:, 0, :].rearrange("p (c n) -> p c n", c=NC))\
                   .then_inc(s("ktok_sb"), 1)
                dve.wait_ge(s("kv_ps"), b + 1)
                link(dve.tensor_tensor(kvtmp, ps[:, 1:3, :].rearrange("p b (c n) -> p (b c) n", c=2),
                                       rep(bdmask[:, :], 1, NC), ALU.mult))
                for c in range(NC):
                    link(dve.scalar_tensor_tensor(state[:, NC * b + c + 1, :], state[:, NC * b + c, :],
                                                  dec[:, c:c + 1], kvtmp[:, c, :], ALU.mult, ALU.add))
                    dve.sem_inc(s("state_ready"), 1)
                dve.wait_ge(s("o_sq"), b + 1)
                link(dve.tensor_reduce(ssq[:, :], sq.rearrange("p c (h v) -> p (c h) v", v=DV), AX.X, ALU.add))
                rsqrt(ssq[:, :], 1.0 / DV, GH * NC, 2 * b + 1)
                r16 = rep(rs[:, 3, 0:GH * NC], 2, DV).rearrange("p (c h) v -> p c h v", c=NC)
                link(dve.tensor_tensor(og.rearrange("p c (h v) -> p c h v", v=DV),
                                       ps[:, 4:8, 0:256].rearrange("p c (h v) -> p c h v", v=DV), r16, ALU.mult))
                link(dve.tensor_tensor(og, og, gw, ALU.mult))
                dve.sem_inc(s("og"), 1)
                dve.wait_ge(s("wo_ps"), b + 1)
                link(dve.tensor_tensor(ln_r[:, :, :], ps[:, 2, :].rearrange("p (c d) -> p c d", c=NC),
                                       xtok[:, NC * b:NC * b + NC, :], ALU.add))
                layer_norm(b, 2 * b + 2, "x1_ready")
                dve.wait_ge(s("q2_ps"), b + 1)
                if b:
                    dve.wait_ge(s("q_out"), 16 * b)
                link(dve.tensor_scalar(z1[:, :], ps[:, 0, :], xb[:, 0:1], float(DH) ** -0.5, ALU.add, ALU.mult))
                split3(lambda i: qp[:, i, :], z1[:, :], z2[:, :], "q_parts")

            dve.sem_inc(s("m_red"), 2)
            with dve.Fori(0, UNITS) as u:
                with dve.Fori(0, HG * NC) as r:
                    for j in range(4):
                        n = 4 if j < 3 else 1
                        w = 512 if j < 3 else SP - 12 * 512
                        dve.wait_ge(s("m_ps"), u * (HG * NC * 4) + r * 4 + (j + 1))
                        bank = 4 * (j % 2)
                        dve.tensor_reduce(mpart[:, 0, j:j + 1], ps[:, bank:bank + n, 0:w], AX.XY, ALU.max)\
                           .then_inc(s("m_red"), 1)
                    dve.wait_ge(s("m_red"), u * (HG * NC * 4) + r * 4 + 6)
                    dve.tensor_reduce(mall[:, bass.ds(u * (HG * NC) + r, 1)], mpart[:, 0, :], AX.X, ALU.max)\
                       .then_inc(s("m_done"), 1)
                    dve.wait_ge(s("m_done"), u * (HG * NC) + r + 1)
            for b in range(NB):
                dve.wait_ge(s("mT_ps"), b + 1)
                if b:
                    dve.wait_ge(s("m_out"), 16 * b)
                link(dve.tensor_scalar(mneg[:, 0, :], ps[0:XH, 0, :], -1.0, None, ALU.mult))
                dve.sem_inc(s("mT_free"), 1)
                split3(lambda i: mp[:, i, :], mneg[:, 0, :], mneg[:, 1, :], "m_parts")

            dve.sem_inc(s("o_free"), 1)
            with dve.Fori(0, UNITS - 1) as u:
                dve.wait_ge(s("p_free"), u * (NG * STEPS) + (NG * STEPS + STEPS))
                dve.tensor_copy(osb[:, bass.ds(u, 1), :], ps[:, 6, :]).then_inc(s("o_free"), 1)
            dve.wait_ge(s("k_slot_free"), 2 + UNITS + UNITS - 1)
            dve.memset(wox[:, :, :], 0.0).then_inc(s("wox_zero"), 1)
            dve.wait_ge(s("p_free"), UNITS * NG * STEPS + STEPS)
            dve.tensor_copy(osb[:, UNITS - 1, :], ps[:, 6, :]).then_inc(s("o_free"), 1)

            dve.wait_ge(s("in_late"), 16 * len(loads["late"]))
            for b in range(NB):
                for hg in range(NHG):
                    n = b * NHG + hg
                    dve.wait_ge(s("den_ps"), n + 1)
                    link(dve.reciprocal(rden[:, n % 2, :], ps[:, 2 + n % 2, :]))
                    link(dve.tensor_tensor(osb[:, n, :], osb[:, n, :], rden[:, n % 2, :], ALU.mult))
                    dve.sem_inc(s("o_norm"), 1)
                dve.wait_ge(s("xo_ps"), b + 1)
                link(dve.tensor_tensor(ln_r[:, :, :], ps[:, 0, :].rearrange("p (c d) -> p c d", c=NC),
                                       x1[:, NC * b:NC * b + NC, :], ALU.add))
                link(dve.tensor_tensor(ln_r[:, :, :], ln_r[:, :, :], rep(bo[:, :], 1, NC), ALU.add))
                layer_norm(b, 2 * NB + 2 * b + 1, "x2_ready")
                dve.wait_ge(s("rt_exp"), b + 1)
                link(dve.tensor_copy(rt[:, 0, :, :], ps[:, 2, 0:NC * E].rearrange("p (c e) -> p c e", e=E)))
                dve.sem_inc(s("rt_sb"), 1)
                for c in range(NC):
                    link(dve.max(top[:, c, :], rt[:, 0, c, :]))
                link(dve.memset(top[:, :, TOPK:8], 3e38))
                for c in range(NC):
                    link(dve.match_replace(rt[:, 2, c, :], top[:, c, :], rt[:, 0, c, :], -3e38))
                dve.wait_ge(s("rt_exp"), b + 1)
                link(dve.tensor_scalar(rt[:, 1, :, :], rt[:, 1, :, :], 1.0, None, ALU.add))
                link(dve.reciprocal(rt[:, 1, :, :], rt[:, 1, :, :]))
                link(dve.tensor_scalar(rt[:, 2, :, :], rt[:, 2, :, :], -3e38, None, ALU.is_equal))
                link(dve.tensor_tensor(rt[:, 1, :, :], rt[:, 1, :, :], rt[:, 2, :, :], ALU.mult))
                link(dve.tensor_reduce(st6[:, :, 0], rt[:, 1, :, :], AX.X, ALU.add))
                link(dve.reciprocal(st6[:, :, 1], st6[:, :, 0]))
                link(dve.tensor_tensor(rt[:, 1, :, :], rt[:, 1, :, :], rep(st6[:, :, 1], 2, E), ALU.mult))
                link(dve.tensor_copy(cb[:, :, :], rt[:, 1, :, :]))
                link(dve.tensor_copy(comb[:, :, 0:E], cb[:, :, :]))
                link(dve.tensor_tensor(rt[:, 2, :, :], rt[:, 1, :, :], comb[:, :, 0:E], ALU.subtract))
                link(dve.tensor_copy(cb[:, :, :], rt[:, 2, :, :]))
                link(dve.tensor_copy(comb[:, :, E:2 * E], cb[:, :, :]))
                link(dve.tensor_tensor(comb[:, :, 2 * E:3 * E], rt[:, 2, :, :], comb[:, :, E:2 * E], ALU.subtract))
                dve.sem_inc(s("comb"), 1)
                dve.wait_ge(s("cT_ps"), b + 1)
                link(dve.tensor_copy(combT[:, :], ps[0:3 * E, 0, :]))
                dve.sem_inc(s("combT"), 1)
                for p in range(NPS):
                    n = b * NPS + p
                    bank = 1 + 3 * (n % 2)
                    dve.wait_ge(s("h_exp"), n + 1)
                    if n >= 2:
                        dve.wait_ge(s("y_mm"), n - 1)
                    dve.wait_ge(s("hv_ps"), n + 1)
                    if p:
                        dve.wait_ge(s("hc_ps"), b * (NPS - 1) + p)
                    h = hsig[:, n % 2, :]
                    link(dve.tensor_scalar(h, h, 1.0, None, ALU.add))
                    link(dve.reciprocal(h, h))
                    link(dve.tensor_tensor(h, h, ps[:, bank, :], ALU.mult))
                    if p:
                        link(dve.tensor_tensor(h, h, ps[:, bank + 2, :], ALU.mult))
                    link(dve.tensor_tensor(hid[:, n % 2, :], h, ps[:, bank + 1, :], ALU.mult))
                    dve.sem_inc(s("hid"), 1)
                dve.wait_ge(s("y_mm"), (b + 1) * NPS)
                link(dve.tensor_tensor(ln_r[:, :, :], ps[:, 7, :].rearrange("p (c d) -> p c d", c=NC),
                                       x1[:, NC * b:NC * b + NC, :], ALU.add))
                dve.sem_inc(s("y_free"), 1)
                layer_norm(b, 2 * NB + 2 * b + 2, "y_ready")

        @block.tensor
        def _(pe):
            mm = pe.matmul

            pe.wait_ge(s("in_xw"), 16 * len(loads["xw"]))
            pe.wait_ge(s("in_ctx"), 16)
            pe.wait_ge(s("ctx_pad"), 1)
            for c in range(NG):
                if c >= 2:
                    pe.wait_ge(s("k_f"), c - 1)
                    pe.wait_ge(s("v_done"), c - 1)
                mm(ps[:, c % 2, 0:KC], xw[:, 1, :], ctxT[:, KC * c:KC * c + KC], start=True, stop=True)\
                    .then_inc(s("k_ps"), 1)
                for i in range(GT):
                    ins = mm(ps[:, 2 + c % 2, P * i:P * i + P], ctxT[:, KC * c + P * i:KC * c + P * i + P],
                             xw[:, 2, :], start=True, stop=True)
                ins.then_inc(s("v_ps"), 1)

            pe.wait_ge(s("v_ps"), NG)
            pe.sem_inc(s("ctx_used"), 1)
            pe.wait_ge(s("in_gw"), 16 * len(loads["gw"]))
            pe.wait_ge(s("in_x"), 16 * len(loads["x"]))
            pe.wait_ge(s("in_cst"), 16 * len(loads["cst"]))
            pe.wait_ge(s("k_f"), NG)
            pe.wait_ge(s("v_done"), NG)
            for b in range(NB):
                xb_ = xT[:, TB * b:TB * b + TB]
                if b:
                    pe.wait_ge(s("q_parts"), b)
                    pe.wait_ge(s("x1T_sb"), b)
                mm(ps[0:16, 2, :], w1[:, :], xb_, start=True, stop=True).then_inc(s("low_ps"), 1)
                mm(ps[:, 0, :], wqk[:, 0, :], xb_, start=True, stop=True)
                mm(ps[:, 1, :], wqk[:, 1, :], xb_, start=True, stop=True).then_inc(s("qk_ps"), 1)
                pe.wait_ge(s("low_sb"), b + 1)
                mm(ps[:, 3, :], w2[:, :], low[:, :], start=True, stop=True).then_inc(s("z_ps"), 1)
                for c in range(NC):
                    ins = mm(ps[:, 4 + c, :], xT[:, TB * b + P * c:TB * b + P * c + P],
                             wvg[:, :, :].rearrange("p a n -> p (a n)"), start=True, stop=True)
                ins.then_inc(s("vg_ps"), 1)

                def heads_scores(bank, keys, queries, width):
                    for c in range(NC):
                        for h in range(GH):
                            r = slice(DK * h, DK * h + DK)
                            ins = mm(ps[:, bank + h, width * c:width * c + width], keys[r, P * c:P * c + P],
                                     queries[r, width * c:width * c + width], start=True, stop=True)
                    return ins

                pe.wait_ge(s("q_sb"), b + 1)
                pe.wait_ge(s("k_sb"), b + 1)
                pe.wait_ge(s("gate"), b + 1)
                heads_scores(0, k_t[:, :], q_t[:, :], P).then_inc(s("diag_ps"), 1)
                for lv in range(LEVELS):
                    pe.wait_ge(s("lvl_kq"), b * LEVELS + lv + 1)
                    if lv == 0:
                        pe.wait_ge(s("vg_free"), b + 1)
                    elif lv == 1:
                        pe.wait_ge(s("a_diag"), b + 1)
                    else:
                        pe.wait_ge(s("a_sel"), b * LEVELS + lv - 1)
                    heads_scores(4 * ((lv + 1) % 2), k_l[:, lv % 2, :], q_l[:, lv % 2, :], P // 2)\
                        .then_inc(s("lvl_ps"), 1)
                pe.wait_ge(s("a_sel"), b * LEVELS + LEVELS - 1)
                pe.wait_ge(s("qkd"), b + 1)
                for c in range(NC):
                    ins = pe.transpose(ps[:, 0, P * c:P * c + P], kd[:, P * c:P * c + P], eye[:, :])
                ins.then_inc(s("ktok_ps"), 1)
                pe.wait_ge(s("ktok_sb"), b + 1)
                pe.wait_ge(s("v_sb"), b + 1)
                for c in range(NC):
                    ins = mm(ps[:, 1 + c // 2, 256 * (c % 2):256 * (c % 2) + 256], ktok[:, c, :], v_g[:, c, :],
                             start=True, stop=True)
                ins.then_inc(s("kv_ps"), 1)
                pe.wait_ge(s("a_sel"), (b + 1) * LEVELS)
                for c in range(NC):
                    if NC * b + c:
                        pe.wait_ge(s("state_ready"), NC * b + c)
                    mm(ps[:, 4 + c, 0:256], qd[:, P * c:P * c + P], state[:, NC * b + c, :],
                       start=True, stop=False, skip_group_check=True)
                    for h in range(GH):
                        ins = mm(ps[:, 4 + c, DV * h:DV * h + DV], a_sc[:, h, P * c:P * c + P],
                                 v_g[:, c, DV * h:DV * h + DV], start=False, stop=(h == GH - 1),
                                 skip_group_check=True)
                ins.then_inc(s("o_ps"), 1)
                pe.wait_ge(s("og"), b + 1)
                pe.wait_ge(s("state_ready"), NC * (b + 1))
                for a in range(2):
                    for c in range(NC):
                        ins = pe.transpose(ps[:, a, P * c:P * c + P], og[:, c, P * a:P * a + P], eye[:, :])
                ins.then_inc(s("ogT_ps"), 1)
                pe.wait_ge(s("ogT_sb"), b + 1)
                for c in range(NC):
                    for a in range(2):
                        ins = mm(ps[:, 2, P * c:P * c + P], ogT[:, a, P * c:P * c + P], wo[:, a, :],
                                 start=(a == 0), stop=(a == 1))
                ins.then_inc(s("wo_ps"), 1)
                pe.wait_ge(s("x1_ready"), b + 1)
                for c in range(NC):
                    ins = pe.transpose(ps[:, 3, P * c:P * c + P], x1[:, NC * b + c, :], eye[:, :])
                ins.then_inc(s("x1T_ps"), 1)
                pe.wait_ge(s("x1T_sb"), b + 1)
                mm(ps[:, 0, :], xw[:, 0, :], x1T[:, :], start=True, stop=True).then_inc(s("q2_ps"), 1)

            pe.sem_inc(s("k_slot_free"), 2)
            pe.wait_ge(s("q_in"), 16 * 14 * NB)
            pe.wait_ge(s("k_rows"), 16 * 16)
            pe.wait_ge(s("q_parts"), NB)
            def max_unit(v, slot):
                for h in range(HG):
                    with pe.Fori(0, NC) as i:
                        pe.wait_ge(s(f"keys_in{slot}"), v * 32 + 32)
                        for j in range(4):
                            n = 4 if j < 3 else 1
                            w = 512 if j < 3 else SP - 12 * 512
                            pe.wait_ge(s("m_red"), (v * 2 + slot) * (HG * NC * 4) + i * 4 + (h * NC * 4 + j + 1))
                            for k in range(n):
                                key = 512 * (4 * j + k)
                                ins = mm(ps[:, 4 * (j % 2) + k, 0:w],
                                         qaug[:, bass.ds(v * (2 * HG) + (slot * HG + h), 1), bass.ds(i * P, P)],
                                         kbuf[:, slot, h // 2, key:key + w], start=True, stop=True)
                            ins.then_inc(s("m_ps"), 1)
                pe.wait_ge(s("m_ps"), (v * 2 + slot + 1) * (HG * NC * 4))
                pe.sem_inc(s("k_slot_free"), 1)

            with pe.Fori(0, UNITS // 2) as v:
                max_unit(v, 0)
                max_unit(v, 1)
            pe.wait_ge(s("m_done"), UNITS * HG * NC)
            for b in range(NB):
                if b:
                    pe.wait_ge(s("mT_free"), b)
                for i in range(NC):
                    cols = mall[:, b * XH * NC:(b + 1) * XH * NC].rearrange("p (h i) -> p i h", i=NC)[:, i, :]
                    ins = pe.transpose(ps[0:XH, 0, P * i:P * i + P], cols, eye[:, :])
                ins.then_inc(s("mT_ps"), 1)

            pe.wait_ge(s("m_in"), 16 * 2 * NB)
            pe.wait_ge(s("mT_free"), NB)
            pe.wait_ge(s("v_zero"), 1)
            pe.sem_inc(s("p_free"), STEPS)

            def scores(v, slot, g, a, step):
                pe.wait_ge(s("s_free"), step + 1)
                for i in range(3):
                    tile, h = divmod(3 * a + i, HG)
                    ins = mm(ps[:, 3 * (a % 2) + i, :], kbuf[:, slot, h // 2, bass.ds(g * KC + tile * P, P)],
                             qaug[:, bass.ds(v * (2 * HG) + (slot * HG + h), 1), :], start=True, stop=True)
                ins.then_inc(s("scores"), 1)

            def sums(g_all, a, step, first_group, last_group, unit):
                pe.wait_ge(s("s_free"), step + 3)
                if first_group and a == 0:
                    pe.wait_ge(s("o_free"), unit + 1)
                for i in range(3):
                    tile, h = divmod(3 * a + i, HG)
                    if h == 0:
                        pe.wait_ge(s("v_staged"), g_all * GT + (tile + 1))
                    ins = mm(ps[32 * h:32 * h + 32, 6, :], vst[:, tile, h, :], prob[:, a, i, :],
                             start=(first_group and tile == 0), stop=(last_group and tile == GT - 1), skip_group_check=True)
                ins.then_inc(s("p_free"), 1)

            def group(v, slot, g, first_group, last_group, last_unit):
                g_all = v * (2 * NG) + slot * NG + g
                for a in range(STEPS):
                    step = g_all * STEPS + a
                    sums(g_all, a, step, first_group, last_group, v * 2 + slot)
                    if a + 2 < STEPS:
                        scores(v, slot, g, a + 2, step + 2)
                        if a + 2 == STEPS - 1 and last_group:
                            pe.wait_ge(s("scores"), step + 3)
                            pe.sem_inc(s("k_slot_free"), 1)
                    elif not last_group:
                        scores(v, slot, g + 1, a - 2, step + 2)
                    elif not last_unit:
                        nv, ns = (v, 1) if slot == 0 else (v + 1, 0)
                        if a == 2:
                            pe.wait_ge(s(f"keys_in{ns}"), nv * 32 + (32 + 16 * UNITS))
                        scores(nv, ns, 0, a - 2, step + 2)

            def unit(v, slot, last_unit):
                group(v, slot, 0, True, False, last_unit)
                with pe.Fori(1, NG - 1) as g:
                    group(v, slot, g, False, False, last_unit)
                group(v, slot, NG - 1, False, True, last_unit)

            pe.wait_ge(s("keys_in0"), 16 * UNITS + 32)
            scores(0, 0, 0, 0, 0)
            scores(0, 0, 0, 1, 1)
            with pe.Fori(0, UNITS // 2 - 1) as v:
                unit(v, 0, False)
                unit(v, 1, False)
            unit(UNITS // 2 - 1, 0, False)
            unit(UNITS // 2 - 1, 1, True)

            pe.wait_ge(s("in_late"), 16 * len(loads["late"]))
            pe.wait_ge(s("o_free"), UNITS + 1)
            pe.wait_ge(s("s_free"), UNITS * NG * STEPS + 2)
            for b in range(NB):
                if b:
                    pe.wait_ge(s("y_free"), b)
                for hg in range(NHG):
                    n = b * NHG + hg
                    if n >= 2:
                        pe.wait_ge(s("o_norm"), n - 1)
                    mm(ps[:, 2 + n % 2, :], dsel[:, :], osb[:, n, :], start=True, stop=True)\
                        .then_inc(s("den_ps"), 1)
                for hg in range(NHG):
                    n = b * NHG + hg
                    pe.wait_ge(s("o_norm"), n + 1)
                    for c in range(NC):
                        ins = mm(ps[:, 0, P * c:P * c + P], osb[:, n, P * c:P * c + P], wox[:, hg, :],
                                 start=(hg == 0 and c == 0), stop=(hg == NHG - 1), skip_group_check=True)
                ins.then_inc(s("xo_ps"), 1)
                pe.wait_ge(s("x2_ready"), b + 1)
                for c in range(NC):
                    ins = pe.transpose(ps[:, 1, P * c:P * c + P], x1[:, NC * b + c, :], eye[:, :])
                ins.then_inc(s("x2T_ps"), 1)
                pe.wait_ge(s("x2T_sb"), b + 1)
                for c in range(NC):
                    ins = mm(ps[:, 2, E * c:E * c + E], x1T[:, P * c:P * c + P], gate[:, :], start=True, stop=True)
                ins.then_inc(s("rt_ps"), 1)
                for p in range(NPS + 1):
                    if p < NPS:
                        n = b * NPS + p
                        bank = 1 + 3 * (n % 2)
                        if n >= 2:
                            pe.wait_ge(s("hid"), n - 1)
                        if p <= 1:
                            pe.wait_ge(s("rt_exp"), b + 1)
                            pe.wait_ge(s("rt_sb"), b + 1)
                        mm(ps[:, bank, :], win[:, p, :], x1T[:, :], start=True, stop=True).then_inc(s("h_ps"), 1)
                        ins = mm(ps[:, bank + 1, :], vin[:, p, :], x1T[:, :], start=True, stop=True)
                        ins.then_inc(s("hv_ps"), 1)
                        if p == 1:
                            pe.wait_ge(s("comb"), b + 1)
                            for c in range(NC):
                                ins = pe.transpose(ps[0:3 * E, 0, P * c:P * c + P], comb[:, c, :], eye[:, :])
                            ins.then_inc(s("cT_ps"), 1)
                            pe.wait_ge(s("combT"), b + 1)
                        if p:
                            mm(ps[:, bank + 2, :], csel[:, p - 1, :], combT[:, :], start=True, stop=True)\
                                .then_inc(s("hc_ps"), 1)
                    if p:
                        n = b * NPS + p - 1
                        pe.wait_ge(s("hid"), n + 1)
                        for c in range(NC):
                            ins = mm(ps[:, 7, P * c:P * c + P], hid[:, n % 2, P * c:P * c + P], wout[:, p - 1, :],
                                     start=(p == 1 and c == 0), stop=(p == NPS), skip_group_check=True)
                        ins.then_inc(s("y_mm"), 1)


def kernel(**inputs):
    import ml_dtypes
    import numpy as np
    import concourse.bacc as bacc
    from concourse.bass_utils import run_bass_kernel_spmd

    a = {k: np.asarray(v) for k, v in inputs.items()}
    arrays = layout(a, np, ml_dtypes.bfloat16)
    nc = bacc.Bacc("TRN2", target_bir_lowering=False, num_devices=1)
    aps = {k: nc.dram_tensor("in_" + k, v.shape, mybir.dt.from_np(v.dtype), kind="ExternalInput").ap()
           for k, v in arrays.items()}
    y = nc.dram_tensor("y", (T, D), F32, kind="ExternalOutput").ap()
    build(nc, aps, y)
    r = run_bass_kernel_spmd(nc, [{"in_" + k: v for k, v in arrays.items()}], core_ids=[0])
    return r.results[0]["y"].reshape(1, T, D)


def layout(a, np, bf16):
    c = np.ascontiguousarray
    g = lambda n: c(a["L0_attn_" + n])
    f = lambda n: c(a["L0_ffn_" + n])
    x = a["x"].reshape(T, D)
    d = {"x": c(x), "xT": c(x.T), "ctxT": c(a["ctx_1024"].reshape(SKV, D).T),
         "mask": c(a["mask_Bx1x1xS2_fk0"].reshape(SKV)), "Wq": g("Wq"), "Wk": g("Wk"), "Wv": g("Wv"),
         "Wg": g("Wg"), "gk_w1": g("gk_w1"), "gk_w2": g("gk_w2"), "gk_b2": g("gk_b2"),
         "g_norm_w": g("g_norm_w"), "Wo": g("Wo"), "gate_wT": c(f("gate_w").T), "ws_in": f("ws_in"),
         "vs_in": f("vs_in"), "ws_out": f("ws_out"),
         "e_winT": c(f("e_win").transpose(1, 0, 2).reshape(D, E * EH)),
         "e_vinT": c(f("e_vin").transpose(1, 0, 2).reshape(D, E * EH)),
         "e_wout": c(f("e_wout").reshape(E * EH, D))}
    for n in ("Wq", "bq", "Wk", "bk", "Wv", "bv", "Wo", "bo"):
        d["x" + n] = c(a["L0_xattn_" + n])
    p = np.arange(P)
    d["c_eye"] = np.eye(P, dtype=np.float32)
    masks = []
    for lv in range(LEVELS):
        m = 1 << lv
        t = np.arange(TB).reshape(-1, 2, m)[:, 1, :].reshape(-1) % P
        masks.append((p[:, None] // m == (t // m - 1)[None, :]).astype(bf16))
    d["c_lmask"] = c(np.stack(masks, 1))
    d["c_bd"] = (p[:, None] // DK == np.arange(256)[None, :] // DV).astype(np.float32)
    rows = np.zeros((HALF - ROW_MAX, SP), bf16)
    rows[0:3] = 1
    d["c_krows"] = rows
    d["c_ones"] = np.ones((3, XH // 2, TB), bf16)
    d["c_dsel"] = (p[:, None] == p[None, :] // 32 * 32 + DH).astype(np.float32)
    e = np.arange(3 * E) % E
    d["c_csel"] = c((e[:, None, None] == (2 * np.arange(E // 2)[:, None] + p[None, :] // EH)[None]).astype(bf16))
    return d
```

```python
from contextlib import ExitStack

import concourse.bass as bass
from concourse import mybir

F32 = mybir.dt.float32
BF16 = mybir.dt.bfloat16
U16 = mybir.dt.uint16
ACT = mybir.ActivationFunctionType
ALU = mybir.AluOpType
AX = mybir.AxisListType

P = 128
T = 1024
D = 128
NB, TB = 2, 512
NC = TB // P
GH, DK, DV = 4, 32, 64
LEVELS = 7
SKV = 6404
KT = -(-SKV // P)
SP = KT * P
XH, DH = 16, 8
NHG, HG = 4, 4
GT = 3
NG = KT // GT
STEPS = 4
UNITS = NB * NHG
SPLIT = 48
HALF = 64
ROW_MASK, ROW_SPLIT, ROW_MAX = 0, 3, 51
E, EH, TOPK = 16, 64, 4
NPS = E // 2 + 1
EPS = 1e-5
KC = GT * P
BOUND_MAX = 60.0
K_PART = (0, 0, 1, 1, 0, 2)
Q_PART = (0, 1, 0, 1, 2, 0)


def build(nc, A, out, dbg=None):
    dbg = dbg or {}
    with ExitStack() as ctx:
        def sb(name, shape, dt=F32):
            return ctx.enter_context(nc.sbuf_tensor(name, shape, dt))

        def sem(name):
            return ctx.enter_context(nc.semaphore(name))

        def dram(name, shape, dt):
            return nc.dram_tensor(name, shape, dt, kind="Internal").ap()

        def rep(ap, axis, n):
            dims = [list(d) for d in ap.ap]
            return bass.AP(ap.tensor, ap.offset, dims[:axis] + [[0, n]] + dims[axis:])

        ps = ctx.enter_context(nc.psum_tensor("ps", [P, 8, 512], F32))

        kbuf = sb("kbuf", [P, 2, 2, SP], BF16)
        qaug = sb("qaug", [P, NB * XH, TB], BF16)
        vaug = sb("vaug", [P, KT, XH, DH])
        vst = sb("vst", [P, GT, HG, 32])
        prob = sb("prob", [P, STEPS, 3, 512])
        osb = sb("osb", [P, UNITS, TB])
        ctxT = kbuf[:, 1, :, :].rearrange("p a s -> p (a s)").bitcast(F32)
        early = prob[:, :, :, :].rearrange("p a b c -> p (a b c)")

        def arena(area):
            at = [0]

            def carve(*shape, dt=F32):
                words = 1
                for n in shape:
                    words *= n
                words = words * (2 if dt == BF16 else 4) // 4
                at[0] += words
                assert at[0] <= area.shape[1], (at[0], area.shape)
                part = area[:, at[0] - words:at[0]]
                part = part.bitcast(dt) if dt != F32 else part
                names = "abc"[:len(shape)]
                return part.rearrange(f"p ({' '.join(names)}) -> p {' '.join(names)}",
                                      **dict(zip(names, shape)))

            return carve

        slot0 = kbuf[:, 0, :, :].rearrange("p a s -> p (a s)").bitcast(F32)
        probs = prob[:, :, :, :].rearrange("p a b c -> p (a b c)")
        sums_area = osb[:, :, :].rearrange("p a b -> p (a b)")
        shared = sb("shared", [P, 2304])

        carve = arena(slot0)
        q_t, k_t, pre, suf, z1, z2, zm = (carve(TB) for _ in range(7))
        ek, eq, q_l = (carve(2, TB // 2) for _ in range(3))
        k_l = carve(2, TB)
        carve = arena(probs)
        a_sc = carve(GH, TB)
        v_g, gw, og = (carve(NC, 256) for _ in range(3))
        ktok = carve(NC, P)
        qsq = ktok[:, 0:2, :].rearrange("p c n -> p (c n)").bitcast(BF16)
        carve = arena(sums_area)
        sq = carve(NC, 256)
        kd, qd = carve(TB), carve(TB)
        ogT = carve(2, TB)
        kvtmp = carve(NC, 256)
        carve = arena(shared[:, :])
        kf = carve(2, KC)
        kr = carve(KC)
        kp = carve(2, 3 * KC, dt=BF16)
        kp = kp.rearrange("p a (i k) -> p a i k", i=3)
        carve = arena(sums_area)
        wvalid = carve(3 * KC)
        cjunk = carve(KC)
        ksq = carve(2, KC, dt=BF16)
        carve = arena(shared[:, :])
        mneg = carve(3, TB)[0:XH]
        mp = carve(3, TB, dt=BF16)[0:XH]
        carve = arena(slot0)
        win, vin, wout = (carve(NPS, P) for _ in range(3))
        wox = carve(NHG, D)
        dsel, bo = carve(P), carve(D)
        gate = carve(E)
        csel = carve(E // 2, P, dt=BF16)[0:3 * E]
        carve = arena(probs)
        rden, hsig, hid = (carve(2, TB) for _ in range(3))

        xT = sb("xT", [D, T])
        xtok = sb("xtok", [P, NB * NC, D])
        wqk = sb("wqk", [D, 2, P])
        wvg = sb("wvg", [D, 2, 256])
        w1 = sb("w1", [D, 16])
        w2 = sb("w2", [16, P])
        b2 = sb("b2", [P, 1])
        gnw = sb("gnw", [P, DV])
        wo = sb("wo", [P, 2, D])
        eye = sb("eye", [P, P])
        lmask = sb("lmask", [P, LEVELS, TB // 2], BF16)
        bdmask = sb("bdmask", [P, 256])
        xw = sb("xw", [D, 3, P])
        xb = sb("xb", [P, 2])
        bv = sb("bv", [P, P])
        low = sb("low", [16, TB])
        dec = sb("dec", [P, NC])
        state = sb("state", [P, NB * NC + 1, 256])
        ln_r = sb("ln_r", [P, NC, D])
        st6 = sb("st6", [P, NC, 6])
        mv = sb("mv", [P, NC, 2])
        rs = sb("rs", [P, 4, 16])
        x1 = sb("x1", [P, NB * NC, D])
        x1T = sb("x1T", [P, TB])
        qp = sb("qp", [P, 3, TB], BF16)
        mk = sb("mk", [KT, 2, P])
        mkp = sb("mkp", [KT, 3, P], BF16)
        mpart = sb("mpart", [P, 2, 4])
        mall = sb("mall", [P, UNITS * HG * NC])

        bound = zm[0:XH, :]
        flag = sb("flag", [1, 1], mybir.dt.int32)
        vsum = sb("vsum", [1, 1])
        viol = sb("viol", [P, 4])
        onesf = sb("onesf", [P, 1])
        csum = sb("csum", [P, 5])
        kbias = sb("kbias", [P, 1])
        dist = sb("dist", [XH, NG + 1])
        mkmin = sb("mkmin", [KT, 1])
        bmax = sb("bmax", [XH, 1])
        hsel = sb("hsel", [P, XH], BF16)
        ssq = sb("ssq", [P, GH * NC])
        rt = sb("rt", [P, 3, NC, E])
        top = sb("top", [P, NC, 8])
        cb = sb("cb", [P, NC, E], BF16)
        comb = sb("comb", [P, NC, 3 * E])
        combT = sb("combT", [3 * E, TB], BF16)

        k_dram = dram("k_dram", [XH, SPLIT, SP], BF16)
        q_dram = dram("q_dram", [NB, 3, XH, DH, TB], BF16)
        m_dram = dram("m_dram", [NB, 3, XH, TB], BF16)
        mask_dram = dram("mask_dram", [3, SP], BF16)

        S = {}

        def s(name):
            if name not in S:
                S[name] = sem(name)
            return S[name]

        loads = {
            "ctx": [(ctxT[:, 0:SKV], A["ctxT"])],
            "xw": [(xw[:, 0, :], A["xWq"]), (xw[:, 1, :], A["xWk"]), (xw[:, 2, :], A["xWv"]),
                   (xb[:, 0:1], A["xbq"].rearrange("(p a) -> p a", a=1)),
                   (xb[:, 1:2], A["xbk"].rearrange("(p a) -> p a", a=1)),
                   (bv[:, :], A["xbv"].partition_broadcast(P))],
            "gw": [(wqk[:, 0, :], A["Wq"]), (wqk[:, 1, :], A["Wk"]), (w1[:, :], A["gk_w1"]),
                   (w2[:, :], A["gk_w2"]), (b2[:, :], A["gk_b2"].rearrange("(p a) -> p a", a=1)),
                   (wvg[:, 0, :], A["Wv"]), (wvg[:, 1, :], A["Wg"]),
                   (gnw[:, :], A["g_norm_w"].partition_broadcast(P)),
                   (wo[:, :, :], A["Wo"].rearrange("(a p) n -> p a n", p=P))],
            "x": [(xT[:, :], A["xT"]), (xtok[:, :, :], A["x"].rearrange("(c p) d -> p c d", p=P))],
            "late": [(bo[:, :], A["xbo"].partition_broadcast(P)), (dsel[:, :], A["c_dsel"]),
                     (gate[:, :], A["gate_wT"]), (csel[:, :, :], A["c_csel"]),
                     (win[:, 0, :], A["ws_in"]), (vin[:, 0, :], A["vs_in"]), (wout[:, 0, :], A["ws_out"]),
                     (win[:, 1:, :], A["e_winT"].rearrange("d (p n) -> d p n", n=P)),
                     (vin[:, 1:, :], A["e_vinT"].rearrange("d (p n) -> d p n", n=P)),
                     (wout[:, 1:, :], A["e_wout"].rearrange("(p n) d -> n p d", n=P))] +
                    [(wox[32 * h:32 * h + DH, :, :],
                      A["xWo"].rearrange("(g h d) n -> h d g n", h=HG, d=DH)[h]) for h in range(HG)],
            "cst": [(eye[:, :], A["c_eye"]), (lmask[:, :, :], A["c_lmask"]), (bdmask[:, :], A["c_bd"]),
                    (hsel[:, :], A["c_hsel"])],
        }
        LAST = SKV - (KT - 1) * P

        block = ctx.enter_context(nc.Block())

        @block.sync
        def _(sp):
            def load(key):
                for dst, src in loads[key]:
                    sp.dma_start(dst, src).then_inc(s("in_" + key), 16)

            load("xw")
            load("ctx")
            sp.dma_start(wvalid, A["mask"][0:3 * KC].partition_broadcast(P)).then_inc(s("in_wv"), 16)
            load("gw")
            load("x")
            load("cst")
            sp.wait_ge(s("mask_clear"), 1)
            sp.dma_start(mk[0:KT - 1, 0, :], A["mask"][0:(KT - 1) * P].rearrange("(a b) -> a b", b=P))\
              .then_inc(s("in_mask"), 16)
            sp.dma_start(mk[KT - 1:KT, 0, 0:LAST], A["mask"][(KT - 1) * P:SKV].rearrange("(a b) -> a b", a=1))\
              .then_inc(s("in_mask"), 16)
            for c in range(NG):
                sp.wait_ge(s("k_parts"), c + 1)
                for r in range(6):
                    sp.dma_start(k_dram[:, 8 * r:8 * r + 8, KC * c:KC * c + KC], kp[:, c % 2, K_PART[r], :])\
                      .then_inc(s(f"k_out{c % 2}"), 16)
            sp.wait_ge(s("k_out0"), 16 * 6 * (NG - NG // 2))
            sp.wait_ge(s("k_out1"), 16 * 6 * (NG // 2))
            sp.wait_ge(s("q_zero"), 1)
            for b in range(NB):
                sp.wait_ge(s("q_parts"), b + 1)
                sp.dma_start(q_dram[b].rearrange("i h d t -> (h d) i t"), qp[:, :, :]).then_inc(s("q_out"), 16)
                sp.wait_ge(s("q_out"), 16 * (b + 1))
                for par in range(2):
                    heads = slice(XH * b + par, XH * (b + 1), 2)
                    sp.dma_start(qaug[HALF * par:HALF * par + 3, heads, :], A["c_ones"]).then_inc(s("q_in"), 16)
                    for r in range(6):
                        row = HALF * par + ROW_SPLIT + 8 * r
                        sp.dma_start(qaug[row:row + 8, heads, :],
                                     q_dram[b, Q_PART[r], par:XH:2, :, :].rearrange("h d t -> d h t"))\
                          .then_inc(s("q_in"), 16)

            sp.wait_ge(s("mask_parts"), 1)
            for i in range(3):
                sp.dma_start(mask_dram[i].rearrange("(a b) -> a b", b=P), mkp[:, i, :])\
                  .then_inc(s("mask_out"), 16)
            sp.wait_ge(s("mask_out"), 48)
            sp.wait_ge(s("ctx_used"), 1)
            sp.wait_ge(s("viol"), 1)
            for slot in range(2):
                for par in range(2):
                    for pair in range(2):
                        sp.dma_start(kbuf[HALF * par:HALF * par + 3, slot, pair, :], mask_dram)\
                          .then_inc(s("k_rows"), 16)
                        sp.dma_start(kbuf[HALF * par + ROW_MAX:HALF * par + HALF, slot, pair, :], A["c_krows"])\
                          .then_inc(s("k_rows"), 16)
            def load_keys(v, slot, done):
                head = (v % 2) * (2 * HG) + slot * HG
                for par in range(2):
                    sp.dma_start(kbuf[HALF * par + ROW_SPLIT:HALF * par + ROW_MAX, slot, :, :],
                                 k_dram[bass.ds(head, HG), :, :].rearrange("(a two) r k -> two r a k", two=2)[par])\
                      .then_inc(done, 16)

            sp.wait_ge(s("flag"), 1)
            general = sp.value_load(flag[0:1, 0:1], min_val=0, max_val=1)
            with sp.If(general > 0):
                load_keys(0, 0, s("g_keys0"))
                load_keys(0, 1, s("g_keys1"))
                with sp.Fori(1, UNITS // 2) as v:
                    for slot in range(2):
                        sp.wait_ge(s("g_slot_free"), v * 2 + (slot - 1))
                        load_keys(v, slot, s(f"g_keys{slot}"))
                sp.wait_ge(s("g_slot_free"), UNITS)
            for b in range(NB):
                sp.wait_ge(s("m_parts"), b + 1)
                sp.dma_start(m_dram[b].rearrange("i h t -> h i t"), mp[:, :, :]).then_inc(s("m_out"), 16)
                sp.wait_ge(s("m_out"), 16 * (b + 1))
                for par in range(2):
                    sp.dma_start(qaug[HALF * par + ROW_MAX:HALF * par + ROW_MAX + 3,
                                      XH * b + par:XH * (b + 1):2, :],
                                 m_dram[b, :, par:XH:2, :]).then_inc(s("m_in"), 16)
            load_keys(0, 0, s("keys_in0"))
            load_keys(0, 1, s("keys_in1"))
            with sp.Fori(1, UNITS // 2) as v:
                for slot in range(2):
                    sp.wait_ge(s("k_slot_free"), v * 2 + (slot - 1))
                    load_keys(v, slot, s(f"keys_in{slot}"))
            sp.wait_ge(s("wox_zero"), 1)
            load("late")
            for b in range(NB):
                sp.wait_ge(s("y_ready"), b + 1)
                sp.dma_start(out[b * TB:(b + 1) * TB, :].rearrange("(c p) d -> p c d", p=P), x1[:, NC * b:NC * b + NC, :])\
                  .then_inc(s("stored"), 16)
            sp.wait_ge(s("stored"), 16 * NB)

        @block.gpsimd
        def _(pool):
            order = [0]

            def link(ins):
                order[0] += 1
                ins.then_inc(s("pool_order"), 1)
                pool.wait_ge(s("pool_order"), order[0])

            for c in range(NG):
                pool.wait_ge(s("k_f"), c + 1)
                if c >= 2:
                    pool.wait_ge(s("kn_ps"), c - 1)
                link(pool.tensor_tensor(ksq[:, c % 2, :], kf[:, c % 2, :], kf[:, c % 2, :], ALU.mult))
                pool.sem_inc(s("k_sq"), 1)
                pool.wait_ge(s("k_hi"), c + 1)
                if c >= 2:
                    pool.wait_ge(s(f"k_out{c % 2}"), 16 * 6 * (c // 2))
                link(pool.tensor_tensor(kr[:, :], kf[:, c % 2, :], kp[:, c % 2, 0, :], ALU.subtract))
                link(pool.tensor_copy(kp[:, c % 2, 1, :], kr[:, :]))
                link(pool.tensor_tensor(kp[:, c % 2, 2, :], kr[:, :], kp[:, c % 2, 1, :], ALU.subtract))
                pool.sem_inc(s("k_parts"), 1)

            for b in range(NB):
                for lv in range(LEVELS):
                    m = 1 << lv
                    pv = pre[:, :].rearrange("p (n two m) -> p n two m", two=2, m=m)
                    sv = suf[:, :].rearrange("p (n two m) -> p n two m", two=2, m=m)
                    pool.wait_ge(s("lvl_exp"), b * LEVELS + lv + 1)
                    link(pool.tensor_tensor(sv[:, :, 0, :], sv[:, :, 0, :],
                                            rep(pv[:, :, 1, m - 1], 2, m), ALU.add))
                    pool.tensor_tensor(pv[:, :, 1, :], pv[:, :, 1, :],
                                       rep(pv[:, :, 0, m - 1], 2, m), ALU.add).then_inc(s("lvl_upd"), 1)
                    pool.wait_ge(s("lvl_upd"), b * LEVELS + lv + 1)

            pool.wait_ge(s("v_aug"), NG)
            pool.wait_ge(s("v_zero"), 1)
            with pool.Fori(0, UNITS // 2) as v:
                for slot in range(2):
                    head = (v % 2) * (2 * HG) + slot * HG
                    with pool.Fori(0, NG) as g:
                        for i in range(GT):
                            pool.wait_ge(s("p_free"), (v * (2 * NG) + slot * NG + g) * GT + (i + 1))
                            pool.tensor_copy(vst[:, i, :, 0:DH],
                                             vaug[:, bass.ds(g * GT + i, 1), bass.ds(head, HG), :])\
                                .then_inc(s("v_staged"), 1)

        @block.scalar
        def _(act):
            act.preload_act_table_set("natural_log_exp_and_others")
            order = [0]

            def link(ins):
                order[0] += 1
                ins.then_inc(s("act_order"), 1)
                act.wait_ge(s("act_order"), order[0])

            act.wait_ge(s("centre"), 1)
            for c in range(NG):
                act.wait_ge(s("k_ps"), c + 1)
                if c >= 2:
                    act.wait_ge(s("k_parts"), c - 1)
                    act.wait_ge(s("k_sq"), c - 1)
                act.activation(kf[:, c % 2, :], ps[:, c % 3, 0:KC], ACT.Identity, bias=kbias[:, 0:1])\
                   .then_inc(s("k_f"), 1)

            def rsqrt(n):
                act.wait_ge(s("rs_in"), n)
                link(act.activation(rs[:, 1, :], rs[:, 0, :], ACT.Ln))
                act.activation(rs[:, 2, :], rs[:, 1, :], ACT.Exp, scale=-0.5).then_inc(s("rs_exp"), 1)

            act.wait_ge(s("in_gw"), 16 * len(loads["gw"]))
            for b in range(NB):
                act.wait_ge(s("qk_ps"), b + 1)
                act.activation(q_t[:, :], ps[:, 0, :], ACT.Copy, scale=float(DK) ** -0.5)\
                   .then_inc(s("q_sb"), 1)
                act.wait_ge(s("z_ps"), b + 1)
                link(act.activation(z1[:, :], ps[:, 3, :], ACT.Abs, bias=b2[:, 0:1]))
                act.sem_inc(s("abs_sb"), 1)
                link(act.activation(z2[:, :], z1[:, :], ACT.Exp, scale=-1.0))
                act.activation(z1[:, :], z2[:, :], ACT.Ln, bias=1.0).then_inc(s("log_sb"), 1)
                for lv in range(LEVELS):
                    m = 1 << lv
                    pv = pre[:, :].rearrange("p (n two m) -> p n two m", two=2, m=m)
                    sv = suf[:, :].rearrange("p (n two m) -> p n two m", two=2, m=m)
                    if lv == 0:
                        act.wait_ge(s("gate"), b + 1)
                    else:
                        act.wait_ge(s("lvl_upd"), b * LEVELS + lv)
                    if b * LEVELS + lv >= 2:
                        act.wait_ge(s("lvl_kq"), b * LEVELS + lv - 1)
                    e1 = ek[:, lv % 2, :].rearrange("p (n m) -> p n m", m=m)
                    e2 = eq[:, lv % 2, :].rearrange("p (n m) -> p n m", m=m)
                    act.activation(e1, sv[:, :, 0, :], ACT.Exp, scale=1.0 / 16)
                    act.activation(e2, pv[:, :, 1, :], ACT.Exp, scale=1.0 / 16).then_inc(s("lvl_exp"), 1)
                    if lv == 0:
                        act.wait_ge(s("vg_ps"), b + 1)
                        if b:
                            act.wait_ge(s("og"), b)
                        act.activation(gw, ps[:, 4:8, 256:512], ACT.Exp, scale=-1.0)\
                           .then_inc(s("gate_exp"), 1)
                act.wait_ge(s("lvl_upd"), (b + 1) * LEVELS)
                act.activation(z1[:, :], suf[:, :], ACT.Exp, scale=1.0 / 16)
                act.activation(z2[:, :], pre[:, :], ACT.Exp, scale=1.0 / 16)
                act.activation(dec[:, :], pre[:, P - 1:TB:P], ACT.Exp, scale=1.0 / 16)\
                   .then_inc(s("fin_exp"), 1)
                act.wait_ge(s("o_ps"), b + 1)
                act.activation(sq, ps[:, 4:8, 0:256], ACT.Square).then_inc(s("o_sq"), 1)
                rsqrt(2 * b + 1)
                act.wait_ge(s("ogT_ps"), b + 1)
                act.activation(ogT, ps[:, 0:2, :], ACT.Copy).then_inc(s("ogT_sb"), 1)
                rsqrt(2 * b + 2)
                act.wait_ge(s("x1T_ps"), b + 1)
                act.activation(x1T[:, :], ps[:, 3, :], ACT.Copy).then_inc(s("x1T_sb"), 1)
                act.wait_ge(s("bound_sq"), b + 1)
                link(act.activation(bound[:, :], bound[:, :], ACT.Ln))
                act.activation(bound[:, :], bound[:, :], ACT.Exp, scale=0.5).then_inc(s("bound"), 1)

            act.sem_inc(s("s_free"), 2)
            act.wait_ge(s("x1T_sb"), NB)
            with act.Fori(0, UNITS * NG) as g:
                for a in range(STEPS):
                    act.wait_ge(s("scores"), g * STEPS + (a + 1))
                    if a < GT:
                        act.wait_ge(s("p_free"), g * GT + (a + 1))
                    act.activation(prob[:, a, :, :], ps[:, 3 * (a % 2):3 * (a % 2) + 3, :], ACT.Exp)\
                       .then_inc(s("s_free"), 1)

            for b in range(NB):
                rsqrt(2 * NB + 2 * b + 1)
                act.wait_ge(s("x2T_ps"), b + 1)
                act.activation(x1T[:, :], ps[:, 1, :], ACT.Copy).then_inc(s("x2T_sb"), 1)
                act.wait_ge(s("rt_ps"), b + 1)
                act.activation(rt[:, 1, :, :], ps[:, 2, 0:NC * E].rearrange("p (c e) -> p c e", e=E),
                               ACT.Exp, scale=-1.0).then_inc(s("rt_exp"), 1)
                for p in range(NPS):
                    n = b * NPS + p
                    act.wait_ge(s("h_ps"), n + 1)
                    if n >= 2:
                        act.wait_ge(s("hid"), n - 1)
                    act.activation(hsig[:, n % 2, :], ps[:, 1 + 3 * (n % 2), :], ACT.Exp, scale=-1.0)\
                       .then_inc(s("h_exp"), 1)
                rsqrt(2 * NB + 2 * b + 2)

        @block.vector
        def _(dve):
            order = [0]

            def link(ins):
                order[0] += 1
                ins.then_inc(s("dve_order"), 1)
                dve.wait_ge(s("dve_order"), order[0])

            dve.memset(mk[:, 0, :], 3e29).then_inc(s("mask_clear"), 1)
            dve.memset(ctxT[:, SKV:SP], 0.0).then_inc(s("ctx_pad"), 1)
            dve.memset(qaug[:, :, :], 0.0).then_inc(s("q_zero"), 1)
            link(dve.memset(vst[:, :, :, :], 0.0))
            dve.memset(vst[:, :, :, DH:DH + 1], 1.0).then_inc(s("v_zero"), 1)
            dve.memset(state[:, 0, :], 0.0)
            link(dve.memset(k_l[:, :, :], 0.0))

            dve.wait_ge(s("in_mask"), 32)
            link(dve.tensor_reduce(mkmin[:, :], mk[:, 0, :], AX.X, ALU.min))
            link(dve.memset(viol[:, :], 0.0))
            link(dve.tensor_scalar(viol[0:KT, 1:2], mkmin[:, :], 0.0, 0.0, ALU.is_ge, ALU.is_equal))
            link(dve.tensor_scalar(mk[:, 1, :], mk[:, 0, :], -1e9, None, ALU.mult))
            link(dve.tensor_copy(mkp[:, 0, :], mk[:, 1, :]))
            link(dve.tensor_tensor(mk[:, 0, :], mk[:, 1, :], mkp[:, 0, :], ALU.subtract))
            link(dve.tensor_copy(mkp[:, 1, :], mk[:, 0, :]))
            dve.tensor_tensor(mkp[:, 2, :], mk[:, 0, :], mkp[:, 1, :], ALU.subtract)\
               .then_inc(s("mask_parts"), 1)

            def split3(parts, full, rest, done):
                link(dve.tensor_copy(parts(0), full))
                link(dve.tensor_tensor(rest, full, parts(0), ALU.subtract))
                link(dve.tensor_copy(parts(1), rest))
                dve.tensor_tensor(parts(2), rest, parts(1), ALU.subtract).then_inc(s(done), 1)

            link(dve.memset(onesf[:, :], 1.0))
            dve.wait_ge(s("in_wv"), 16)
            dve.wait_ge(s("in_xw"), 16 * len(loads["xw"]))
            link(dve.tensor_scalar(wvalid[:, :], wvalid[:, :], 0.0, None, ALU.is_equal))
            link(dve.tensor_reduce(csum[:, 3:4], wvalid[:, :], AX.X, ALU.add))
            for c in range(3):
                dve.wait_ge(s("k_ps"), c + 1)
                link(dve.scalar_tensor_tensor(cjunk[:, :], ps[:, c, 0:KC], xb[:, 1:2], wvalid[:, KC * c:KC * c + KC],
                                              ALU.add, ALU.mult, accum_out=csum[:, c:c + 1]))
            link(dve.tensor_reduce(csum[:, 4:5], csum[:, 0:3], AX.X, ALU.add))
            link(dve.tensor_scalar(viol[:, 0:1], csum[:, 3:4], 1.0, 0.0, ALU.is_ge, ALU.is_equal))
            link(dve.tensor_scalar(csum[:, 3:4], csum[:, 3:4], 1.0, None, ALU.max))
            link(dve.reciprocal(csum[:, 3:4], csum[:, 3:4]))
            link(dve.tensor_tensor(csum[:, 4:5], csum[:, 4:5], csum[:, 3:4], ALU.mult))
            dve.tensor_tensor(kbias[:, :], xb[:, 1:2], csum[:, 4:5], ALU.subtract).then_inc(s("centre"), 1)

            for c in range(NG):
                dve.wait_ge(s("k_f"), c + 1)
                if c >= 2:
                    dve.wait_ge(s(f"k_out{c % 2}"), 16 * 6 * (c // 2))
                dve.tensor_copy(kp[:, c % 2, 0, :], kf[:, c % 2, :]).then_inc(s("k_hi"), 1)
                dve.wait_ge(s("v_ps"), c + 1)
                dve.tensor_tensor(vaug[:, GT * c:GT * c + GT, :, :],
                                  ps[:, 3 + c % 2, 0:GT * P].rearrange("p (a h d) -> p a h d", a=GT, h=XH),
                                  rep(bv[:, :], 1, GT).rearrange("p a (h d) -> p a h d", h=XH), ALU.add)\
                   .then_inc(s("v_aug"), 1)
                dve.wait_ge(s("kn_ps"), c + 1)
                dve.tensor_reduce(dist[:, c:c + 1], ps[0:XH, 5 + c % 2, 0:KC], AX.X, ALU.max)\
                   .then_inc(s("kn_max"), 1)
            dve.wait_ge(s("kn_max"), NG)
            link(dve.tensor_reduce(dist[:, NG:NG + 1], dist[:, 0:NG], AX.X, ALU.max))
            link(dve.tensor_scalar(dist[:, NG:NG + 1], dist[:, NG:NG + 1], 1.02, None, ALU.mult))

            def rsqrt(src, scale, n, idx):
                dve.memset(rs[:, 0, :], 1.0)
                link(dve.memset(rs[:, 3, :], 1.0))
                dve.tensor_scalar(rs[:, 0, 0:n], src, scale, EPS, ALU.mult, ALU.add).then_inc(s("rs_in"), 1)
                dve.wait_ge(s("rs_exp"), idx)
                link(dve.tensor_tensor(rs[:, 1, 0:n], rs[:, 2, 0:n], rs[:, 2, 0:n], ALU.mult))
                link(dve.tensor_tensor(rs[:, 1, 0:n], rs[:, 1, 0:n], rs[:, 0, 0:n], ALU.mult))
                link(dve.tensor_scalar(rs[:, 1, 0:n], rs[:, 1, 0:n], -0.5, 1.5, ALU.mult, ALU.add))
                link(dve.tensor_tensor(rs[:, 3, 0:n], rs[:, 2, 0:n], rs[:, 1, 0:n], ALU.mult))

            def layer_norm(b, idx, done):
                for c in range(NC):
                    link(dve.bn_stats(st6[:, c, :], ln_r[:, c, :]))
                for c in range(NC):
                    link(dve.bn_aggr(mv[:, c, :], st6[:, c, :]))
                rsqrt(mv[:, :, 1], 1.0, NC, idx)
                for c in range(NC):
                    link(dve.tensor_scalar(x1[:, NC * b + c, :], ln_r[:, c, :], mv[:, c, 0:1], rs[:, 3, c:c + 1],
                                           ALU.subtract, ALU.mult))
                dve.sem_inc(s(done), 1)

            dve.wait_ge(s("in_gw"), 16 * len(loads["gw"]))
            dve.wait_ge(s("in_cst"), 16 * len(loads["cst"]))
            dve.wait_ge(s("in_x"), 16 * len(loads["x"]))
            for b in range(NB):
                dve.wait_ge(s("low_ps"), b + 1)
                link(dve.tensor_copy(low[:, :], ps[0:16, 2, :]))
                dve.sem_inc(s("low_sb"), 1)
                dve.wait_ge(s("qk_ps"), b + 1)
                dve.tensor_copy(k_t[:, :], ps[:, 1, :]).then_inc(s("k_sb"), 1)
                link(dve.memset(suf[:, :], 0.0))
                dve.wait_ge(s("abs_sb"), b + 1)
                link(dve.tensor_scalar(zm[:, :], ps[:, 3, :], b2[:, 0:1], 0.0, ALU.add, ALU.min))
                dve.wait_ge(s("log_sb"), b + 1)
                dve.tensor_tensor(pre[:, :], zm[:, :], z1[:, :], ALU.subtract).then_inc(s("gate"), 1)
                dve.wait_ge(s("gate_exp"), b + 1)
                link(dve.tensor_copy(v_g, ps[:, 4:8, 0:256]))
                dve.sem_inc(s("v_sb"), 1)
                link(dve.tensor_scalar(gw, gw, 1.0, None, ALU.add))
                link(dve.reciprocal(gw, gw))
                link(dve.tensor_tensor(gw, gw, ps[:, 4:8, 256:512], ALU.mult))
                dve.sem_inc(s("vg_free"), 1)
                gw4 = gw.rearrange("p c (h v) -> p (c h) v", v=DV)
                link(dve.tensor_tensor(gw4, gw4, rep(gnw[:, :], 1, NC * GH), ALU.mult))
                dve.wait_ge(s("diag_ps"), b + 1)
                link(dve.tensor_tensor(a_sc.rearrange("p h (c t) -> p (h c) t", c=NC),
                                       ps[:, 0:4, :].rearrange("p h (c t) -> p (h c) t", c=NC),
                                       rep(eye[:, :], 1, GH * NC), ALU.mult))
                dve.sem_inc(s("a_diag"), 1)

                def decayed(lv):
                    m = 1 << lv
                    n = b * LEVELS + lv
                    dve.wait_ge(s("lvl_exp"), n + 1)
                    if n >= 2:
                        dve.wait_ge(s("lvl_ps"), n - 1)
                    two = lambda t: t.rearrange("p (n two m) -> p n two m", two=2, m=m)
                    one = lambda t: t.rearrange("p (n m) -> p n m", m=m)
                    dve.tensor_tensor(two(k_l[:, lv % 2, :])[:, :, 0, :], two(k_t[:, :])[:, :, 0, :],
                                      one(ek[:, lv % 2, :]), ALU.mult)
                    dve.tensor_tensor(one(q_l[:, lv % 2, :]), two(q_t[:, :])[:, :, 1, :],
                                      one(eq[:, lv % 2, :]), ALU.mult).then_inc(s("lvl_kq"), 1)

                def select(lv):
                    m = 1 << lv
                    dve.wait_ge(s("lvl_ps"), b * LEVELS + lv + 1)
                    bank = 4 * ((lv + 1) % 2)
                    tgt = a_sc.rearrange("p h (n two m) -> p h n two m", two=2, m=m)[:, :, :, 1, :]
                    src = ps[:, bank:bank + 4, 0:TB // 2].rearrange("p h (n m) -> p h n m", m=m)
                    msk = rep(lmask[:, lv, :].bitcast(U16), 1, GH).rearrange("p h (n m) -> p h n m", m=m)
                    link(dve.copy_predicated(tgt, msk, src))
                    dve.sem_inc(s("a_sel"), 1)

                decayed(0)
                for lv in range(1, LEVELS):
                    decayed(lv)
                    select(lv - 1)
                select(LEVELS - 1)
                dve.wait_ge(s("fin_exp"), b + 1)
                dve.tensor_tensor(kd, k_t[:, :], z1[:, :], ALU.mult)
                dve.tensor_tensor(qd, q_t[:, :], z2[:, :], ALU.mult).then_inc(s("qkd"), 1)
                dve.wait_ge(s("ktok_ps"), b + 1)
                dve.tensor_copy(ktok[:, :, :], ps[:, 0, :].rearrange("p (c n) -> p c n", c=NC))\
                   .then_inc(s("ktok_sb"), 1)
                dve.wait_ge(s("kv_ps"), b + 1)
                link(dve.tensor_tensor(kvtmp, ps[:, 1:3, :].rearrange("p b (c n) -> p (b c) n", c=2),
                                       rep(bdmask[:, :], 1, NC), ALU.mult))
                for c in range(NC):
                    link(dve.scalar_tensor_tensor(state[:, NC * b + c + 1, :], state[:, NC * b + c, :],
                                                  dec[:, c:c + 1], kvtmp[:, c, :], ALU.mult, ALU.add))
                    dve.sem_inc(s("state_ready"), 1)
                dve.wait_ge(s("o_sq"), b + 1)
                link(dve.tensor_reduce(ssq[:, :], sq.rearrange("p c (h v) -> p (c h) v", v=DV), AX.X, ALU.add))
                rsqrt(ssq[:, :], 1.0 / DV, GH * NC, 2 * b + 1)
                r16 = rep(rs[:, 3, 0:GH * NC], 2, DV).rearrange("p (c h) v -> p c h v", c=NC)
                link(dve.tensor_tensor(og.rearrange("p c (h v) -> p c h v", v=DV),
                                       ps[:, 4:8, 0:256].rearrange("p c (h v) -> p c h v", v=DV), r16, ALU.mult))
                link(dve.tensor_tensor(og, og, gw, ALU.mult))
                dve.sem_inc(s("og"), 1)
                dve.wait_ge(s("wo_ps"), b + 1)
                link(dve.tensor_tensor(ln_r[:, :, :], ps[:, 2, :].rearrange("p (c d) -> p c d", c=NC),
                                       xtok[:, NC * b:NC * b + NC, :], ALU.add))
                layer_norm(b, 2 * b + 2, "x1_ready")
                dve.wait_ge(s("q2_ps"), b + 1)
                if b:
                    dve.wait_ge(s("q_out"), 16 * b)
                link(dve.tensor_scalar(z1[:, :], ps[:, 0, :], xb[:, 0:1], float(DH) ** -0.5, ALU.add, ALU.mult))
                split3(lambda i: qp[:, i, :], z1[:, :], z2[:, :], "q_parts")
                link(dve.tensor_tensor(qsq[:, :], z1[:, :], z1[:, :], ALU.mult))
                dve.sem_inc(s("q_sq"), 1)
                dve.wait_ge(s("qn_ps"), b + 1)
                dve.tensor_scalar(bound[:, :], ps[0:XH, 2, :], dist[:, NG:NG + 1], 1e-20, ALU.mult, ALU.add)\
                   .then_inc(s("bound_sq"), 1)
                dve.wait_ge(s("bound"), b + 1)
                if b == 0:
                    dve.wait_ge(s("k_out0"), 16 * 6 * (NG - NG // 2))
                    dve.wait_ge(s("k_out1"), 16 * 6 * (NG // 2))
                    dve.wait_ge(s("k_parts"), NG)
                link(dve.tensor_scalar(mneg[:, b, :], bound[:, :], -1.0, None, ALU.mult))
                link(dve.tensor_reduce(bmax[:, :], bound[:, :], AX.X, ALU.max))
                link(dve.tensor_scalar(viol[0:XH, 2 + b:3 + b], bmax[:, :], BOUND_MAX, 0.0, ALU.is_le, ALU.is_equal))
                if b == NB - 1:
                    dve.sem_inc(s("viol"), 1)

            dve.wait_ge(s("viol_ps"), 1)
            link(dve.tensor_reduce(vsum[:, :], ps[0:1, 1, 0:4], AX.X, ALU.add))
            dve.tensor_scalar(flag[:, :], vsum[:, :], 0.0, None, ALU.is_gt).then_inc(s("flag"), 1)
            dve.wait_ge(s("flag"), 1)
            general = dve.value_load(flag[0:1, 0:1], min_val=0, max_val=1)
            with dve.If(general > 0):
                dve.sem_inc(s("m_red"), 2)
                with dve.Fori(0, UNITS) as u:
                    with dve.Fori(0, HG * NC) as r:
                        for j in range(4):
                            n = 4 if j < 3 else 1
                            w = 512 if j < 3 else SP - 12 * 512
                            dve.wait_ge(s("m_ps"), u * (HG * NC * 4) + r * 4 + (j + 1))
                            bank = 4 * (j % 2)
                            dve.tensor_reduce(mpart[:, 0, j:j + 1], ps[:, bank:bank + n, 0:w], AX.XY, ALU.max)\
                               .then_inc(s("m_red"), 1)
                        dve.wait_ge(s("m_red"), u * (HG * NC * 4) + r * 4 + 6)
                        dve.tensor_reduce(mall[:, bass.ds(u * (HG * NC) + r, 1)], mpart[:, 0, :], AX.X, ALU.max)\
                           .then_inc(s("m_done"), 1)
                        dve.wait_ge(s("m_done"), u * (HG * NC) + r + 1)
                for b in range(NB):
                    dve.wait_ge(s("mT_ps"), b + 1)
                    dve.tensor_scalar(mneg[:, b, :], ps[0:XH, 0, :], -1.0, None, ALU.mult)\
                       .then_inc(s("mT_free"), 1)
                dve.wait_ge(s("mT_free"), NB)
            for b in range(NB):
                if b:
                    dve.wait_ge(s("m_out"), 16 * b)
                split3(lambda i: mp[:, i, :], mneg[:, b, :], mneg[:, 2, :], "m_parts")

            dve.sem_inc(s("o_free"), 1)
            with dve.Fori(0, UNITS - 1) as u:
                dve.wait_ge(s("p_free"), u * KT + (KT + GT))
                dve.tensor_copy(osb[:, bass.ds(u, 1), :], ps[:, 6, :]).then_inc(s("o_free"), 1)
            dve.wait_ge(s("k_slot_free"), UNITS - 1)
            dve.memset(wox[:, :, :], 0.0).then_inc(s("wox_zero"), 1)
            dve.wait_ge(s("p_free"), UNITS * KT + GT)
            dve.tensor_copy(osb[:, UNITS - 1, :], ps[:, 6, :]).then_inc(s("o_free"), 1)

            dve.wait_ge(s("in_late"), 16 * len(loads["late"]))
            for b in range(NB):
                for hg in range(NHG):
                    n = b * NHG + hg
                    dve.wait_ge(s("den_ps"), n + 1)
                    link(dve.reciprocal(rden[:, n % 2, :], ps[:, 2 + n % 2, :]))
                    link(dve.tensor_tensor(osb[:, n, :], osb[:, n, :], rden[:, n % 2, :], ALU.mult))
                    dve.sem_inc(s("o_norm"), 1)
                dve.wait_ge(s("xo_ps"), b + 1)
                link(dve.tensor_tensor(ln_r[:, :, :], ps[:, 0, :].rearrange("p (c d) -> p c d", c=NC),
                                       x1[:, NC * b:NC * b + NC, :], ALU.add))
                link(dve.tensor_tensor(ln_r[:, :, :], ln_r[:, :, :], rep(bo[:, :], 1, NC), ALU.add))
                layer_norm(b, 2 * NB + 2 * b + 1, "x2_ready")
                dve.wait_ge(s("rt_exp"), b + 1)
                link(dve.tensor_copy(rt[:, 0, :, :], ps[:, 2, 0:NC * E].rearrange("p (c e) -> p c e", e=E)))
                dve.sem_inc(s("rt_sb"), 1)
                for c in range(NC):
                    link(dve.max(top[:, c, :], rt[:, 0, c, :]))
                link(dve.memset(top[:, :, TOPK:8], 3e38))
                for c in range(NC):
                    link(dve.match_replace(rt[:, 2, c, :], top[:, c, :], rt[:, 0, c, :], -3e38))
                dve.wait_ge(s("rt_exp"), b + 1)
                link(dve.tensor_scalar(rt[:, 1, :, :], rt[:, 1, :, :], 1.0, None, ALU.add))
                link(dve.reciprocal(rt[:, 1, :, :], rt[:, 1, :, :]))
                link(dve.tensor_scalar(rt[:, 2, :, :], rt[:, 2, :, :], -3e38, None, ALU.is_equal))
                link(dve.tensor_tensor(rt[:, 1, :, :], rt[:, 1, :, :], rt[:, 2, :, :], ALU.mult))
                link(dve.tensor_reduce(st6[:, :, 0], rt[:, 1, :, :], AX.X, ALU.add))
                link(dve.reciprocal(st6[:, :, 1], st6[:, :, 0]))
                link(dve.tensor_tensor(rt[:, 1, :, :], rt[:, 1, :, :], rep(st6[:, :, 1], 2, E), ALU.mult))
                link(dve.tensor_copy(cb[:, :, :], rt[:, 1, :, :]))
                link(dve.tensor_copy(comb[:, :, 0:E], cb[:, :, :]))
                link(dve.tensor_tensor(rt[:, 2, :, :], rt[:, 1, :, :], comb[:, :, 0:E], ALU.subtract))
                link(dve.tensor_copy(cb[:, :, :], rt[:, 2, :, :]))
                link(dve.tensor_copy(comb[:, :, E:2 * E], cb[:, :, :]))
                link(dve.tensor_tensor(comb[:, :, 2 * E:3 * E], rt[:, 2, :, :], comb[:, :, E:2 * E], ALU.subtract))
                dve.sem_inc(s("comb"), 1)
                dve.wait_ge(s("cT_ps"), b + 1)
                link(dve.tensor_copy(combT[:, :], ps[0:3 * E, 0, :]))
                dve.sem_inc(s("combT"), 1)
                for p in range(NPS):
                    n = b * NPS + p
                    bank = 1 + 3 * (n % 2)
                    dve.wait_ge(s("h_exp"), n + 1)
                    if n >= 2:
                        dve.wait_ge(s("y_mm"), n - 1)
                    dve.wait_ge(s("hv_ps"), n + 1)
                    if p:
                        dve.wait_ge(s("hc_ps"), b * (NPS - 1) + p)
                    h = hsig[:, n % 2, :]
                    link(dve.tensor_scalar(h, h, 1.0, None, ALU.add))
                    link(dve.reciprocal(h, h))
                    link(dve.tensor_tensor(h, h, ps[:, bank, :], ALU.mult))
                    if p:
                        link(dve.tensor_tensor(h, h, ps[:, bank + 2, :], ALU.mult))
                    link(dve.tensor_tensor(hid[:, n % 2, :], h, ps[:, bank + 1, :], ALU.mult))
                    dve.sem_inc(s("hid"), 1)
                dve.wait_ge(s("y_mm"), (b + 1) * NPS)
                link(dve.tensor_tensor(ln_r[:, :, :], ps[:, 7, :].rearrange("p (c d) -> p c d", c=NC),
                                       x1[:, NC * b:NC * b + NC, :], ALU.add))
                dve.sem_inc(s("y_free"), 1)
                layer_norm(b, 2 * NB + 2 * b + 2, "y_ready")

        @block.tensor
        def _(pe):
            mm = pe.matmul

            pe.wait_ge(s("in_xw"), 16 * len(loads["xw"]))
            pe.wait_ge(s("in_ctx"), 16)
            pe.wait_ge(s("ctx_pad"), 1)
            def key_chunk(c):
                if c >= 3:
                    pe.wait_ge(s("k_f"), c - 2)
                mm(ps[:, c % 3, 0:KC], xw[:, 1, :], ctxT[:, KC * c:KC * c + KC], start=True, stop=True)\
                    .then_inc(s("k_ps"), 1)

            def key_squares(c):
                pe.wait_ge(s("k_sq"), c + 1)
                if c >= 2:
                    pe.wait_ge(s("kn_max"), c - 1)
                mm(ps[0:XH, 5 + c % 2, 0:KC], hsel[:, :], ksq[:, c % 2, :], start=True, stop=True)\
                    .then_inc(s("kn_ps"), 1)

            def value_chunk(c):
                if c >= 2:
                    pe.wait_ge(s("v_aug"), c - 1)
                for i in range(GT):
                    ins = mm(ps[:, 3 + c % 2, P * i:P * i + P], ctxT[:, KC * c + P * i:KC * c + P * i + P],
                             xw[:, 2, :], start=True, stop=True)
                ins.then_inc(s("v_ps"), 1)

            pe.wait_ge(s("in_cst"), 16 * len(loads["cst"]))
            key_chunk(0)
            key_chunk(1)
            for c in range(NG):
                if c + 2 < NG:
                    key_chunk(c + 2)
                value_chunk(c)
                if c:
                    key_squares(c - 1)
            key_squares(NG - 1)

            pe.wait_ge(s("v_ps"), NG)
            pe.sem_inc(s("ctx_used"), 1)
            pe.wait_ge(s("in_gw"), 16 * len(loads["gw"]))
            pe.wait_ge(s("in_x"), 16 * len(loads["x"]))
            pe.wait_ge(s("k_f"), NG)
            pe.wait_ge(s("v_aug"), NG)
            pe.wait_ge(s("kn_max"), NG)
            for b in range(NB):
                xb_ = xT[:, TB * b:TB * b + TB]
                if b:
                    pe.wait_ge(s("q_parts"), b)
                    pe.wait_ge(s("x1T_sb"), b)
                mm(ps[0:16, 2, :], w1[:, :], xb_, start=True, stop=True).then_inc(s("low_ps"), 1)
                mm(ps[:, 0, :], wqk[:, 0, :], xb_, start=True, stop=True)
                mm(ps[:, 1, :], wqk[:, 1, :], xb_, start=True, stop=True).then_inc(s("qk_ps"), 1)
                pe.wait_ge(s("low_sb"), b + 1)
                mm(ps[:, 3, :], w2[:, :], low[:, :], start=True, stop=True).then_inc(s("z_ps"), 1)
                for c in range(NC):
                    ins = mm(ps[:, 4 + c, :], xT[:, TB * b + P * c:TB * b + P * c + P],
                             wvg[:, :, :].rearrange("p a n -> p (a n)"), start=True, stop=True)
                ins.then_inc(s("vg_ps"), 1)

                def heads_scores(bank, keys, queries, width):
                    for c in range(NC):
                        for h in range(GH):
                            r = slice(DK * h, DK * h + DK)
                            ins = mm(ps[:, bank + h, width * c:width * c + width], keys[r, P * c:P * c + P],
                                     queries[r, width * c:width * c + width], start=True, stop=True)
                    return ins

                pe.wait_ge(s("q_sb"), b + 1)
                pe.wait_ge(s("k_sb"), b + 1)
                pe.wait_ge(s("gate"), b + 1)
                heads_scores(0, k_t[:, :], q_t[:, :], P).then_inc(s("diag_ps"), 1)
                for lv in range(LEVELS):
                    pe.wait_ge(s("lvl_kq"), b * LEVELS + lv + 1)
                    if lv == 0:
                        pe.wait_ge(s("vg_free"), b + 1)
                    elif lv == 1:
                        pe.wait_ge(s("a_diag"), b + 1)
                    else:
                        pe.wait_ge(s("a_sel"), b * LEVELS + lv - 1)
                    heads_scores(4 * ((lv + 1) % 2), k_l[:, lv % 2, :], q_l[:, lv % 2, :], P // 2)\
                        .then_inc(s("lvl_ps"), 1)
                pe.wait_ge(s("a_sel"), b * LEVELS + LEVELS - 1)
                pe.wait_ge(s("qkd"), b + 1)
                for c in range(NC):
                    ins = pe.transpose(ps[:, 0, P * c:P * c + P], kd[:, P * c:P * c + P], eye[:, :])
                ins.then_inc(s("ktok_ps"), 1)
                pe.wait_ge(s("ktok_sb"), b + 1)
                pe.wait_ge(s("v_sb"), b + 1)
                for c in range(NC):
                    ins = mm(ps[:, 1 + c // 2, 256 * (c % 2):256 * (c % 2) + 256], ktok[:, c, :], v_g[:, c, :],
                             start=True, stop=True)
                ins.then_inc(s("kv_ps"), 1)
                pe.wait_ge(s("a_sel"), (b + 1) * LEVELS)
                for c in range(NC):
                    if NC * b + c:
                        pe.wait_ge(s("state_ready"), NC * b + c)
                    mm(ps[:, 4 + c, 0:256], qd[:, P * c:P * c + P], state[:, NC * b + c, :],
                       start=True, stop=False, skip_group_check=True)
                    for h in range(GH):
                        ins = mm(ps[:, 4 + c, DV * h:DV * h + DV], a_sc[:, h, P * c:P * c + P],
                                 v_g[:, c, DV * h:DV * h + DV], start=False, stop=(h == GH - 1),
                                 skip_group_check=True)
                ins.then_inc(s("o_ps"), 1)
                pe.wait_ge(s("og"), b + 1)
                pe.wait_ge(s("state_ready"), NC * (b + 1))
                for a in range(2):
                    for c in range(NC):
                        ins = pe.transpose(ps[:, a, P * c:P * c + P], og[:, c, P * a:P * a + P], eye[:, :])
                ins.then_inc(s("ogT_ps"), 1)
                pe.wait_ge(s("ogT_sb"), b + 1)
                for c in range(NC):
                    for a in range(2):
                        ins = mm(ps[:, 2, P * c:P * c + P], ogT[:, a, P * c:P * c + P], wo[:, a, :],
                                 start=(a == 0), stop=(a == 1))
                ins.then_inc(s("wo_ps"), 1)
                pe.wait_ge(s("x1_ready"), b + 1)
                for c in range(NC):
                    ins = pe.transpose(ps[:, 3, P * c:P * c + P], x1[:, NC * b + c, :], eye[:, :])
                ins.then_inc(s("x1T_ps"), 1)
                pe.wait_ge(s("x1T_sb"), b + 1)
                mm(ps[:, 0, :], xw[:, 0, :], x1T[:, :], start=True, stop=True).then_inc(s("q2_ps"), 1)
                pe.wait_ge(s("q_sq"), b + 1)
                mm(ps[0:XH, 2, :], hsel[:, :], qsq[:, :], start=True, stop=True).then_inc(s("qn_ps"), 1)
                pe.wait_ge(s("bound_sq"), b + 1)

            pe.wait_ge(s("viol"), 1)
            mm(ps[0:1, 1, 0:4], onesf[:, :], viol[:, :], start=True, stop=True).then_inc(s("viol_ps"), 1)
            pe.wait_ge(s("q_in"), 16 * 14 * NB)
            pe.wait_ge(s("k_rows"), 16 * 16)
            pe.wait_ge(s("flag"), 1)
            general = pe.value_load(flag[0:1, 0:1], min_val=0, max_val=1)

            def max_unit(v, slot):
                for h in range(HG):
                    with pe.Fori(0, NC) as i:
                        pe.wait_ge(s(f"g_keys{slot}"), v * 32 + 32)
                        for j in range(4):
                            n = 4 if j < 3 else 1
                            w = 512 if j < 3 else SP - 12 * 512
                            pe.wait_ge(s("m_red"), (v * 2 + slot) * (HG * NC * 4) + i * 4 + (h * NC * 4 + j + 1))
                            for k in range(n):
                                key = 512 * (4 * j + k)
                                ins = mm(ps[:, 4 * (j % 2) + k, 0:w],
                                         qaug[:, bass.ds(v * (2 * HG) + (slot * HG + h), 1), bass.ds(i * P, P)],
                                         kbuf[:, slot, h // 2, key:key + w], start=True, stop=True)
                            ins.then_inc(s("m_ps"), 1)
                pe.wait_ge(s("m_ps"), (v * 2 + slot + 1) * (HG * NC * 4))
                pe.sem_inc(s("g_slot_free"), 1)

            with pe.If(general > 0):
                with pe.Fori(0, UNITS // 2) as v:
                    max_unit(v, 0)
                    max_unit(v, 1)
                pe.wait_ge(s("m_done"), UNITS * HG * NC)
                for b in range(NB):
                    if b:
                        pe.wait_ge(s("mT_free"), b)
                    for i in range(NC):
                        cols = mall[:, b * XH * NC:(b + 1) * XH * NC].rearrange("p (h i) -> p i h", i=NC)[:, i, :]
                        ins = pe.transpose(ps[0:XH, 0, P * i:P * i + P], cols, eye[:, :])
                    ins.then_inc(s("mT_ps"), 1)

            pe.wait_ge(s("m_in"), 16 * 2 * NB)
            pe.wait_ge(s("v_zero"), 1)
            pe.sem_inc(s("p_free"), GT)

            def scores(v, slot, g, a, step):
                pe.wait_ge(s("s_free"), step + 1)
                for i in range(3):
                    tile, h = divmod(3 * a + i, HG)
                    ins = mm(ps[:, 3 * (a % 2) + i, :], kbuf[:, slot, h // 2, bass.ds(g * KC + tile * P, P)],
                             qaug[:, bass.ds(v * (2 * HG) + (slot * HG + h), 1), :], start=True, stop=True)
                ins.then_inc(s("scores"), 1)

            def sums(g_all, tile, first_group, last_group):
                pe.wait_ge(s("v_staged"), g_all * GT + (tile + 1))
                pe.wait_ge(s("s_free"), g_all * STEPS + (tile + 4))
                for h in range(HG):
                    a, i = divmod(HG * tile + h, 3)
                    ins = mm(ps[32 * h:32 * h + 32, 6, :], vst[:, tile, h, :], prob[:, a, i, :],
                             start=(first_group and tile == 0), stop=(last_group and tile == GT - 1),
                             skip_group_check=True)
                ins.then_inc(s("p_free"), 1)

            def group(v, slot, g, first_group, last_group, last_unit):
                g_all = v * (2 * NG) + slot * NG + g
                scores(v, slot, g, 2, g_all * STEPS + 2)
                scores(v, slot, g, 3, g_all * STEPS + 3)
                if last_group:
                    pe.wait_ge(s("scores"), g_all * STEPS + 4)
                    pe.sem_inc(s("k_slot_free"), 1)
                if first_group:
                    pe.wait_ge(s("o_free"), v * 2 + (slot + 1))
                sums(g_all, 0, first_group, last_group)
                for a in range(2):
                    if not last_group:
                        scores(v, slot, g + 1, a, g_all * STEPS + (4 + a))
                    elif not last_unit:
                        nv, ns = (v, 1) if slot == 0 else (v + 1, 0)
                        if a == 0:
                            pe.wait_ge(s(f"keys_in{ns}"), nv * 32 + 32)
                        scores(nv, ns, 0, a, g_all * STEPS + (4 + a))
                    sums(g_all, 1 + a, first_group, last_group)

            def unit(v, slot, last_unit):
                group(v, slot, 0, True, False, last_unit)
                with pe.Fori(1, NG - 1) as g:
                    group(v, slot, g, False, False, last_unit)
                group(v, slot, NG - 1, False, True, last_unit)

            pe.wait_ge(s("keys_in0"), 32)
            scores(0, 0, 0, 0, 0)
            scores(0, 0, 0, 1, 1)
            with pe.Fori(0, UNITS // 2 - 1) as v:
                unit(v, 0, False)
                unit(v, 1, False)
            unit(UNITS // 2 - 1, 0, False)
            unit(UNITS // 2 - 1, 1, True)

            pe.wait_ge(s("in_late"), 16 * len(loads["late"]))
            pe.wait_ge(s("o_free"), UNITS + 1)
            pe.wait_ge(s("s_free"), UNITS * NG * STEPS + 2)
            for b in range(NB):
                if b:
                    pe.wait_ge(s("y_free"), b)
                for hg in range(NHG):
                    n = b * NHG + hg
                    if n >= 2:
                        pe.wait_ge(s("o_norm"), n - 1)
                    mm(ps[:, 2 + n % 2, :], dsel[:, :], osb[:, n, :], start=True, stop=True)\
                        .then_inc(s("den_ps"), 1)
                for hg in range(NHG):
                    n = b * NHG + hg
                    pe.wait_ge(s("o_norm"), n + 1)
                    for c in range(NC):
                        ins = mm(ps[:, 0, P * c:P * c + P], osb[:, n, P * c:P * c + P], wox[:, hg, :],
                                 start=(hg == 0 and c == 0), stop=(hg == NHG - 1), skip_group_check=True)
                ins.then_inc(s("xo_ps"), 1)
                pe.wait_ge(s("x2_ready"), b + 1)
                for c in range(NC):
                    ins = pe.transpose(ps[:, 1, P * c:P * c + P], x1[:, NC * b + c, :], eye[:, :])
                ins.then_inc(s("x2T_ps"), 1)
                pe.wait_ge(s("x2T_sb"), b + 1)
                for c in range(NC):
                    ins = mm(ps[:, 2, E * c:E * c + E], x1T[:, P * c:P * c + P], gate[:, :], start=True, stop=True)
                ins.then_inc(s("rt_ps"), 1)
                for p in range(NPS + 1):
                    if p < NPS:
                        n = b * NPS + p
                        bank = 1 + 3 * (n % 2)
                        if n >= 2:
                            pe.wait_ge(s("hid"), n - 1)
                        if p <= 1:
                            pe.wait_ge(s("rt_exp"), b + 1)
                            pe.wait_ge(s("rt_sb"), b + 1)
                        mm(ps[:, bank, :], win[:, p, :], x1T[:, :], start=True, stop=True).then_inc(s("h_ps"), 1)
                        ins = mm(ps[:, bank + 1, :], vin[:, p, :], x1T[:, :], start=True, stop=True)
                        ins.then_inc(s("hv_ps"), 1)
                        if p == 1:
                            pe.wait_ge(s("comb"), b + 1)
                            for c in range(NC):
                                ins = pe.transpose(ps[0:3 * E, 0, P * c:P * c + P], comb[:, c, :], eye[:, :])
                            ins.then_inc(s("cT_ps"), 1)
                            pe.wait_ge(s("combT"), b + 1)
                        if p:
                            mm(ps[:, bank + 2, :], csel[:, p - 1, :], combT[:, :], start=True, stop=True)\
                                .then_inc(s("hc_ps"), 1)
                    if p:
                        n = b * NPS + p - 1
                        pe.wait_ge(s("hid"), n + 1)
                        for c in range(NC):
                            ins = mm(ps[:, 7, P * c:P * c + P], hid[:, n % 2, P * c:P * c + P], wout[:, p - 1, :],
                                     start=(p == 1 and c == 0), stop=(p == NPS), skip_group_check=True)
                        ins.then_inc(s("y_mm"), 1)


def kernel(**inputs):
    import ml_dtypes
    import numpy as np
    import concourse.bacc as bacc
    from concourse.bass_utils import run_bass_kernel_spmd

    a = {k: np.asarray(v) for k, v in inputs.items()}
    arrays = layout(a, np, ml_dtypes.bfloat16)
    nc = bacc.Bacc("TRN2", target_bir_lowering=False, num_devices=1)
    aps = {k: nc.dram_tensor("in_" + k, v.shape, mybir.dt.from_np(v.dtype), kind="ExternalInput").ap()
           for k, v in arrays.items()}
    y = nc.dram_tensor("y", (T, D), F32, kind="ExternalOutput").ap()
    build(nc, aps, y)
    r = run_bass_kernel_spmd(nc, [{"in_" + k: v for k, v in arrays.items()}], core_ids=[0])
    return r.results[0]["y"].reshape(1, T, D)


def layout(a, np, bf16):
    c = np.ascontiguousarray
    g = lambda n: c(a["L0_attn_" + n])
    f = lambda n: c(a["L0_ffn_" + n])
    x = a["x"].reshape(T, D)
    d = {"x": c(x), "xT": c(x.T), "ctxT": c(a["ctx_1024"].reshape(SKV, D).T),
         "mask": c(a["mask_Bx1x1xS2_fk0"].reshape(SKV)), "Wq": g("Wq"), "Wk": g("Wk"), "Wv": g("Wv"),
         "Wg": g("Wg"), "gk_w1": g("gk_w1"), "gk_w2": g("gk_w2"), "gk_b2": g("gk_b2"),
         "g_norm_w": g("g_norm_w"), "Wo": g("Wo"), "gate_wT": c(f("gate_w").T), "ws_in": f("ws_in"),
         "vs_in": f("vs_in"), "ws_out": f("ws_out"),
         "e_winT": c(f("e_win").transpose(1, 0, 2).reshape(D, E * EH)),
         "e_vinT": c(f("e_vin").transpose(1, 0, 2).reshape(D, E * EH)),
         "e_wout": c(f("e_wout").reshape(E * EH, D))}
    for n in ("Wq", "bq", "Wk", "bk", "Wv", "bv", "Wo", "bo"):
        d["x" + n] = c(a["L0_xattn_" + n])
    p = np.arange(P)
    d["c_hsel"] = (p[:, None] // DH == np.arange(XH)[None, :]).astype(bf16)
    d["c_eye"] = np.eye(P, dtype=np.float32)
    masks = []
    for lv in range(LEVELS):
        m = 1 << lv
        t = np.arange(TB).reshape(-1, 2, m)[:, 1, :].reshape(-1) % P
        masks.append((p[:, None] // m == (t // m - 1)[None, :]).astype(bf16))
    d["c_lmask"] = c(np.stack(masks, 1))
    d["c_bd"] = (p[:, None] // DK == np.arange(256)[None, :] // DV).astype(np.float32)
    rows = np.zeros((HALF - ROW_MAX, SP), bf16)
    rows[0:3] = 1
    d["c_krows"] = rows
    d["c_ones"] = np.ones((3, XH // 2, TB), bf16)
    d["c_dsel"] = (p[:, None] == p[None, :] // 32 * 32 + DH).astype(np.float32)
    e = np.arange(3 * E) % E
    d["c_csel"] = c((e[:, None, None] == (2 * np.arange(E // 2)[:, None] + p[None, :] // EH)[None]).astype(bf16))
    return d
```

```python
from contextlib import ExitStack

import concourse.bass as bass
from concourse import mybir

F32 = mybir.dt.float32
BF16 = mybir.dt.bfloat16
U16 = mybir.dt.uint16
ACT = mybir.ActivationFunctionType
ALU = mybir.AluOpType
AX = mybir.AxisListType

P = 128
T = 1024
D = 128
NB, TB = 2, 512
NC = TB // P
GH, DK, DV = 4, 32, 64
LEVELS = 7
SKV = 6404
KT = -(-SKV // P)
SP = KT * P
XH, DH = 16, 8
NHG, HG = 4, 4
GT = 3
NG = KT // GT
STEPS = 4
UNITS = NB * NHG
SPLIT = 48
HALF = 64
ROW_MASK, ROW_SPLIT, ROW_MAX = 0, 3, 51
E, EH, TOPK = 16, 64, 4
NPS = E // 2 + 1
EPS = 1e-5
KC = GT * P
BOUND_MAX = 60.0
K_PART = (0, 0, 0, 1, 1, 2)
Q_PART = (0, 1, 2, 0, 1, 0)
LOAD = 16 * 2 * 6
KP = 3


def build(nc, A, out):
    with ExitStack() as ctx:
        def sb(name, shape, dt=F32):
            return ctx.enter_context(nc.sbuf_tensor(name, shape, dt))

        def sem(name):
            return ctx.enter_context(nc.semaphore(name))

        def dram(name, shape, dt):
            return nc.dram_tensor(name, shape, dt, kind="Internal").ap()

        def rep(ap, axis, n):
            dims = [list(d) for d in ap.ap]
            return bass.AP(ap.tensor, ap.offset, dims[:axis] + [[0, n]] + dims[axis:])

        ps = ctx.enter_context(nc.psum_tensor("ps", [P, 8, 512], F32))

        kbuf = sb("kbuf", [P, 2, 2, SP], BF16)
        qaug = sb("qaug", [P, NB * XH, TB], BF16)
        vaug = sb("vaug", [P, KT, XH, DH])
        vst = sb("vst", [P, GT, HG, 32])
        prob = sb("prob", [P, STEPS, 3, 512])
        osb = sb("osb", [P, UNITS, TB])
        ctxT = kbuf[:, 0, :, :].rearrange("p a s -> p (a s)").bitcast(F32)

        def arena(area):
            at = [0]

            def carve(*shape, dt=F32):
                words = 1
                for n in shape:
                    words *= n
                words = words * (2 if dt == BF16 else 4) // 4
                at[0] += words
                assert at[0] <= area.shape[1], (at[0], area.shape)
                part = area[:, at[0] - words:at[0]]
                part = part.bitcast(dt) if dt != F32 else part
                names = "abc"[:len(shape)]
                return part.rearrange(f"p ({' '.join(names)}) -> p {' '.join(names)}",
                                      **dict(zip(names, shape)))

            return carve

        slot1 = kbuf[:, 1, :, :].rearrange("p a s -> p (a s)").bitcast(F32)
        slot0 = kbuf[:, 0, :, :].rearrange("p a s -> p (a s)").bitcast(F32)
        probs = prob[:, :, :, :].rearrange("p a b c -> p (a b c)")
        sums_area = osb[:, :, :].rearrange("p a b -> p (a b)")
        shared = sb("shared", [P, 2304])

        carve = arena(slot1)
        q_t, k_t, pre, suf, z1, z2, zm = (carve(TB) for _ in range(7))
        ek, eq, q_l = (carve(2, TB // 2) for _ in range(3))
        k_l = carve(2, TB)
        carve = arena(probs)
        a_sc = carve(NC * GH, P)
        v_g, gw, og = (carve(NC, 256) for _ in range(3))
        ktok = carve(NC, P)
        qsq = ktok[:, 0:2, :].rearrange("p c n -> p (c n)").bitcast(BF16)
        carve = arena(sums_area)
        sq = carve(NC, 256)
        ogT = carve(2, TB)
        kd, qd = carve(TB), carve(TB)
        kvtmp = carve(NC, 256)
        qx = sums_area[:, 0:2 * GH * (TB // 2)].rearrange("p (l h t) -> p l h t", l=2, h=GH)
        carve = arena(shared[:, :])
        kp = carve(KP, 3 * KC, dt=BF16)
        kp = kp.rearrange("p a (i k) -> p a i k", i=3)
        carve = arena(slot1)
        kf = carve(2, KC)
        kr = carve(2, KC)
        carve = arena(sums_area)
        wvalid = carve(3 * KC)
        cjunk = carve(KC)
        ksq = carve(2, KC, dt=BF16)
        carve = arena(shared[:, :])
        mneg = carve(3, TB)[0:XH]
        mp = carve(3, TB, dt=BF16)[0:XH]
        carve = arena(shared[:, :])
        rden, dsel = carve(TB), carve(P)
        carve = arena(slot0)
        win, vin, wout = (carve(NPS, P) for _ in range(3))
        wox = carve(NHG, D)
        bo = carve(D)
        gate = carve(E)
        csel = carve(E // 2, P, dt=BF16)[0:3 * E]
        carve = arena(probs)
        hsig, hid, x2T = (carve(2, TB) for _ in range(3))
        rt = carve(3, NB * NC, E)
        top = carve(NB * NC, 8)
        wsum = carve(2, NB * NC)
        comb = carve(NB * NC, 3 * E)
        cb = carve(NB * NC, E, dt=BF16)
        combT = carve(NB, TB, dt=BF16)[0:3 * E]

        xT = sb("xT", [D, T])
        xtok = sb("xtok", [P, NB * NC, D])
        wqk = sb("wqk", [D, 2, P])
        wvg = sb("wvg", [D, 2, 256])
        w1 = sb("w1", [D, 16])
        w2 = sb("w2", [16, P])
        b2 = sb("b2", [P, 1])
        gnw = sb("gnw", [P, DV])
        wo = sb("wo", [P, 2, D])
        eye = sb("eye", [P, P])
        lmask = sb("lmask", [P, LEVELS, TB // 2], BF16)
        bdmask = sb("bdmask", [P, 256])
        xw = sb("xw", [D, 3, P])
        xb = sb("xb", [P, 2])
        bv = sb("bv", [P, P])
        low = sb("low", [16, TB])
        dec = sb("dec", [P, NC])
        state = sb("state", [P, NB * NC + 1, 256])
        ln_r = sb("ln_r", [P, NC, D])
        st6 = sb("st6", [P, NC, 6])
        mv = sb("mv", [P, NC, 2])
        rs = sb("rs", [P, 2, 16])
        minus_half = sb("minus_half", [P, 1])
        x1 = sb("x1", [P, NB * NC, D])
        x1T = sb("x1T", [P, TB])
        qp = sb("qp", [P, 3, TB], BF16)
        mk = sb("mk", [KT, 2, P])
        mkp = sb("mkp", [KT, 3, P], BF16)
        mpart = sb("mpart", [P, 2, 4])
        mall = sb("mall", [P, UNITS * HG * NC])

        bound = zm[0:XH, :]
        flag = sb("flag", [1, 1], mybir.dt.int32)
        vsum = sb("vsum", [1, 1])
        viol = sb("viol", [P, 4])
        onesf = sb("onesf", [P, 1])
        csum = sb("csum", [P, 5])
        kbias = sb("kbias", [P, 1])
        dist = sb("dist", [XH, NG + 1])
        mkmin = sb("mkmin", [KT, 1])
        bmax = sb("bmax", [XH, 1])
        hsel = sb("hsel", [P, XH], BF16)
        ssq = sb("ssq", [P, GH * NC])

        k_dram = dram("k_dram", [3, XH * DH, SP], BF16)
        q_dram = dram("q_dram", [NB, 3, XH, DH, TB], BF16)
        m_dram = dram("m_dram", [NB, 3, XH, TB], BF16)
        mask_dram = dram("mask_dram", [3, SP], BF16)

        S = {}

        def s(name):
            if name not in S:
                S[name] = sem(name)
            return S[name]

        CTX = ((0, 3), (3, 7), (7, 12), (12, NG))
        loads = {
            "ctx": [(ctxT[:, KC * a:min(KC * z, SKV)], A["ctxT"][:, KC * a:min(KC * z, SKV)]) for a, z in CTX],
            "xw": [(xw[:, 0, :], A["xWq"]), (xw[:, 1, :], A["xWk"]), (xw[:, 2, :], A["xWv"]),
                   (xb[:, 0:1], A["xbq"].rearrange("(p a) -> p a", a=1)),
                   (xb[:, 1:2], A["xbk"].rearrange("(p a) -> p a", a=1)),
                   (bv[:, :], A["xbv"].partition_broadcast(P)), (hsel[:, :], A["c_hsel"])],
            "gw": [(wqk[:, 0, :], A["Wq"]), (wqk[:, 1, :], A["Wk"]), (w1[:, :], A["gk_w1"]),
                   (w2[:, :], A["gk_w2"]), (b2[:, :], A["gk_b2"].rearrange("(p a) -> p a", a=1)),
                   (wvg[:, 0, :], A["Wv"]), (wvg[:, 1, :], A["Wg"]),
                   (gnw[:, :], A["g_norm_w"].partition_broadcast(P)),
                   (wo[:, :, :], A["Wo"].rearrange("(a p) n -> p a n", p=P))],
            "x": [(xT[:, :], A["xT"]), (xtok[:, :, :], A["x"].rearrange("(c p) d -> p c d", p=P))],
            "late": [(bo[:, :], A["xbo"].partition_broadcast(P)),
                     (gate[:, :], A["gate_wT"]), (csel[:, :, :], A["c_csel"]),
                     (win[:, 0, :], A["ws_in"]), (vin[:, 0, :], A["vs_in"]), (wout[:, 0, :], A["ws_out"]),
                     (win[:, 1:, :], A["e_winT"].rearrange("d (p n) -> d p n", n=P)),
                     (vin[:, 1:, :], A["e_vinT"].rearrange("d (p n) -> d p n", n=P)),
                     (wout[:, 1:, :], A["e_wout"].rearrange("(p n) d -> n p d", n=P))] +
                    [(wox[32 * h:32 * h + DH, :, :],
                      A["xWo"].rearrange("(g h d) n -> h d g n", h=HG, d=DH)[h]) for h in range(HG)],
            "cst": [(eye[:, :], A["c_eye"]), (lmask[:, :, :], A["c_lmask"]), (bdmask[:, :], A["c_bd"])],
        }
        LAST = SKV - (KT - 1) * P

        block = ctx.enter_context(nc.Block())

        @block.sync
        def _(sp):
            def load(key):
                for dst, src in loads[key]:
                    sp.dma_start(dst, src).then_inc(s("in_" + key), 16)

            load("xw")
            def load_context(i):
                dst, src = loads["ctx"][i]
                sp.dma_start(dst, src).then_inc(s(f"in_ctx{i}"), 16)

            load_context(0)
            sp.dma_start(wvalid, A["mask"][0:3 * KC].partition_broadcast(P)).then_inc(s("in_wv"), 16)
            load_context(1)
            sp.wait_ge(s("mask_clear"), 1)
            sp.dma_start(mk[0:KT - 1, 0, :], A["mask"][0:(KT - 1) * P].rearrange("(a b) -> a b", b=P))\
              .then_inc(s("in_mask"), 16)
            sp.dma_start(mk[KT - 1:KT, 0, 0:LAST], A["mask"][(KT - 1) * P:SKV].rearrange("(a b) -> a b", a=1))\
              .then_inc(s("in_mask"), 16)
            load_context(2)
            load_context(3)
            load("gw")
            load("x")
            load("cst")
            for c in range(NG):
                sp.wait_ge(s("k_parts"), c + 1)
                sp.dma_start(k_dram[:, :, KC * c:KC * c + KC].rearrange("i p k -> p i k"),
                             kp[:, c % KP, :, :]).then_inc(s(f"k_out{c % KP}"), 16)
            for i in range(KP):
                sp.wait_ge(s(f"k_out{i}"), 16 * len(range(i, NG, KP)))

            def load_keys(v, slot, done):
                head = (v % 2) * (2 * HG) + slot * HG
                for par in range(2):
                    for r in range(6):
                        row = HALF * par + ROW_SPLIT + DH * r
                        part = k_dram[K_PART[r], bass.ds(head * DH, HG * DH), :]
                        sp.dma_start(kbuf[row:row + DH, slot, :, :],
                                     part.rearrange("(a two d) k -> two d a k", two=2, d=DH)[par])\
                          .then_inc(done, 16)

            def key_rows(slot):
                for par in range(2):
                    for pair in range(2):
                        sp.dma_start(kbuf[HALF * par:HALF * par + 3, slot, pair, :], mask_dram)\
                          .then_inc(s(f"k_rows{slot}"), 16)
                        sp.dma_start(kbuf[HALF * par + ROW_MAX:HALF * par + HALF, slot, pair, :], A["c_krows"])\
                          .then_inc(s(f"k_rows{slot}"), 16)

            def maxima_rows(b, out_done, in_done):
                sp.dma_start(m_dram[b].rearrange("i h t -> h i t"), mp[:, :, :]).then_inc(out_done, 16)
                sp.wait_ge(out_done, 16 * (b + 1))
                for par in range(2):
                    sp.dma_start(qaug[HALF * par + ROW_MAX:HALF * par + ROW_MAX + 3,
                                      XH * b + par:XH * (b + 1):2, :],
                                 m_dram[b, :, par:XH:2, :]).then_inc(in_done, 16)

            sp.wait_ge(s("mask_parts"), 1)
            for i in range(3):
                sp.dma_start(mask_dram[i].rearrange("(a b) -> a b", b=P), mkp[:, i, :])\
                  .then_inc(s("mask_out"), 16)
            sp.wait_ge(s("mask_out"), 48)
            sp.wait_ge(s("ctx_used"), 1)
            key_rows(0)
            load_keys(0, 0, s("keys_in0"))
            sp.wait_ge(s("q_zero"), 1)
            for b in range(NB):
                sp.wait_ge(s("q_parts"), b + 1)
                sp.dma_start(q_dram[b].rearrange("i h d t -> (h d) i t"), qp[:, :, :]).then_inc(s("q_out"), 16)
                sp.wait_ge(s("q_out"), 16 * (b + 1))
                for par in range(2):
                    heads = slice(XH * b + par, XH * (b + 1), 2)
                    sp.dma_start(qaug[HALF * par:HALF * par + 3, heads, :], A["c_ones"]).then_inc(s(f"q_in{b}"), 16)
                    for r in range(6):
                        row = HALF * par + ROW_SPLIT + DH * r
                        sp.dma_start(qaug[row:row + DH, heads, :],
                                     q_dram[b, Q_PART[r], par:XH:2, :, :].rearrange("h d t -> d h t"))\
                          .then_inc(s(f"q_in{b}"), 16)
                sp.wait_ge(s("m_parts"), b + 1)
                maxima_rows(b, s("m_out"), s(f"m_in{b}"))
            sp.wait_ge(s("slot1_free"), 1)
            key_rows(1)
            load_keys(0, 1, s("keys_in1"))
            sp.wait_ge(s("flag"), 1)
            general = sp.value_load(flag[0:1, 0:1], min_val=0, max_val=1)
            with sp.If(general > 0):
                sp.wait_ge(s("keys_in0"), LOAD)
                sp.wait_ge(s("keys_in1"), LOAD)
                load_keys(0, 0, s("g_keys0"))
                load_keys(0, 1, s("g_keys1"))
                with sp.Fori(1, UNITS // 2) as v:
                    for slot in range(2):
                        sp.wait_ge(s("g_slot_free"), v * 2 + (slot - 1))
                        load_keys(v, slot, s(f"g_keys{slot}"))
                sp.wait_ge(s("g_slot_free"), UNITS)
                load_keys(0, 0, s("g_keys0"))
                load_keys(0, 1, s("g_keys1"))
                for b in range(NB):
                    sp.wait_ge(s("g_m_parts"), b + 1)
                    maxima_rows(b, s("g_m_out"), s("g_m_in"))
            sp.dma_start(dsel[:, :], A["c_dsel"]).then_inc(s("in_dsel"), 16)
            with sp.Fori(1, UNITS // 2) as v:
                for slot in range(2):
                    sp.wait_ge(s("k_slot_free"), v * 2 + (slot - 1))
                    load_keys(v, slot, s(f"keys_in{slot}"))
            sp.wait_ge(s("wox_zero"), 1)
            load("late")
            for b in range(NB):
                sp.wait_ge(s("y_ready"), b + 1)
                sp.dma_start(out[b * TB:(b + 1) * TB, :].rearrange("(c p) d -> p c d", p=P), x1[:, NC * b:NC * b + NC, :])\
                  .then_inc(s("stored"), 16)
            sp.wait_ge(s("stored"), 16 * NB)

        @block.gpsimd
        def _(pool):
            order = [0]

            def link(ins):
                order[0] += 1
                ins.then_inc(s("pool_order"), 1)
                pool.wait_ge(s("pool_order"), order[0])

            pool.memset(qaug[:, :, :].rearrange("p h t -> p (h t)").bitcast(F32), 0.0).then_inc(s("q_zero"), 1)
            for c in range(NG + 1):
                if c < NG:
                    pool.wait_ge(s("k_hi"), c + 1)
                    if c >= 2:
                        pool.wait_ge(s("k_parts"), c - 1)
                    pool.tensor_tensor(kr[:, c % 2, :], kf[:, c % 2, :], kp[:, c % KP, 0, :], ALU.subtract)\
                        .then_inc(s("k_rest"), 1)
                if c:
                    pool.wait_ge(s("k_mid"), c)
                    pool.tensor_tensor(kp[:, (c - 1) % KP, 2, :], kr[:, (c - 1) % 2, :], kp[:, (c - 1) % KP, 1, :],
                                       ALU.subtract).then_inc(s("k_parts"), 1)

            link(pool.memset(minus_half[:, :], -0.5))

            def rsqrt(n, width):
                pool.wait_ge(s("rs_in"), n)
                pool.tensor_tensor(rs[:, 1, 0:width], rs[:, 0, 0:width], minus_half[:, :].broadcast_to([P, width]),
                                   ALU.pow).then_inc(s("rs_out"), 1)

            for b in range(NB):
                if b == 0:
                    pool.wait_ge(s("kn_ps"), NG)
                    pool.wait_ge(s("centre"), 1)
                else:
                    pool.wait_ge(s("wo_ps"), b)
                pool.memset(qx[:, :, :, :], 0.0).then_inc(s("qx_zero"), 1)
                for lv in range(LEVELS):
                    m = 1 << lv
                    pv = pre[:, :].rearrange("p (n two m) -> p n two m", two=2, m=m)
                    sv = suf[:, :].rearrange("p (n two m) -> p n two m", two=2, m=m)
                    pool.wait_ge(s("lvl_exp"), b * LEVELS + lv + 1)
                    link(pool.tensor_tensor(sv[:, :, 0, :], sv[:, :, 0, :],
                                            rep(pv[:, :, 1, m - 1], 2, m), ALU.add))
                    pool.tensor_tensor(pv[:, :, 1, :], pv[:, :, 1, :],
                                       rep(pv[:, :, 0, m - 1], 2, m), ALU.add).then_inc(s("lvl_upd"), 1)
                    pool.wait_ge(s("lvl_upd"), b * LEVELS + lv + 1)
                pool.wait_ge(s("vg_free"), b + 1)
                gw4 = gw.rearrange("p c (h v) -> p (c h) v", v=DV)
                pool.tensor_tensor(gw4, gw4, rep(gnw[:, :], 1, NC * GH), ALU.mult).then_inc(s("gw"), 1)
                rsqrt(2 * b + 1, GH * NC)
                rsqrt(2 * b + 2, NC)

            pool.wait_ge(s("v_aug"), NG)
            pool.wait_ge(s("v_zero"), 1)
            with pool.Fori(0, UNITS // 2) as v:
                for slot in range(2):
                    head = (v % 2) * (2 * HG) + slot * HG
                    with pool.Fori(0, NG) as g:
                        for i in range(GT):
                            pool.wait_ge(s("p_free"), (v * (2 * NG) + slot * NG + g) * GT + (i + 1))
                            pool.tensor_copy(vst[:, i, :, 0:DH],
                                             vaug[:, bass.ds(g * GT + i, 1), bass.ds(head, HG), :])\
                                .then_inc(s("v_staged"), 1)

            for n in range(2 * NB):
                rsqrt(2 * NB + n + 1, NC)

        @block.scalar
        def _(act):
            act.preload_act_table_set("natural_log_exp_and_others")
            order = [0]

            def link(ins):
                order[0] += 1
                ins.then_inc(s("act_order"), 1)
                act.wait_ge(s("act_order"), order[0])

            act.wait_ge(s("centre"), 1)
            for c in range(NG):
                act.wait_ge(s("k_ps"), c + 1)
                if c >= 2:
                    act.wait_ge(s("k_rest"), c - 1)
                    act.wait_ge(s("kn_ps"), c - 1)
                act.activation(kf[:, c % 2, :], ps[:, c % 3, 0:KC], ACT.Identity, bias=kbias[:, 0:1])\
                   .then_inc(s("k_f"), 1)
                act.activation(ksq[:, c % 2, :], ps[:, c % 3, 0:KC], ACT.Square, bias=kbias[:, 0:1])\
                   .then_inc(s("k_sq"), 1)

            act.wait_ge(s("k_parts"), NG)
            act.wait_ge(s("in_gw"), 16 * len(loads["gw"]))
            for b in range(NB):
                act.wait_ge(s("z_ps"), b + 1)
                link(act.activation(z1[:, :], ps[:, 3, :], ACT.Abs, bias=b2[:, 0:1]))
                act.sem_inc(s("abs_sb"), 1)
                link(act.activation(z2[:, :], z1[:, :], ACT.Exp, scale=-1.0))
                act.activation(z1[:, :], z2[:, :], ACT.Ln, bias=1.0).then_inc(s("log_sb"), 1)
                act.wait_ge(s("qt_ps"), b + 1)
                act.activation(q_t[:, :], ps[:, 0, :], ACT.Copy, scale=float(DK) ** -0.5)\
                   .then_inc(s("q_sb"), 1)

                def decays(lv):
                    m = 1 << lv
                    pv = pre[:, :].rearrange("p (n two m) -> p n two m", two=2, m=m)
                    sv = suf[:, :].rearrange("p (n two m) -> p n two m", two=2, m=m)
                    if lv == 0:
                        act.wait_ge(s("gate"), b + 1)
                    else:
                        act.wait_ge(s("lvl_upd"), b * LEVELS + lv)
                    if b * LEVELS + lv >= 2:
                        act.wait_ge(s("lvl_kq"), b * LEVELS + lv - 1)
                    e1 = ek[:, lv % 2, :].rearrange("p (n m) -> p n m", m=m)
                    e2 = eq[:, lv % 2, :].rearrange("p (n m) -> p n m", m=m)
                    act.activation(e1, sv[:, :, 0, :], ACT.Exp, scale=1.0 / 16)
                    act.activation(e2, pv[:, :, 1, :], ACT.Exp, scale=1.0 / 16).then_inc(s("lvl_exp"), 1)

                def spread(lv):
                    n = b * LEVELS + lv
                    act.wait_ge(s("lvl_kq"), n + 1)
                    if n >= 2:
                        act.wait_ge(s("lvl_ps"), n - 1)
                    for h in range(GH):
                        r = slice(DK * h, DK * h + DK)
                        ins = act.activation(qx[r, lv % 2, h, :], q_l[r, lv % 2, :], ACT.Copy)
                    ins.then_inc(s("lvl_qx"), 1)

                decays(0)
                decays(1)
                act.wait_ge(s("qx_zero"), b + 1)
                spread(0)
                act.wait_ge(s("vg_ps"), b + 1)
                if b:
                    act.wait_ge(s("og"), b)
                act.activation(gw, ps[:, 4:8, 256:512], ACT.Tanh, scale=0.5)
                act.activation(v_g, ps[:, 4:8, 0:256], ACT.Copy).then_inc(s("v_sb"), 1)
                for lv in range(2, LEVELS):
                    decays(lv)
                    spread(lv - 1)
                act.wait_ge(s("lvl_upd"), (b + 1) * LEVELS)
                act.activation(z1[:, :], suf[:, :], ACT.Exp, scale=1.0 / 16)
                act.activation(z2[:, :], pre[:, :], ACT.Exp, scale=1.0 / 16)
                act.activation(dec[:, :], pre[:, P - 1:TB:P], ACT.Exp, scale=1.0 / 16)\
                   .then_inc(s("fin_exp"), 1)
                spread(LEVELS - 1)
                act.preload_act_table_set("natural_log_exp_and_others")
                act.wait_ge(s("o_ps"), b + 1)
                act.activation(sq, ps[:, 4:8, 0:256], ACT.Square).then_inc(s("o_sq"), 1)
                act.wait_ge(s("ogT_ps"), b + 1)
                act.activation(ogT, ps[:, 0:2, :], ACT.Copy).then_inc(s("ogT_sb"), 1)
                act.wait_ge(s("x1T_ps"), b + 1)
                act.activation(x1T[:, :], ps[:, 3, :], ACT.Copy).then_inc(s("x1T_sb"), 1)
                act.wait_ge(s("bound_sq"), b + 1)
                link(act.activation(bound[:, :], bound[:, :], ACT.Ln))
                act.activation(bound[:, :], bound[:, :], ACT.Exp, scale=0.5).then_inc(s("bound"), 1)

            act.sem_inc(s("s_free"), 2)
            act.wait_ge(s("x1T_sb"), NB)
            with act.Fori(0, UNITS * NG) as g:
                for a in range(STEPS):
                    act.wait_ge(s("scores"), g * STEPS + (a + 1))
                    if a < GT:
                        act.wait_ge(s("p_free"), g * GT + (a + 1))
                    act.activation(prob[:, a, :, :], ps[:, 3 * (a % 2):3 * (a % 2) + 3, :], ACT.Exp)\
                       .then_inc(s("s_free"), 1)

            for b in range(NB):
                act.wait_ge(s("x2T_ps"), b + 1)
                act.activation(x2T[:, b, :], ps[:, 2 + b, :], ACT.Copy).then_inc(s("x2T_sb"), 1)
            for b in range(NB):
                act.wait_ge(s("rt_ps"), b + 1)
                act.activation(rt[:, 1, NC * b:NC * b + NC, :], ps[:, 4 + b, 0:NC * E].rearrange("p (c e) -> p c e", e=E),
                               ACT.Exp, scale=-1.0).then_inc(s("rt_exp"), 1)
            for b in range(NB):
                for p in range(NPS):
                    n = b * NPS + p
                    act.wait_ge(s("h_ps"), n + 1)
                    if n >= 2:
                        act.wait_ge(s("hid"), n - 1)
                    act.activation(hsig[:, n % 2, :], ps[:, 1 + 3 * (n % 2), :], ACT.Tanh, scale=0.5)\
                       .then_inc(s("h_tanh"), 1)

        @block.vector
        def _(dve):
            order = [0]

            def link(ins):
                order[0] += 1
                ins.then_inc(s("dve_order"), 1)
                dve.wait_ge(s("dve_order"), order[0])

            dve.memset(mk[:, 0, :], 3e29).then_inc(s("mask_clear"), 1)
            dve.memset(ctxT[:, SKV:SP], 0.0).then_inc(s("ctx_pad"), 1)
            link(dve.memset(vst[:, :, :, :], 0.0))
            dve.memset(vst[:, :, :, DH:DH + 1], 1.0).then_inc(s("v_zero"), 1)
            dve.memset(state[:, 0, :], 0.0)
            link(dve.memset(k_l[:, :, :], 0.0))

            def split3(parts, full, rest, done, link=link):
                link(dve.tensor_copy(parts(0), full))
                link(dve.tensor_tensor(rest, full, parts(0), ALU.subtract))
                link(dve.tensor_copy(parts(1), rest))
                dve.tensor_tensor(parts(2), rest, parts(1), ALU.subtract).then_inc(s(done), 1)

            link(dve.memset(viol[:, :], 0.0))
            link(dve.memset(onesf[:, :], 1.0))
            dve.wait_ge(s("in_wv"), 16)
            dve.wait_ge(s("in_xw"), 16 * len(loads["xw"]))
            link(dve.tensor_scalar(wvalid[:, :], wvalid[:, :], 0.0, None, ALU.is_equal))
            link(dve.tensor_reduce(csum[:, 3:4], wvalid[:, :], AX.X, ALU.add))
            for c in range(3):
                dve.wait_ge(s("k_ps"), c + 1)
                link(dve.scalar_tensor_tensor(cjunk[:, :], ps[:, c, 0:KC], xb[:, 1:2], wvalid[:, KC * c:KC * c + KC],
                                              ALU.add, ALU.mult, accum_out=csum[:, c:c + 1]))
            link(dve.tensor_reduce(csum[:, 4:5], csum[:, 0:3], AX.X, ALU.add))
            link(dve.tensor_scalar(viol[:, 0:1], csum[:, 3:4], 1.0, 0.0, ALU.is_ge, ALU.is_equal))
            link(dve.tensor_scalar(csum[:, 3:4], csum[:, 3:4], 1.0, None, ALU.max))
            link(dve.reciprocal(csum[:, 3:4], csum[:, 3:4]))
            link(dve.tensor_tensor(csum[:, 4:5], csum[:, 4:5], csum[:, 3:4], ALU.mult))
            dve.tensor_tensor(kbias[:, :], xb[:, 1:2], csum[:, 4:5], ALU.subtract).then_inc(s("centre"), 1)

            dve.wait_ge(s("in_mask"), 32)
            link(dve.tensor_reduce(mkmin[:, :], mk[:, 0, :], AX.X, ALU.min))
            link(dve.tensor_scalar(viol[0:KT, 1:2], mkmin[:, :], 0.0, 0.0, ALU.is_ge, ALU.is_equal))
            link(dve.tensor_scalar(mk[:, 1, :], mk[:, 0, :], -1e9, None, ALU.mult))
            link(dve.tensor_copy(mkp[:, 0, :], mk[:, 1, :]))
            link(dve.tensor_tensor(mk[:, 0, :], mk[:, 1, :], mkp[:, 0, :], ALU.subtract))
            link(dve.tensor_copy(mkp[:, 1, :], mk[:, 0, :]))
            dve.tensor_tensor(mkp[:, 2, :], mk[:, 0, :], mkp[:, 1, :], ALU.subtract)\
               .then_inc(s("mask_parts"), 1)

            for c in range(NG + 1):
                if c < NG:
                    dve.wait_ge(s("k_f"), c + 1)
                    if c >= KP:
                        dve.wait_ge(s(f"k_out{c % KP}"), 16 * (c // KP))
                    dve.tensor_copy(kp[:, c % KP, 0, :], kf[:, c % 2, :]).then_inc(s("k_hi"), 1)
                if c:
                    dve.wait_ge(s("k_rest"), c)
                    dve.tensor_copy(kp[:, (c - 1) % KP, 1, :], kr[:, (c - 1) % 2, :]).then_inc(s("k_mid"), 1)
                if c < NG:
                    dve.wait_ge(s("v_ps"), c + 1)
                    dve.tensor_tensor(vaug[:, GT * c:GT * c + GT, :, :],
                                      ps[:, 3 + c % 2, 0:GT * P].rearrange("p (a h d) -> p a h d", a=GT, h=XH),
                                      rep(bv[:, :], 1, GT).rearrange("p a (h d) -> p a h d", h=XH), ALU.add)\
                       .then_inc(s("v_aug"), 1)
                if c:
                    dve.wait_ge(s("kn_ps"), c)
                    dve.tensor_reduce(dist[:, c - 1:c], ps[0:XH, 5 + (c - 1) % 2, 0:KC], AX.X, ALU.max)\
                       .then_inc(s("kn_max"), 1)
            dve.wait_ge(s("k_parts"), NG)
            dve.wait_ge(s("kn_max"), NG)
            link(dve.tensor_reduce(dist[:, NG:NG + 1], dist[:, 0:NG], AX.X, ALU.max))
            link(dve.tensor_scalar(dist[:, NG:NG + 1], dist[:, NG:NG + 1], 1.02, None, ALU.mult))

            def norm_stats():
                for c in range(NC - 1):
                    dve.bn_stats(st6[:, c, :], ln_r[:, c, :])
                link(dve.bn_stats(st6[:, NC - 1, :], ln_r[:, NC - 1, :]))

            def norm_root():
                for c in range(NC - 1):
                    dve.bn_aggr(mv[:, c, :], st6[:, c, :])
                link(dve.bn_aggr(mv[:, NC - 1, :], st6[:, NC - 1, :]))
                dve.tensor_scalar(rs[:, 0, 0:NC], mv[:, :, 1], 1.0, EPS, ALU.mult, ALU.add).then_inc(s("rs_in"), 1)

            def norm_apply(b, idx, done):
                dve.wait_ge(s("rs_out"), idx)
                for c in range(NC):
                    ins = dve.tensor_scalar(x1[:, NC * b + c, :], ln_r[:, c, :], mv[:, c, 0:1], rs[:, 1, c:c + 1],
                                            ALU.subtract, ALU.mult)
                link(ins)
                dve.sem_inc(s(done), 1)

            def layer_norm(b, idx, done):
                norm_stats()
                norm_root()
                norm_apply(b, idx, done)

            dve.wait_ge(s("in_gw"), 16 * len(loads["gw"]))
            dve.wait_ge(s("in_cst"), 16 * len(loads["cst"]))
            link(dve.tensor_scalar(gnw[:, :], gnw[:, :], 0.5, None, ALU.mult))
            dve.wait_ge(s("in_x"), 16 * len(loads["x"]))

            def block_start(b):
                dve.wait_ge(s("low_ps"), b + 1)
                dve.tensor_copy(low[:, :], ps[0:16, 2, :]).then_inc(s("low_sb"), 1)
                dve.wait_ge(s("qk_ps"), b + 1)
                dve.tensor_copy(k_t[:, :], ps[:, 1, :]).then_inc(s("k_sb"), 1)

            block_start(0)
            for b in range(NB):
                link(dve.memset(suf[:, :], 0.0))
                dve.wait_ge(s("abs_sb"), b + 1)
                link(dve.tensor_scalar(zm[:, :], ps[:, 3, :], b2[:, 0:1], 0.0, ALU.add, ALU.min))
                dve.wait_ge(s("log_sb"), b + 1)
                dve.tensor_tensor(pre[:, :], zm[:, :], z1[:, :], ALU.subtract).then_inc(s("gate"), 1)

                def decayed(lv):
                    m = 1 << lv
                    n = b * LEVELS + lv
                    dve.wait_ge(s("lvl_exp"), n + 1)
                    if n >= 2:
                        dve.wait_ge(s("lvl_ps"), n - 1)
                    two = lambda t: t.rearrange("p (n two m) -> p n two m", two=2, m=m)
                    one = lambda t: t.rearrange("p (n m) -> p n m", m=m)
                    dve.tensor_tensor(two(k_l[:, lv % 2, :])[:, :, 0, :], two(k_t[:, :])[:, :, 0, :],
                                      one(ek[:, lv % 2, :]), ALU.mult)
                    dve.tensor_tensor(one(q_l[:, lv % 2, :]), two(q_t[:, :])[:, :, 1, :],
                                      one(eq[:, lv % 2, :]), ALU.mult).then_inc(s("lvl_kq"), 1)

                def select(lv):
                    m = 1 << lv
                    dve.wait_ge(s("lvl_ps"), b * LEVELS + lv + 1)
                    bank = 2 * (lv % 2)
                    tgt = a_sc.rearrange("p k (n two m) -> p k n two m", two=2, m=m)[:, :, :, 1, :]
                    src = ps[:, bank:bank + 2, :].rearrange("p b (k n m) -> p (b k) n m", n=P // 2 // m, m=m)
                    msk = rep(lmask[:, lv, 0:P // 2].bitcast(U16), 1, NC * GH)\
                        .rearrange("p k (n m) -> p k n m", m=m)
                    link(dve.copy_predicated(tgt, msk, src))
                    dve.sem_inc(s("a_sel"), 1)

                decayed(0)
                dve.wait_ge(s("diag_ps"), b + 1)
                link(dve.tensor_tensor(a_sc.rearrange("p (c h) t -> p h c t", c=NC),
                                       ps[:, 0:4, :].rearrange("p h (c t) -> p h c t", c=NC),
                                       rep(rep(eye[:, :], 1, NC), 1, GH), ALU.mult))
                dve.sem_inc(s("a_diag"), 1)
                decayed(1)
                for lv in range(LEVELS):
                    select(lv)
                    if lv + 2 < LEVELS:
                        decayed(lv + 2)
                    if lv == 0:
                        dve.wait_ge(s("v_sb"), b + 1)
                        dve.scalar_tensor_tensor(gw, gw, 1.0, ps[:, 4:8, 256:512], ALU.add, ALU.mult)\
                           .then_inc(s("vg_free"), 1)
                dve.wait_ge(s("fin_exp"), b + 1)
                dve.tensor_tensor(kd, k_t[:, :], z1[:, :], ALU.mult)
                dve.tensor_tensor(qd, q_t[:, :], z2[:, :], ALU.mult).then_inc(s("qkd"), 1)
                dve.wait_ge(s("ktok_ps"), b + 1)
                dve.tensor_copy(ktok[:, :, :], ps[:, 0, :].rearrange("p (c n) -> p c n", c=NC))\
                   .then_inc(s("ktok_sb"), 1)
                dve.wait_ge(s("kv_ps"), b + 1)
                link(dve.tensor_tensor(kvtmp, ps[:, 1:3, :].rearrange("p b (c n) -> p (b c) n", c=2),
                                       rep(bdmask[:, :], 1, NC), ALU.mult))
                for c in range(NC):
                    link(dve.scalar_tensor_tensor(state[:, NC * b + c + 1, :], state[:, NC * b + c, :],
                                                  dec[:, c:c + 1], kvtmp[:, c, :], ALU.mult, ALU.add))
                    dve.sem_inc(s("state_ready"), 1)
                dve.wait_ge(s("o_sq"), b + 1)
                link(dve.tensor_reduce(ssq[:, :], sq.rearrange("p c (h v) -> p (c h) v", v=DV), AX.X, ALU.add))
                dve.tensor_scalar(rs[:, 0, :], ssq[:, :], 1.0 / DV, EPS, ALU.mult, ALU.add).then_inc(s("rs_in"), 1)
                dve.wait_ge(s("gw"), b + 1)
                link(dve.tensor_tensor(og, ps[:, 4:8, 0:256], gw, ALU.mult))
                dve.wait_ge(s("rs_out"), 2 * b + 1)
                r16 = rep(rs[:, 1, 0:GH * NC], 2, DV)
                og4 = og.rearrange("p c (h v) -> p (c h) v", v=DV)
                link(dve.tensor_tensor(og4, og4, r16, ALU.mult))
                dve.sem_inc(s("og"), 1)
                dve.wait_ge(s("wo_ps"), b + 1)
                link(dve.tensor_tensor(ln_r[:, :, :], ps[:, 2, :].rearrange("p (c d) -> p c d", c=NC),
                                       xtok[:, NC * b:NC * b + NC, :], ALU.add))
                layer_norm(b, 2 * b + 2, "x1_ready")
                dve.wait_ge(s("q2_ps"), b + 1)
                if b:
                    dve.wait_ge(s("q_out"), 16 * b)
                link(dve.tensor_scalar(z1[:, :], ps[:, 0, :], xb[:, 0:1], float(DH) ** -0.5, ALU.add, ALU.mult))
                split3(lambda i: qp[:, i, :], z1[:, :], z2[:, :], "q_parts")
                link(dve.tensor_tensor(qsq[:, :], z1[:, :], z1[:, :], ALU.mult))
                dve.sem_inc(s("q_sq"), 1)
                dve.wait_ge(s("qn_ps"), b + 1)
                dve.tensor_scalar(bound[:, :], ps[0:XH, 2, :], dist[:, NG:NG + 1], 1e-20, ALU.mult, ALU.add)\
                   .then_inc(s("bound_sq"), 1)
                if b + 1 < NB:
                    block_start(b + 1)
                dve.wait_ge(s("bound"), b + 1)
                if b == 0:
                    for i in range(KP):
                        dve.wait_ge(s(f"k_out{i}"), 16 * len(range(i, NG, KP)))
                link(dve.tensor_reduce(bmax[:, :], bound[:, :], AX.X, ALU.max))
                link(dve.tensor_scalar(viol[0:XH, 2 + b:3 + b], bmax[:, :], BOUND_MAX, 0.0, ALU.is_le, ALU.is_equal))
                if b == NB - 1:
                    dve.sem_inc(s("viol"), 1)
                    dve.wait_ge(s("viol_ps"), 1)
                    link(dve.tensor_reduce(vsum[:, :], ps[0:1, 1, 0:4], AX.X, ALU.add))
                    dve.tensor_scalar(flag[:, :], vsum[:, :], 0.0, None, ALU.is_gt).then_inc(s("flag"), 1)
                link(dve.tensor_scalar(mneg[:, b, :], bound[:, :], -1.0, -BOUND_MAX, ALU.mult, ALU.max))
                if b:
                    dve.wait_ge(s("m_out"), 16 * b)
                split3(lambda i: mp[:, i, :], mneg[:, b, :], mneg[:, 2, :], "m_parts")
            dve.sem_inc(s("slot1_free"), 1)
            dve.wait_ge(s("flag"), 1)
            general = dve.value_load(flag[0:1, 0:1], min_val=0, max_val=1)
            with dve.If(general > 0):
                dve.sem_inc(s("m_red"), 2)
                with dve.Fori(0, UNITS) as u:
                    with dve.Fori(0, HG * NC) as r:
                        for j in range(4):
                            n = 4 if j < 3 else 1
                            w = 512 if j < 3 else SP - 12 * 512
                            dve.wait_ge(s("m_ps"), u * (HG * NC * 4) + r * 4 + (j + 1))
                            bank = 4 * (j % 2)
                            dve.tensor_reduce(mpart[:, 0, j:j + 1], ps[:, bank:bank + n, 0:w], AX.XY, ALU.max)\
                               .then_inc(s("m_red"), 1)
                        dve.wait_ge(s("m_red"), u * (HG * NC * 4) + r * 4 + 6)
                        dve.tensor_reduce(mall[:, bass.ds(u * (HG * NC) + r, 1)], mpart[:, 0, :], AX.X, ALU.max)\
                           .then_inc(s("m_done"), 1)
                        dve.wait_ge(s("m_done"), u * (HG * NC) + r + 1)
                dve.wait_ge(s("m_out"), 16 * NB)
                g_order = [0]

                def g_link(ins):
                    g_order[0] += 1
                    ins.then_inc(s("g_order"), 1)
                    dve.wait_ge(s("g_order"), g_order[0])

                for b in range(NB):
                    dve.wait_ge(s("mT_ps"), b + 1)
                    g_link(dve.tensor_tensor(mneg[:, b, :], mneg[:, b, :], ps[0:XH, 0, :], ALU.subtract))
                    dve.sem_inc(s("mT_free"), 1)
                    if b:
                        dve.wait_ge(s("g_m_out"), 16 * b)
                    split3(lambda i: mp[:, i, :], mneg[:, b, :], mneg[:, 2, :], "g_m_parts", g_link)
                dve.wait_ge(s("g_m_out"), 16 * NB)

            dve.sem_inc(s("o_free"), 1)
            dve.sem_inc(s("o_norm"), 1)
            dve.wait_ge(s("m_out"), 16 * NB)

            def normalise(u):
                dve.wait_ge(s("p_free"), u * KT + (KT + GT))
                dve.tensor_copy(osb[:, bass.ds(u, 1), :], ps[:, 6, :]).then_inc(s("o_free"), 1)
                dve.wait_ge(s("den_ps"), u + 1)
                dve.reciprocal(rden[:, :], ps[:, 7, :]).then_inc(s("rden"), 1)
                dve.wait_ge(s("rden"), u + 1)
                dve.wait_ge(s("o_free"), u + 2)
                dve.tensor_tensor(osb[:, bass.ds(u, 1), :], osb[:, bass.ds(u, 1), :], rep(rden, 1, 1), ALU.mult)\
                   .then_inc(s("o_norm"), 1)

            with dve.Fori(0, UNITS - 1) as u:
                normalise(u)
            dve.wait_ge(s("k_slot_free"), UNITS - 1)
            dve.memset(wox[:, :, :], 0.0).then_inc(s("wox_zero"), 1)

            def add_attention(b):
                link(dve.tensor_tensor(ln_r[:, :, :], x1[:, NC * b:NC * b + NC, :], rep(bo[:, :], 1, NC), ALU.add))
                dve.wait_ge(s("xo_ps"), b + 1)
                link(dve.tensor_tensor(ln_r[:, :, :], ln_r[:, :, :],
                                       ps[:, 7 - 6 * b, :].rearrange("p (c d) -> p c d", c=NC), ALU.add))
                layer_norm(b, 2 * NB + b + 1, "x2_ready")

            dve.wait_ge(s("in_late"), 16 * len(loads["late"]))
            add_attention(0)
            normalise(UNITS - 1)
            add_attention(1)
            for b in range(NB):
                dve.wait_ge(s("rt_exp"), b + 1)
                dve.tensor_copy(rt[:, 0, NC * b:NC * b + NC, :],
                                ps[:, 4 + b, 0:NC * E].rearrange("p (c e) -> p c e", e=E)).then_inc(s("rt_sb"), 1)
            dve.wait_ge(s("rt_sb"), NB)
            for c in range(NB * NC - 1):
                dve.max(top[:, c, :], rt[:, 0, c, :])
            link(dve.max(top[:, NB * NC - 1, :], rt[:, 0, NB * NC - 1, :]))
            link(dve.memset(top[:, :, TOPK:8], 3e38))
            for c in range(NB * NC - 1):
                dve.match_replace(rt[:, 2, c, :], top[:, c, :], rt[:, 0, c, :], -3e38)
            link(dve.match_replace(rt[:, 2, NB * NC - 1, :], top[:, NB * NC - 1, :], rt[:, 0, NB * NC - 1, :], -3e38))
            link(dve.tensor_scalar(rt[:, 1, :, :], rt[:, 1, :, :], 1.0, None, ALU.add))
            link(dve.reciprocal(rt[:, 1, :, :], rt[:, 1, :, :]))
            link(dve.scalar_tensor_tensor(rt[:, 1, :, :], rt[:, 2, :, :], -3e38, rt[:, 1, :, :], ALU.is_equal, ALU.mult))
            link(dve.tensor_reduce(wsum[:, 0, :], rt[:, 1, :, :], AX.X, ALU.add))
            link(dve.reciprocal(wsum[:, 1, :], wsum[:, 0, :]))
            link(dve.tensor_tensor(rt[:, 1, :, :], rt[:, 1, :, :], rep(wsum[:, 1, :], 2, E), ALU.mult))
            link(dve.tensor_copy(cb, rt[:, 1, :, :]))
            link(dve.tensor_copy(comb[:, :, 0:E], cb))
            link(dve.tensor_tensor(rt[:, 2, :, :], rt[:, 1, :, :], comb[:, :, 0:E], ALU.subtract))
            link(dve.tensor_copy(cb, rt[:, 2, :, :]))
            link(dve.tensor_copy(comb[:, :, E:2 * E], cb))
            link(dve.tensor_tensor(comb[:, :, 2 * E:3 * E], rt[:, 2, :, :], comb[:, :, E:2 * E], ALU.subtract))
            dve.sem_inc(s("comb"), 1)
            for b in range(NB):
                dve.wait_ge(s("cT_ps"), b + 1)
                dve.tensor_copy(combT[:, b, :], ps[0:3 * E, 7 * b, :]).then_inc(s("combT"), 1)

            def add_experts(b):
                dve.wait_ge(s("y_mm"), (b + 1) * NPS)
                link(dve.tensor_tensor(ln_r[:, :, :], ps[:, 7 * (1 - b), :].rearrange("p (c d) -> p c d", c=NC),
                                       x1[:, NC * b:NC * b + NC, :], ALU.add))

            for b in range(NB):
                for p in range(NPS):
                    n = b * NPS + p
                    bank = 1 + 3 * (n % 2)
                    dve.wait_ge(s("h_tanh"), n + 1)
                    if n >= 2:
                        dve.wait_ge(s("y_mm"), n - 1)
                    dve.wait_ge(s("hv_ps"), n + 1)
                    if p:
                        dve.wait_ge(s("hc_ps"), b * (NPS - 1) + p)
                    h = hsig[:, n % 2, :]
                    link(dve.scalar_tensor_tensor(h, h, 1.0, ps[:, bank, :], ALU.add, ALU.mult))
                    if p:
                        link(dve.tensor_tensor(h, h, ps[:, bank + 2, :], ALU.mult))
                    link(dve.scalar_tensor_tensor(hid[:, n % 2, :], h, 0.5, ps[:, bank + 1, :], ALU.mult, ALU.mult))
                    dve.sem_inc(s("hid"), 1)
                    if b and p == 1:
                        add_experts(0)
                        norm_stats()
                    elif b and p == 2:
                        norm_root()
                    elif b and p == 3:
                        norm_apply(0, 3 * NB + 1, "y_ready")
            add_experts(1)
            layer_norm(1, 3 * NB + 2, "y_ready")

        @block.tensor
        def _(pe):
            mm = pe.matmul

            pe.wait_ge(s("in_xw"), 16 * len(loads["xw"]))
            pe.wait_ge(s("ctx_pad"), 1)
            def key_chunk(c):
                for i, (a, z) in enumerate(CTX):
                    if a == c:
                        pe.wait_ge(s(f"in_ctx{i}"), 16)
                if c >= 3:
                    pe.wait_ge(s("k_sq"), c - 2)
                mm(ps[:, c % 3, 0:KC], xw[:, 1, :], ctxT[:, KC * c:KC * c + KC], start=True, stop=True)\
                    .then_inc(s("k_ps"), 1)

            def key_squares(c):
                pe.wait_ge(s("k_sq"), c + 1)
                if c >= 2:
                    pe.wait_ge(s("kn_max"), c - 1)
                mm(ps[0:XH, 5 + c % 2, 0:KC], hsel[:, :], ksq[:, c % 2, :], start=True, stop=True)\
                    .then_inc(s("kn_ps"), 1)

            def value_chunk(c):
                if c >= 2:
                    pe.wait_ge(s("v_aug"), c - 1)
                for i in range(GT):
                    ins = mm(ps[:, 3 + c % 2, P * i:P * i + P], ctxT[:, KC * c + P * i:KC * c + P * i + P],
                             xw[:, 2, :], start=True, stop=True)
                ins.then_inc(s("v_ps"), 1)

            key_chunk(0)
            key_chunk(1)
            for c in range(NG):
                if c + 2 < NG:
                    key_chunk(c + 2)
                value_chunk(c)
                if c:
                    key_squares(c - 1)
            key_squares(NG - 1)

            pe.wait_ge(s("v_ps"), NG)
            pe.sem_inc(s("ctx_used"), 1)
            pe.wait_ge(s("in_gw"), 16 * len(loads["gw"]))
            pe.wait_ge(s("in_x"), 16 * len(loads["x"]))
            pe.wait_ge(s("in_cst"), 16 * len(loads["cst"]))
            pe.wait_ge(s("k_sq"), NG)
            pe.wait_ge(s("v_aug"), NG)
            pe.wait_ge(s("kn_max"), NG)
            for b in range(NB):
                xb_ = xT[:, TB * b:TB * b + TB]
                if b:
                    pe.wait_ge(s("q_parts"), b)
                    pe.wait_ge(s("x1T_sb"), b)
                mm(ps[0:16, 2, :], w1[:, :], xb_, start=True, stop=True).then_inc(s("low_ps"), 1)
                mm(ps[:, 1, :], wqk[:, 1, :], xb_, start=True, stop=True).then_inc(s("qk_ps"), 1)
                pe.wait_ge(s("low_sb"), b + 1)
                mm(ps[:, 3, :], w2[:, :], low[:, :], start=True, stop=True).then_inc(s("z_ps"), 1)
                mm(ps[:, 0, :], wqk[:, 0, :], xb_, start=True, stop=True).then_inc(s("qt_ps"), 1)
                for c in range(NC):
                    ins = mm(ps[:, 4 + c, :], xT[:, TB * b + P * c:TB * b + P * c + P],
                             wvg[:, :, :].rearrange("p a n -> p (a n)"), start=True, stop=True)
                ins.then_inc(s("vg_ps"), 1)

                def heads_scores(bank, keys, queries, width):
                    for c in range(NC):
                        for h in range(GH):
                            r = slice(DK * h, DK * h + DK)
                            ins = mm(ps[:, bank + h, width * c:width * c + width], keys[r, P * c:P * c + P],
                                     queries[r, width * c:width * c + width], start=True, stop=True)
                    return ins

                pe.wait_ge(s("q_sb"), b + 1)
                pe.wait_ge(s("k_sb"), b + 1)
                pe.wait_ge(s("gate"), b + 1)
                heads_scores(0, k_t[:, :], q_t[:, :], P).then_inc(s("diag_ps"), 1)
                for lv in range(LEVELS):
                    pe.wait_ge(s("lvl_qx"), b * LEVELS + lv + 1)
                    if lv <= 1:
                        pe.wait_ge(s("a_diag"), b + 1)
                    else:
                        pe.wait_ge(s("a_sel"), b * LEVELS + lv - 1)
                    for c in range(NC):
                        ins = mm(ps[:, 2 * (lv % 2) + c // 2, 256 * (c % 2):256 * (c % 2) + 256],
                                 k_l[:, lv % 2, P * c:P * c + P],
                                 qx[:, lv % 2, :, P // 2 * c:P // 2 * c + P // 2], start=True, stop=True)
                    ins.then_inc(s("lvl_ps"), 1)
                pe.wait_ge(s("a_sel"), (b + 1) * LEVELS)
                pe.wait_ge(s("qkd"), b + 1)
                for c in range(NC):
                    ins = pe.transpose(ps[:, 0, P * c:P * c + P], kd[:, P * c:P * c + P], eye[:, :])
                ins.then_inc(s("ktok_ps"), 1)
                pe.wait_ge(s("ktok_sb"), b + 1)
                pe.wait_ge(s("v_sb"), b + 1)
                for c in range(NC):
                    ins = mm(ps[:, 1 + c // 2, 256 * (c % 2):256 * (c % 2) + 256], ktok[:, c, :], v_g[:, c, :],
                             start=True, stop=True)
                ins.then_inc(s("kv_ps"), 1)
                pe.wait_ge(s("vg_free"), b + 1)
                for c in range(NC):
                    for h in range(GH):
                        mm(ps[:, 4 + c, DV * h:DV * h + DV], a_sc[:, GH * c + h, :], v_g[:, c, DV * h:DV * h + DV],
                           start=(h == 0), stop=False, skip_group_check=True)
                for c in range(NC):
                    if NC * b + c:
                        pe.wait_ge(s("state_ready"), NC * b + c)
                    ins = mm(ps[:, 4 + c, 0:256], qd[:, P * c:P * c + P], state[:, NC * b + c, :],
                             start=False, stop=True, skip_group_check=True)
                ins.then_inc(s("o_ps"), 1)
                pe.wait_ge(s("og"), b + 1)
                pe.wait_ge(s("state_ready"), NC * (b + 1))
                for a in range(2):
                    for c in range(NC):
                        ins = pe.transpose(ps[:, a, P * c:P * c + P], og[:, c, P * a:P * a + P], eye[:, :])
                ins.then_inc(s("ogT_ps"), 1)
                pe.wait_ge(s("ogT_sb"), b + 1)
                for c in range(NC):
                    for a in range(2):
                        ins = mm(ps[:, 2, P * c:P * c + P], ogT[:, a, P * c:P * c + P], wo[:, a, :],
                                 start=(a == 0), stop=(a == 1))
                ins.then_inc(s("wo_ps"), 1)
                pe.wait_ge(s("x1_ready"), b + 1)
                for c in range(NC):
                    ins = pe.transpose(ps[:, 3, P * c:P * c + P], x1[:, NC * b + c, :], eye[:, :])
                ins.then_inc(s("x1T_ps"), 1)
                pe.wait_ge(s("x1T_sb"), b + 1)
                mm(ps[:, 0, :], xw[:, 0, :], x1T[:, :], start=True, stop=True).then_inc(s("q2_ps"), 1)
                pe.wait_ge(s("q_sq"), b + 1)
                mm(ps[0:XH, 2, :], hsel[:, :], qsq[:, :], start=True, stop=True).then_inc(s("qn_ps"), 1)
                pe.wait_ge(s("bound_sq"), b + 1)

            pe.wait_ge(s("viol"), 1)
            mm(ps[0:1, 1, 0:4], onesf[:, :], viol[:, :], start=True, stop=True).then_inc(s("viol_ps"), 1)
            pe.wait_ge(s("q_in0"), 16 * 14)
            pe.wait_ge(s("k_rows0"), 16 * 8)
            pe.wait_ge(s("m_in0"), 16 * 2)
            pe.wait_ge(s("keys_in0"), LOAD)
            pe.wait_ge(s("flag"), 1)
            general = pe.value_load(flag[0:1, 0:1], min_val=0, max_val=1)

            def max_unit(v, slot):
                for h in range(HG):
                    with pe.Fori(0, NC) as i:
                        pe.wait_ge(s(f"g_keys{slot}"), v * LOAD + LOAD)
                        for j in range(4):
                            n = 4 if j < 3 else 1
                            w = 512 if j < 3 else SP - 12 * 512
                            pe.wait_ge(s("m_red"), (v * 2 + slot) * (HG * NC * 4) + i * 4 + (h * NC * 4 + j + 1))
                            for k in range(n):
                                key = 512 * (4 * j + k)
                                ins = mm(ps[:, 4 * (j % 2) + k, 0:w],
                                         qaug[:, bass.ds(v * (2 * HG) + (slot * HG + h), 1), bass.ds(i * P, P)],
                                         kbuf[:, slot, h // 2, key:key + w], start=True, stop=True)
                            ins.then_inc(s("m_ps"), 1)
                pe.wait_ge(s("m_ps"), (v * 2 + slot + 1) * (HG * NC * 4))
                pe.sem_inc(s("g_slot_free"), 1)

            def second_block_in():
                pe.wait_ge(s("k_rows1"), 16 * 8)
                pe.wait_ge(s("q_in1"), 16 * 14)
                pe.wait_ge(s("m_in1"), 16 * 2)

            with pe.If(general > 0):
                second_block_in()
                with pe.Fori(0, UNITS // 2) as v:
                    max_unit(v, 0)
                    max_unit(v, 1)
                pe.wait_ge(s("m_done"), UNITS * HG * NC)
                for b in range(NB):
                    if b:
                        pe.wait_ge(s("mT_free"), b)
                    for i in range(NC):
                        cols = mall[:, b * XH * NC:(b + 1) * XH * NC].rearrange("p (h i) -> p i h", i=NC)[:, i, :]
                        ins = pe.transpose(ps[0:XH, 0, P * i:P * i + P], cols, eye[:, :])
                    ins.then_inc(s("mT_ps"), 1)
                pe.wait_ge(s("g_m_in"), 16 * 2 * NB)
                pe.wait_ge(s("g_keys0"), (UNITS // 2 + 1) * LOAD)
                pe.wait_ge(s("g_keys1"), (UNITS // 2 + 1) * LOAD)

            pe.wait_ge(s("v_zero"), 1)
            pe.sem_inc(s("p_free"), GT)

            def scores(v, slot, g, a, step):
                pe.wait_ge(s("s_free"), step + 1)
                for i in range(3):
                    tile, h = divmod(3 * a + i, HG)
                    ins = mm(ps[:, 3 * (a % 2) + i, :], kbuf[:, slot, h // 2, bass.ds(g * KC + tile * P, P)],
                             qaug[:, bass.ds(v * (2 * HG) + (slot * HG + h), 1), :], start=True, stop=True)
                ins.then_inc(s("scores"), 1)

            def sums(g_all, tile, first_group, last_group):
                pe.wait_ge(s("v_staged"), g_all * GT + (tile + 1))
                pe.wait_ge(s("s_free"), g_all * STEPS + (tile + 4))
                for h in range(HG):
                    a, i = divmod(HG * tile + h, 3)
                    ins = mm(ps[32 * h:32 * h + 32, 6, :], vst[:, tile, h, :], prob[:, a, i, :],
                             start=(first_group and tile == 0), stop=(last_group and tile == GT - 1),
                             skip_group_check=True)
                ins.then_inc(s("p_free"), 1)

            def group(v, slot, g, first_group, last_group, first_unit, last_unit):
                g_all = v * (2 * NG) + slot * NG + g
                scores(v, slot, g, 2, g_all * STEPS + 2)
                scores(v, slot, g, 3, g_all * STEPS + 3)
                if last_group:
                    pe.wait_ge(s("scores"), g_all * STEPS + 4)
                    pe.sem_inc(s("k_slot_free"), 1)
                if first_group:
                    pe.wait_ge(s("o_free"), v * 2 + (slot + 1))
                if last_group and last_unit:
                    project_attention(0, 7)
                sums(g_all, 0, first_group, last_group)
                if first_group and not first_unit:
                    denominators(v * 2 + (slot - 1))
                for a in range(2):
                    if not last_group:
                        scores(v, slot, g + 1, a, g_all * STEPS + (4 + a))
                    elif not last_unit:
                        nv, ns = (v, 1) if slot == 0 else (v + 1, 0)
                        if a == 0:
                            pe.wait_ge(s(f"keys_in{ns}"), nv * LOAD + LOAD)
                            if first_unit:
                                second_block_in()
                        scores(nv, ns, 0, a, g_all * STEPS + (4 + a))
                    sums(g_all, 1 + a, first_group, last_group)

            def project_attention(b, bank):
                for hg in range(NHG):
                    n = b * NHG + hg
                    pe.wait_ge(s("o_norm"), n + 2)
                    if n == 0:
                        pe.wait_ge(s("in_late"), 16 * len(loads["late"]))
                        pe.wait_ge(s("o_norm"), UNITS)
                    for c in range(NC):
                        ins = mm(ps[:, bank, P * c:P * c + P], osb[:, n, P * c:P * c + P], wox[:, hg, :],
                                 start=(hg == 0 and c == 0), stop=(hg == NHG - 1), skip_group_check=True)
                ins.then_inc(s("xo_ps"), 1)

            def denominators(u):
                pe.wait_ge(s("o_norm"), u + 1)
                mm(ps[:, 7, :], dsel[:, :], osb[:, bass.ds(u, 1), :], start=True, stop=True)\
                    .then_inc(s("den_ps"), 1)

            def unit(v, slot, first_unit=False, last_unit=False):
                group(v, slot, 0, True, False, first_unit, last_unit)
                with pe.Fori(1, NG - 1) as g:
                    group(v, slot, g, False, False, first_unit, last_unit)
                group(v, slot, NG - 1, False, True, first_unit, last_unit)

            pe.wait_ge(s("keys_in0"), LOAD)
            scores(0, 0, 0, 0, 0)
            scores(0, 0, 0, 1, 1)
            unit(0, 0, first_unit=True)
            pe.wait_ge(s("in_dsel"), 16)
            unit(0, 1)
            with pe.Fori(1, UNITS // 2 - 1) as v:
                unit(v, 0)
                unit(v, 1)
            unit(UNITS // 2 - 1, 0)
            unit(UNITS // 2 - 1, 1, last_unit=True)

            pe.wait_ge(s("o_free"), UNITS + 1)
            pe.wait_ge(s("s_free"), UNITS * NG * STEPS + 2)
            pe.wait_ge(s("x2_ready"), 1)
            denominators(UNITS - 1)

            def transpose_x2(b):
                pe.wait_ge(s("x2_ready"), b + 1)
                for c in range(NC):
                    ins = pe.transpose(ps[:, 2 + b, P * c:P * c + P], x1[:, NC * b + c, :], eye[:, :])
                ins.then_inc(s("x2T_ps"), 1)

            def routing_logits(b):
                pe.wait_ge(s("x2T_sb"), b + 1)
                for c in range(NC):
                    ins = mm(ps[:, 4 + b, E * c:E * c + E], x2T[:, b, P * c:P * c + P], gate[:, :],
                             start=True, stop=True)
                ins.then_inc(s("rt_ps"), 1)

            transpose_x2(0)
            routing_logits(0)
            project_attention(1, 1)
            transpose_x2(1)
            routing_logits(1)
            for n in range(NB * NPS + 1):
                if n < NB * NPS:
                    b, p = divmod(n, NPS)
                    bank = 1 + 3 * (n % 2)
                    if n >= 2:
                        pe.wait_ge(s("hid"), n - 1)
                    if n == 1:
                        pe.wait_ge(s("rt_exp"), NB)
                        pe.wait_ge(s("rt_sb"), NB)
                    mm(ps[:, bank, :], win[:, p, :], x2T[:, b, :], start=True, stop=True).then_inc(s("h_ps"), 1)
                    mm(ps[:, bank + 1, :], vin[:, p, :], x2T[:, b, :], start=True, stop=True)\
                        .then_inc(s("hv_ps"), 1)
                    if n == 1:
                        pe.wait_ge(s("comb"), 1)
                        for half in range(NB):
                            for c in range(NC):
                                ins = pe.transpose(ps[0:3 * E, 7 * half, P * c:P * c + P],
                                                   comb[:, NC * half + c, :], eye[:, :])
                            ins.then_inc(s("cT_ps"), 1)
                        pe.wait_ge(s("combT"), 1)
                    if p:
                        mm(ps[:, bank + 2, :], csel[:, p - 1, :], combT[:, b, :], start=True, stop=True)\
                            .then_inc(s("hc_ps"), 1)
                if n:
                    b, p = divmod(n - 1, NPS)
                    pe.wait_ge(s("hid"), n)
                    if n == 1:
                        pe.wait_ge(s("combT"), NB)
                    for c in range(NC):
                        ins = mm(ps[:, 7 * (1 - b), P * c:P * c + P], hid[:, (n - 1) % 2, P * c:P * c + P],
                                 wout[:, p, :], start=(p == 0 and c == 0), stop=(p == NPS - 1),
                                 skip_group_check=True)
                    ins.then_inc(s("y_mm"), 1)


def kernel(**inputs):
    import ml_dtypes
    import numpy as np
    import concourse.bacc as bacc
    from concourse.bass_utils import run_bass_kernel_spmd

    a = {k: np.asarray(v) for k, v in inputs.items()}
    arrays = layout(a, np, ml_dtypes.bfloat16)
    nc = bacc.Bacc("TRN2", target_bir_lowering=False, num_devices=1)
    aps = {k: nc.dram_tensor("in_" + k, v.shape, mybir.dt.from_np(v.dtype), kind="ExternalInput").ap()
           for k, v in arrays.items()}
    y = nc.dram_tensor("y", (T, D), F32, kind="ExternalOutput").ap()
    build(nc, aps, y)
    r = run_bass_kernel_spmd(nc, [{"in_" + k: v for k, v in arrays.items()}], core_ids=[0])
    return r.results[0]["y"].reshape(1, T, D)


def layout(a, np, bf16):
    c = np.ascontiguousarray
    g = lambda n: c(a["L0_attn_" + n])
    f = lambda n: c(a["L0_ffn_" + n])
    x = a["x"].reshape(T, D)
    d = {"x": c(x), "xT": c(x.T), "ctxT": c(a["ctx_1024"].reshape(SKV, D).T),
         "mask": c(a["mask_Bx1x1xS2_fk0"].reshape(SKV)), "Wq": g("Wq"), "Wk": g("Wk"), "Wv": g("Wv"),
         "Wg": g("Wg"), "gk_w1": g("gk_w1"), "gk_w2": g("gk_w2"), "gk_b2": g("gk_b2"),
         "g_norm_w": g("g_norm_w"), "Wo": g("Wo"), "gate_wT": c(f("gate_w").T), "ws_in": f("ws_in"),
         "vs_in": f("vs_in"), "ws_out": f("ws_out"),
         "e_winT": c(f("e_win").transpose(1, 0, 2).reshape(D, E * EH)),
         "e_vinT": c(f("e_vin").transpose(1, 0, 2).reshape(D, E * EH)),
         "e_wout": c(f("e_wout").reshape(E * EH, D))}
    for n in ("Wq", "bq", "Wk", "bk", "Wv", "bv", "Wo", "bo"):
        d["x" + n] = c(a["L0_xattn_" + n])
    p = np.arange(P)
    d["c_hsel"] = (p[:, None] // DH == np.arange(XH)[None, :]).astype(bf16)
    d["c_eye"] = np.eye(P, dtype=np.float32)
    masks = []
    for lv in range(LEVELS):
        m = 1 << lv
        t = np.arange(TB).reshape(-1, 2, m)[:, 1, :].reshape(-1) % P
        masks.append((p[:, None] // m == (t // m - 1)[None, :]).astype(bf16))
    d["c_lmask"] = c(np.stack(masks, 1))
    d["c_bd"] = (p[:, None] // DK == np.arange(256)[None, :] // DV).astype(np.float32)
    rows = np.zeros((HALF - ROW_MAX, SP), bf16)
    rows[0:3] = 1
    d["c_krows"] = rows
    d["c_ones"] = np.ones((3, XH // 2, TB), bf16)
    d["c_dsel"] = (p[:, None] == p[None, :] // 32 * 32 + DH).astype(np.float32)
    e = np.arange(3 * E) % E
    d["c_csel"] = c((e[:, None, None] == (2 * np.arange(E // 2)[:, None] + p[None, :] // EH)[None]).astype(bf16))
    return d
```
